# Optimizing a Trainium2 kernel written in Bass

```python
import numpy as np
import jax
import jax.numpy as jnp

def _softmax(x, axis=-1):
    return jax.nn.softmax(x, axis=axis)

def _gelu(x):
    return jax.nn.gelu(x, approximate=True)

def _silu(x):
    return jax.nn.silu(x)

def _sigmoid(x):
    return jax.nn.sigmoid(x)

def _layernorm(x, axis=-1, eps=1e-05):
    m = jnp.mean(x, axis=axis, keepdims=True)
    v = jnp.var(x, axis=axis, keepdims=True)
    return (x - m) / jnp.sqrt(v + eps)

def _scatter_add(tgt, idx, src, axis=0):
    return tgt.at[idx].add(src)

def _segment_sum(src, seg, n):
    return jax.ops.segment_sum(src, seg, n)
kernel_name = 'mk_decoder_postln_d2_seqx_r8_5df5bc'

def setup_inputs(seed: int=0):
    np.random.seed(seed)
    _w = jnp.asarray

    def _rec_inputs():
        import jax
        import jax.numpy as jnp
        _rk = jax.random.key(seed)
        x = -0.0003929 + 0.9999 * jax.random.normal(jax.random.fold_in(_rk, 1), (32, 128, 128), jnp.float32)
        _lenS = 128 - jax.random.randint(jax.random.fold_in(_rk, 7), (32,), 0, max(1, 128 // 4) + 1, jnp.int32)
        _lenS2 = 128 - jax.random.randint(jax.random.fold_in(_rk, 8), (32,), 0, max(1, 128 // 4) + 1, jnp.int32)
        _ctx_1024P = jax.random.normal(jax.random.fold_in(_rk, 11), (32, 16, 128), jnp.float32)
        _ctx_1024c = jax.random.dirichlet(jax.random.fold_in(_rk, 511), 0.3 * jnp.ones((16,), jnp.float32), (32, 128))
        _ctx_1024t = jnp.einsum('bsk,bkd->bsd', _ctx_1024c, _ctx_1024P)
        _ctx_1024t = _ctx_1024t * jax.lax.rsqrt(jnp.mean(jnp.square(_ctx_1024t)) + 1e-12) * 0.953939
        ctx_1024 = 2.81802e-05 + 1.00001 * (_ctx_1024t + 0.3 * jax.random.normal(jax.random.fold_in(_rk, 611), (32, 128, 128), jnp.float32))
        return (x, ctx_1024)
    x, ctx_1024 = _rec_inputs()

    def _L0_attn_setup():
        import jax, jax.numpy as jnp
        import numpy as np
        B, S, D = (4, 512, 128)
        CHUNK = 64
        MAX_LR = 0.2
        MIN_DECAY = 0.5
        MAX_NORM = 30.0
        NORM_EPS = 1e-05

        def _forward(x, M_init, eta_w, eta_b, alpha_w, alpha_b, gate_w, gate_b, vg_w1, vg_w2):
            b, s, d = x.shape
            n_ch = s // CHUNK

            def value_gen(y):
                h = jax.nn.silu(y @ vg_w1.T) @ vg_w2.T
                return h + y
            x_chunks = x.reshape(b, n_ch, CHUNK, d).transpose(1, 0, 2, 3)
            M0 = jnp.broadcast_to(M_init, (b, d, d))

            def step(M, chunk):
                eta_tok = jax.nn.sigmoid(chunk @ eta_w + eta_b[0]) * MAX_LR
                alpha_tok = MIN_DECAY + jax.nn.sigmoid(chunk @ alpha_w + alpha_b[0]) * (1.0 - MIN_DECAY)
                eta = eta_tok.mean(axis=1)[:, None, None]
                alpha = alpha_tok.mean(axis=1)[:, None, None]
                outputs = jnp.einsum('bci,boi->bco', chunk, M)
                nrm = jnp.sqrt(jnp.sum(chunk * chunk, axis=-1, keepdims=True))
                keys = chunk / jnp.maximum(nrm, NORM_EPS)
                k_mean = keys.mean(axis=1)
                v_target = value_gen(outputs).mean(axis=1)
                Mk = jnp.einsum('boi,bi->bo', M, k_mean)
                err = v_target - Mk
                update = err[:, :, None] * k_mean[:, None, :]
                M_new = alpha * M + eta * update
                gate = jax.nn.sigmoid(k_mean @ gate_w + gate_b[0])[:, None, None]
                M_new = gate * M_new + (1.0 - gate) * M
                M_norm = jnp.sqrt(jnp.sum(M_new * M_new, axis=(-2, -1), keepdims=True))
                scale = jnp.minimum(MAX_NORM / (M_norm + 1e-06), 1.0)
                return (M_new * scale, outputs)
            M_final, outs = jax.lax.scan(step, M0, x_chunks)
            outs = outs.transpose(1, 0, 2, 3).reshape(b, s, d)
            final_out = value_gen(outs)
            return (final_out, M_final)

        def _reference_tuple_inner(x, M_init, eta_w, eta_b, alpha_w, alpha_b, gate_w, gate_b, vg_w1, vg_w2):
            return _forward(x, M_init, eta_w, eta_b, alpha_w, alpha_b, gate_w, gate_b, vg_w1, vg_w2)
        key = jax.random.key(seed)
        ks = jax.random.split(key, 10)
        return {'x': jax.random.normal(ks[0], (B, S, D), jnp.float32), 'M_init': jax.random.normal(ks[1], (D, D), jnp.float32) * 0.02, 'eta_w': jax.random.normal(ks[2], (D,), jnp.float32) * 0.02, 'eta_b': jax.random.normal(ks[3], (1,), jnp.float32), 'alpha_w': jax.random.normal(ks[4], (D,), jnp.float32) * 0.02, 'alpha_b': jax.random.normal(ks[5], (1,), jnp.float32), 'gate_w': jax.random.normal(ks[6], (D,), jnp.float32) * 0.02, 'gate_b': jax.random.normal(ks[7], (1,), jnp.float32), 'vg_w1': jax.random.normal(ks[8], (D, D), jnp.float32) * 0.02, 'vg_w2': jax.random.normal(ks[9], (D, D), jnp.float32) * 0.02}
    _L0_attn_all = _L0_attn_setup()
    _L0_attn_in = {k: v for k, v in _L0_attn_all.items() if k in ('M_init', 'eta_w', 'eta_b', 'alpha_w', 'alpha_b', 'gate_w', 'gate_b', 'vg_w1', 'vg_w2')}
    del _L0_attn_all

    def _L0_xattn_setup():
        import jax, jax.numpy as jnp
        import numpy as np
        B, S, E = (8, 256, 128)
        EPS = 0.001

        def _layer_norm(x, gamma, beta):
            mu = jnp.mean(x, axis=-1, keepdims=True)
            var = jnp.mean(jnp.square(x - mu), axis=-1, keepdims=True)
            return gamma * (x - mu) * jax.lax.rsqrt(var + EPS) + beta

        def _attention(q_in, k_in, v_in, WQ, WK, WV, causal):
            Q = jnp.einsum('bse,ed->bsd', q_in, WQ)
            K = jnp.einsum('bse,ed->bsd', k_in, WK)
            V = jnp.einsum('bse,ed->bsd', v_in, WV)
            d = K.shape[-1]
            scores = jnp.einsum('bqd,bkd->bqk', Q, K) / jnp.sqrt(jnp.float32(d))
            if causal:
                qlen, klen = (scores.shape[-2], scores.shape[-1])
                mask = jnp.triu(jnp.ones((qlen, klen), bool), k=1)
                scores = jnp.where(mask[None], -jnp.inf, scores)
            p = jax.nn.softmax(scores, axis=-1)
            return jnp.einsum('bqk,bkd->bqd', p, V)
        key = jax.random.key(seed)
        ks = jax.random.split(key, 10)
        sc = 1.0 / np.sqrt(E)
        return {'inputs': jax.random.normal(ks[0], (B, S, E), jnp.float32), 'context': jax.random.normal(ks[1], (B, S, E), jnp.float32), 'Wq': jax.random.normal(ks[2], (E, E), jnp.float32) * sc, 'Wk': jax.random.normal(ks[3], (E, E), jnp.float32) * sc, 'Wv': jax.random.normal(ks[4], (E, E), jnp.float32) * sc, 'Wcq': jax.random.normal(ks[5], (E, E), jnp.float32) * sc, 'Wck': jax.random.normal(ks[6], (E, E), jnp.float32) * sc, 'Wcv': jax.random.normal(ks[7], (E, E), jnp.float32) * sc, 'gamma': jnp.ones((E,), jnp.float32), 'beta': jnp.zeros((E,), jnp.float32), 'W1': jax.random.normal(ks[8], (E, E), jnp.float32) * sc, 'b1': jnp.zeros((E,), jnp.float32)}
    _L0_xattn_all = _L0_xattn_setup()
    _L0_xattn_in = {k: v for k, v in _L0_xattn_all.items() if k in ('Wq', 'Wk', 'Wv', 'Wcq', 'Wck', 'Wcv', 'gamma', 'beta', 'W1', 'b1')}
    del _L0_xattn_all

    def _L0_ffn_setup():
        import jax, jax.numpy as jnp
        import numpy as np
        B, S, H = (2, 256, 128)
        E_DYN, E_FIX = (8, 1)
        I_DYN, I_FIX = (64, 256)
        TOP_K = 4
        TOP_P = 0.75
        JITTER_EPS = 0.1
        CAPACITY_FACTOR = 1.25
        MIN_CAPACITY = 4

        def _sparse_mixer(scores):
            T = scores.shape[0]
            rows = jnp.arange(T)
            masked_scores = scores
            mults, sels = ([], [])
            for _ in range(TOP_K):
                thr = jnp.max(masked_scores, axis=-1, keepdims=True)
                sel = jnp.argmax(masked_scores, axis=-1)
                factor = jnp.maximum(jnp.abs(scores), jnp.abs(thr))
                jmask = (thr - scores) / factor > 2.0 * JITTER_EPS
                gates = jax.nn.softmax(jnp.where(jmask, -jnp.inf, masked_scores), axis=-1)
                mult = jnp.take_along_axis(gates, sel[:, None], axis=-1)[:, 0]
                masked_scores = masked_scores.at[rows, sel].set(-jnp.inf)
                mults.append(mult)
                sels.append(sel)
            return (jnp.stack(mults, axis=-1), jnp.stack(sels, axis=-1))
        key = jax.random.key(seed)
        k = jax.random.split(key, 8)
        sc = 0.02
        return {'hidden_states': jax.random.normal(k[0], (B, S, H), jnp.float32), 'gate_w': jax.random.normal(k[1], (E_DYN + E_FIX, H), jnp.float32) * sc, 'dyn_gate_w': jax.random.normal(k[2], (E_DYN, I_DYN, H), jnp.float32) * sc, 'dyn_up_w': jax.random.normal(k[3], (E_DYN, I_DYN, H), jnp.float32) * sc, 'dyn_down_w': jax.random.normal(k[4], (E_DYN, H, I_DYN), jnp.float32) * sc, 'sh_gate_w': jax.random.normal(k[5], (E_FIX, I_FIX, H), jnp.float32) * sc, 'sh_up_w': jax.random.normal(k[6], (E_FIX, I_FIX, H), jnp.float32) * sc, 'sh_down_w': jax.random.normal(k[7], (E_FIX, H, I_FIX), jnp.float32) * sc}
    _L0_ffn_all = _L0_ffn_setup()
    _L0_ffn_in = {k: v for k, v in _L0_ffn_all.items() if k in ('gate_w', 'dyn_gate_w', 'dyn_up_w', 'dyn_down_w', 'sh_gate_w', 'sh_up_w', 'sh_down_w')}
    del _L0_ffn_all

    def _L1_attn_setup():
        import jax, jax.numpy as jnp
        import numpy as np
        H, DK, DV, CHUNK = (4, 32, 32, 32)
        MIN_FLOOR, MAX_FLOOR, TEMP_MIN = (0.01, 0.1, 0.5)

        def _silu(x):
            return x * jax.nn.sigmoid(x)

        def _causal_dw_conv(x_bcl, w_ck):
            K = w_ck.shape[-1]
            return jax.lax.conv_general_dilated(x_bcl, w_ck[:, None, :], window_strides=(1,), padding=[(K - 1, 0)], feature_group_count=x_bcl.shape[1])

        def _l2norm(x):
            return x * jax.lax.rsqrt(jnp.sum(x * x, axis=-1, keepdims=True) + 1e-06)

        def _delta_rule_chunkwise(q, k, v, beta, chunk=CHUNK):
            b, h, L, dk = q.shape
            dv = v.shape[-1]
            n = L // chunk
            q = _l2norm(q)
            k = _l2norm(k)
            v = v * beta[..., None]
            kb = k * beta[..., None]
            qc, kc, vc, kbc = (t.reshape(b, h, n, chunk, -1) for t in (q, k, v, kb))
            A = jnp.einsum('bhncd,bhned->bhnce', kbc, kc)
            eye = jnp.eye(chunk, dtype=q.dtype)
            T = eye + jnp.tril(A, -1)
            inv = jax.scipy.linalg.solve_triangular(T, jnp.broadcast_to(eye, T.shape), lower=True, unit_diagonal=True)
            u = inv @ vc
            w = inv @ kbc
            strict = jnp.triu(jnp.ones((chunk, chunk), dtype=bool), 1)

            def step(S, xs):
                q_i, k_i, u_i, w_i = xs
                att = jnp.where(strict, 0.0, jnp.einsum('bhcd,bhed->bhce', q_i, k_i))
                u_adj = u_i - jnp.einsum('bhck,bhkd->bhcd', w_i, S)
                o = jnp.einsum('bhck,bhkd->bhcd', q_i, S) + att @ u_adj
                S = S + jnp.einsum('bhck,bhcd->bhkd', k_i, u_adj)
                return (S, o)
            mv = lambda t: jnp.moveaxis(t, 2, 0)
            S0 = jnp.zeros((b, h, dk, dv), dtype=q.dtype)
            S, outs = jax.lax.scan(step, S0, (mv(qc), mv(kc), mv(u), mv(w)))
            out = jnp.moveaxis(outs, 0, 2).reshape(b, h, L, dv)
            return (out, S)

        def _fir(x, filt):
            b, l, h, d = x.shape
            xc = x.transpose(0, 2, 3, 1).reshape(b, h * d, l)
            y = _causal_dw_conv(xc, filt.reshape(h * d, -1))
            return y.reshape(b, h, d, l).transpose(0, 3, 1, 2)
        key = jax.random.key(seed)
        ks = iter(jax.random.split(key, 32))
        B, L, D = (4, 256, 128)
        kd, vd = (H * DK, H * DV)
        rn = lambda shp, s=0.02: jax.random.normal(next(ks), shp, jnp.float32) * s
        fir = lambda K: jnp.zeros((H, DV, K), jnp.float32).at[..., -1].set(1.0) + 0.01 * jax.random.normal(next(ks), (H, DV, K), jnp.float32)
        return dict(hidden_states=jax.random.normal(next(ks), (B, L, D), jnp.float32), Wq=rn((D, kd)), Wk=rn((D, kd)), Wv=rn((D, vd)), q_conv_w=rn((kd, 4), 0.3), k_conv_w=rn((kd, 4), 0.3), v_conv_w=rn((vd, 4), 0.3), Wb=rn((D, H)), fir_w3=fir(3), fir_w7=fir(7), fir_w15=fir(15), fir_w31=fir(31), router_W1=rn((D + DV * H * 5, 2 * D)), router_b1=jnp.zeros((2 * D,), jnp.float32), router_W2=rn((2 * D, H * 5)), router_b2=jnp.zeros((H * 5,), jnp.float32), id_gate_W=rn((D, H)), id_gate_b=jnp.full((H,), 2.0, jnp.float32), log_tau=jnp.zeros((H,), jnp.float32), o_norm_w=jnp.ones((DV,), jnp.float32), Wo=rn((vd, D)))
    _L1_attn_all = _L1_attn_setup()
    _L1_attn_in = {k: v for k, v in _L1_attn_all.items() if k in ('Wq', 'Wk', 'Wv', 'q_conv_w', 'k_conv_w', 'v_conv_w', 'Wb', 'fir_w3', 'fir_w7', 'fir_w15', 'fir_w31', 'router_W1', 'router_b1', 'router_W2', 'router_b2', 'id_gate_W', 'id_gate_b', 'log_tau', 'o_norm_w', 'Wo')}
    del _L1_attn_all

    def _L1_xattn_setup():
        import jax, jax.numpy as jnp
        import numpy as np
        D_MODEL = 128
        key = jax.random.key(seed)
        ks = jax.random.split(key, 11)
        B, S, D = (4, 256, D_MODEL)
        scale = 1.0 / np.sqrt(D)
        inp = {'query': jax.random.normal(ks[0], (B, S, D), dtype=jnp.float32), 'key': jax.random.normal(ks[1], (B, S, D), dtype=jnp.float32), 'value': jax.random.normal(ks[2], (B, S, D), dtype=jnp.float32), 'Wq': jax.random.normal(ks[3], (D, D), dtype=jnp.float32) * scale, 'bq': jnp.zeros((D,), dtype=jnp.float32), 'Wk': jax.random.normal(ks[4], (D, D), dtype=jnp.float32) * scale, 'bk': jnp.zeros((D,), dtype=jnp.float32), 'Wv': jax.random.normal(ks[5], (D, D), dtype=jnp.float32) * scale, 'bv': jnp.zeros((D,), dtype=jnp.float32), 'Wo': jax.random.normal(ks[6], (D, D), dtype=jnp.float32) * scale, 'bo': jnp.zeros((D,), dtype=jnp.float32)}
        return inp
    _L1_xattn_all = _L1_xattn_setup()
    _L1_xattn_in = {k: v for k, v in _L1_xattn_all.items() if k in ('Wq', 'bq', 'Wk', 'bk', 'Wv', 'bv', 'Wo', 'bo')}
    del _L1_xattn_all

    def _L1_ffn_setup():
        import jax, jax.numpy as jnp
        import numpy as np
        B, S, H, I, E, K = (4, 256, 128, 512, 4, 2)

        def _layer_norm(h, g, b, eps=1e-05):
            mu = h.mean(-1, keepdims=True)
            var = ((h - mu) ** 2).mean(-1, keepdims=True)
            return (h - mu) * jax.lax.rsqrt(var + eps) * g + b
        key = jax.random.key(seed)
        ks = jax.random.split(key, 24)
        rn = lambda k, shape, s=0.02: jax.random.normal(k, shape, dtype=jnp.float32) * s
        z = lambda shape: jnp.zeros(shape, jnp.float32)
        o = lambda shape: jnp.ones(shape, jnp.float32)
        return {'x': rn(ks[0], (B, S, H), 1.0), 'router_w': rn(ks[1], (H, E)), 'router_b': z((E,)), 'load_balancer': o((E,)), 'sw_w1': rn(ks[2], (H, I)), 'sw_w3': rn(ks[3], (H, I)), 'sw_w2': rn(ks[4], (I, H)), 'me_eq_w': rn(ks[5], (H, H)), 'me_eq_b': z((H,)), 'me_wv': rn(ks[6], (H, H)), 'me_bv': z((H,)), 'me_wo': rn(ks[7], (H, H)), 'me_bo': z((H,)), 'me_c1w': rn(ks[8], (H, 2 * H)), 'me_c1b': z((2 * H,)), 'me_c2w': rn(ks[9], (2 * H, H)), 'me_c2b': z((H,)), 'ce_syn_w': rn(ks[10], (H, H)), 'ce_syn_b': z((H,)), 'ce_wv': rn(ks[11], (H, H)), 'ce_bv': z((H,)), 'ce_wo': rn(ks[12], (H, H)), 'ce_bo': z((H,)), 'ce_n1g': o((H,)), 'ce_n1b': z((H,)), 'ce_f1w': rn(ks[13], (H, 2 * H)), 'ce_f1b': z((2 * H,)), 'ce_f2w': rn(ks[14], (2 * H, H)), 'ce_f2b': z((H,)), 'ce_n2g': o((H,)), 'ce_n2b': z((H,)), 'ce_gen_w': rn(ks[15], (H, H)), 'ce_gen_b': z((H,)), 'ml_w1': rn(ks[16], (H, I)), 'ml_b1': z((I,)), 'ml_w2': rn(ks[17], (I, H)), 'ml_b2': z((H,))}
    _L1_ffn_all = _L1_ffn_setup()
    _L1_ffn_in = {k: v for k, v in _L1_ffn_all.items() if k in ('router_w', 'router_b', 'load_balancer', 'sw_w1', 'sw_w3', 'sw_w2', 'me_eq_w', 'me_eq_b', 'me_wv', 'me_bv', 'me_wo', 'me_bo', 'me_c1w', 'me_c1b', 'me_c2w', 'me_c2b', 'ce_syn_w', 'ce_syn_b', 'ce_wv', 'ce_bv', 'ce_wo', 'ce_bo', 'ce_n1g', 'ce_n1b', 'ce_f1w', 'ce_f1b', 'ce_f2w', 'ce_f2b', 'ce_n2g', 'ce_n2b', 'ce_gen_w', 'ce_gen_b', 'ml_w1', 'ml_b1', 'ml_w2', 'ml_b2')}
    del _L1_ffn_all
    return {'x': x, 'ctx_1024': ctx_1024, 'L0_attn_M_init': _L0_attn_in['M_init'], 'L0_attn_eta_w': _L0_attn_in['eta_w'], 'L0_attn_eta_b': _L0_attn_in['eta_b'], 'L0_attn_alpha_w': _L0_attn_in['alpha_w'], 'L0_attn_alpha_b': _L0_attn_in['alpha_b'], 'L0_attn_gate_w': _L0_attn_in['gate_w'], 'L0_attn_gate_b': _L0_attn_in['gate_b'], 'L0_attn_vg_w1': _L0_attn_in['vg_w1'], 'L0_attn_vg_w2': _L0_attn_in['vg_w2'], 'L0_xattn_Wq': _L0_xattn_in['Wq'], 'L0_xattn_Wk': _L0_xattn_in['Wk'], 'L0_xattn_Wv': _L0_xattn_in['Wv'], 'L0_xattn_Wcq': _L0_xattn_in['Wcq'], 'L0_xattn_Wck': _L0_xattn_in['Wck'], 'L0_xattn_Wcv': _L0_xattn_in['Wcv'], 'L0_xattn_gamma': _L0_xattn_in['gamma'], 'L0_xattn_beta': _L0_xattn_in['beta'], 'L0_xattn_W1': _L0_xattn_in['W1'], 'L0_xattn_b1': _L0_xattn_in['b1'], 'L0_ffn_gate_w': _L0_ffn_in['gate_w'], 'L0_ffn_dyn_gate_w': _L0_ffn_in['dyn_gate_w'], 'L0_ffn_dyn_up_w': _L0_ffn_in['dyn_up_w'], 'L0_ffn_dyn_down_w': _L0_ffn_in['dyn_down_w'], 'L0_ffn_sh_gate_w': _L0_ffn_in['sh_gate_w'], 'L0_ffn_sh_up_w': _L0_ffn_in['sh_up_w'], 'L0_ffn_sh_down_w': _L0_ffn_in['sh_down_w'], 'L1_attn_Wq': _L1_attn_in['Wq'], 'L1_attn_Wk': _L1_attn_in['Wk'], 'L1_attn_Wv': _L1_attn_in['Wv'], 'L1_attn_q_conv_w': _L1_attn_in['q_conv_w'], 'L1_attn_k_conv_w': _L1_attn_in['k_conv_w'], 'L1_attn_v_conv_w': _L1_attn_in['v_conv_w'], 'L1_attn_Wb': _L1_attn_in['Wb'], 'L1_attn_fir_w3': _L1_attn_in['fir_w3'], 'L1_attn_fir_w7': _L1_attn_in['fir_w7'], 'L1_attn_fir_w15': _L1_attn_in['fir_w15'], 'L1_attn_fir_w31': _L1_attn_in['fir_w31'], 'L1_attn_router_W1': _L1_attn_in['router_W1'], 'L1_attn_router_b1': _L1_attn_in['router_b1'], 'L1_attn_router_W2': _L1_attn_in['router_W2'], 'L1_attn_router_b2': _L1_attn_in['router_b2'], 'L1_attn_id_gate_W': _L1_attn_in['id_gate_W'], 'L1_attn_id_gate_b': _L1_attn_in['id_gate_b'], 'L1_attn_log_tau': _L1_attn_in['log_tau'], 'L1_attn_o_norm_w': _L1_attn_in['o_norm_w'], 'L1_attn_Wo': _L1_attn_in['Wo'], 'L1_xattn_Wq': _L1_xattn_in['Wq'], 'L1_xattn_bq': _L1_xattn_in['bq'], 'L1_xattn_Wk': _L1_xattn_in['Wk'], 'L1_xattn_bk': _L1_xattn_in['bk'], 'L1_xattn_Wv': _L1_xattn_in['Wv'], 'L1_xattn_bv': _L1_xattn_in['bv'], 'L1_xattn_Wo': _L1_xattn_in['Wo'], 'L1_xattn_bo': _L1_xattn_in['bo'], 'L1_ffn_router_w': _L1_ffn_in['router_w'], 'L1_ffn_router_b': _L1_ffn_in['router_b'], 'L1_ffn_load_balancer': _L1_ffn_in['load_balancer'], 'L1_ffn_sw_w1': _L1_ffn_in['sw_w1'], 'L1_ffn_sw_w3': _L1_ffn_in['sw_w3'], 'L1_ffn_sw_w2': _L1_ffn_in['sw_w2'], 'L1_ffn_me_eq_w': _L1_ffn_in['me_eq_w'], 'L1_ffn_me_eq_b': _L1_ffn_in['me_eq_b'], 'L1_ffn_me_wv': _L1_ffn_in['me_wv'], 'L1_ffn_me_bv': _L1_ffn_in['me_bv'], 'L1_ffn_me_wo': _L1_ffn_in['me_wo'], 'L1_ffn_me_bo': _L1_ffn_in['me_bo'], 'L1_ffn_me_c1w': _L1_ffn_in['me_c1w'], 'L1_ffn_me_c1b': _L1_ffn_in['me_c1b'], 'L1_ffn_me_c2w': _L1_ffn_in['me_c2w'], 'L1_ffn_me_c2b': _L1_ffn_in['me_c2b'], 'L1_ffn_ce_syn_w': _L1_ffn_in['ce_syn_w'], 'L1_ffn_ce_syn_b': _L1_ffn_in['ce_syn_b'], 'L1_ffn_ce_wv': _L1_ffn_in['ce_wv'], 'L1_ffn_ce_bv': _L1_ffn_in['ce_bv'], 'L1_ffn_ce_wo': _L1_ffn_in['ce_wo'], 'L1_ffn_ce_bo': _L1_ffn_in['ce_bo'], 'L1_ffn_ce_n1g': _L1_ffn_in['ce_n1g'], 'L1_ffn_ce_n1b': _L1_ffn_in['ce_n1b'], 'L1_ffn_ce_f1w': _L1_ffn_in['ce_f1w'], 'L1_ffn_ce_f1b': _L1_ffn_in['ce_f1b'], 'L1_ffn_ce_f2w': _L1_ffn_in['ce_f2w'], 'L1_ffn_ce_f2b': _L1_ffn_in['ce_f2b'], 'L1_ffn_ce_n2g': _L1_ffn_in['ce_n2g'], 'L1_ffn_ce_n2b': _L1_ffn_in['ce_n2b'], 'L1_ffn_ce_gen_w': _L1_ffn_in['ce_gen_w'], 'L1_ffn_ce_gen_b': _L1_ffn_in['ce_gen_b'], 'L1_ffn_ml_w1': _L1_ffn_in['ml_w1'], 'L1_ffn_ml_b1': _L1_ffn_in['ml_b1'], 'L1_ffn_ml_w2': _L1_ffn_in['ml_w2'], 'L1_ffn_ml_b2': _L1_ffn_in['ml_b2']}

def reference(x, ctx_1024, L0_attn_M_init, L0_attn_eta_w, L0_attn_eta_b, L0_attn_alpha_w, L0_attn_alpha_b, L0_attn_gate_w, L0_attn_gate_b, L0_attn_vg_w1, L0_attn_vg_w2, L0_xattn_Wq, L0_xattn_Wk, L0_xattn_Wv, L0_xattn_Wcq, L0_xattn_Wck, L0_xattn_Wcv, L0_xattn_gamma, L0_xattn_beta, L0_xattn_W1, L0_xattn_b1, L0_ffn_gate_w, L0_ffn_dyn_gate_w, L0_ffn_dyn_up_w, L0_ffn_dyn_down_w, L0_ffn_sh_gate_w, L0_ffn_sh_up_w, L0_ffn_sh_down_w, L1_attn_Wq, L1_attn_Wk, L1_attn_Wv, L1_attn_q_conv_w, L1_attn_k_conv_w, L1_attn_v_conv_w, L1_attn_Wb, L1_attn_fir_w3, L1_attn_fir_w7, L1_attn_fir_w15, L1_attn_fir_w31, L1_attn_router_W1, L1_attn_router_b1, L1_attn_router_W2, L1_attn_router_b2, L1_attn_id_gate_W, L1_attn_id_gate_b, L1_attn_log_tau, L1_attn_o_norm_w, L1_attn_Wo, L1_xattn_Wq, L1_xattn_bq, L1_xattn_Wk, L1_xattn_bk, L1_xattn_Wv, L1_xattn_bv, L1_xattn_Wo, L1_xattn_bo, L1_ffn_router_w, L1_ffn_router_b, L1_ffn_load_balancer, L1_ffn_sw_w1, L1_ffn_sw_w3, L1_ffn_sw_w2, L1_ffn_me_eq_w, L1_ffn_me_eq_b, L1_ffn_me_wv, L1_ffn_me_bv, L1_ffn_me_wo, L1_ffn_me_bo, L1_ffn_me_c1w, L1_ffn_me_c1b, L1_ffn_me_c2w, L1_ffn_me_c2b, L1_ffn_ce_syn_w, L1_ffn_ce_syn_b, L1_ffn_ce_wv, L1_ffn_ce_bv, L1_ffn_ce_wo, L1_ffn_ce_bo, L1_ffn_ce_n1g, L1_ffn_ce_n1b, L1_ffn_ce_f1w, L1_ffn_ce_f1b, L1_ffn_ce_f2w, L1_ffn_ce_f2b, L1_ffn_ce_n2g, L1_ffn_ce_n2b, L1_ffn_ce_gen_w, L1_ffn_ce_gen_b, L1_ffn_ml_w1, L1_ffn_ml_b1, L1_ffn_ml_w2, L1_ffn_ml_b2):
    import jax
    import jax.numpy as jnp

    def _L0_attn_ref(x, M_init, eta_w, eta_b, alpha_w, alpha_b, gate_w, gate_b, vg_w1, vg_w2):
        import jax, jax.numpy as jnp
        import numpy as np
        B, S, D = (4, 512, 128)
        CHUNK = 64
        MAX_LR = 0.2
        MIN_DECAY = 0.5
        MAX_NORM = 30.0
        NORM_EPS = 1e-05

        def _forward(x, M_init, eta_w, eta_b, alpha_w, alpha_b, gate_w, gate_b, vg_w1, vg_w2):
            b, s, d = x.shape
            n_ch = s // CHUNK

            def value_gen(y):
                h = jax.nn.silu(y @ vg_w1.T) @ vg_w2.T
                return h + y
            x_chunks = x.reshape(b, n_ch, CHUNK, d).transpose(1, 0, 2, 3)
            M0 = jnp.broadcast_to(M_init, (b, d, d))

            def step(M, chunk):
                eta_tok = jax.nn.sigmoid(chunk @ eta_w + eta_b[0]) * MAX_LR
                alpha_tok = MIN_DECAY + jax.nn.sigmoid(chunk @ alpha_w + alpha_b[0]) * (1.0 - MIN_DECAY)
                eta = eta_tok.mean(axis=1)[:, None, None]
                alpha = alpha_tok.mean(axis=1)[:, None, None]
                outputs = jnp.einsum('bci,boi->bco', chunk, M)
                nrm = jnp.sqrt(jnp.sum(chunk * chunk, axis=-1, keepdims=True))
                keys = chunk / jnp.maximum(nrm, NORM_EPS)
                k_mean = keys.mean(axis=1)
                v_target = value_gen(outputs).mean(axis=1)
                Mk = jnp.einsum('boi,bi->bo', M, k_mean)
                err = v_target - Mk
                update = err[:, :, None] * k_mean[:, None, :]
                M_new = alpha * M + eta * update
                gate = jax.nn.sigmoid(k_mean @ gate_w + gate_b[0])[:, None, None]
                M_new = gate * M_new + (1.0 - gate) * M
                M_norm = jnp.sqrt(jnp.sum(M_new * M_new, axis=(-2, -1), keepdims=True))
                scale = jnp.minimum(MAX_NORM / (M_norm + 1e-06), 1.0)
                return (M_new * scale, outputs)
            M_final, outs = jax.lax.scan(step, M0, x_chunks)
            outs = outs.transpose(1, 0, 2, 3).reshape(b, s, d)
            final_out = value_gen(outs)
            return (final_out, M_final)

        def _reference_tuple_inner(x, M_init, eta_w, eta_b, alpha_w, alpha_b, gate_w, gate_b, vg_w1, vg_w2):
            return _forward(x, M_init, eta_w, eta_b, alpha_w, alpha_b, gate_w, gate_b, vg_w1, vg_w2)
        return _reference_tuple_inner(x, M_init, eta_w, eta_b, alpha_w, alpha_b, gate_w, gate_b, vg_w1, vg_w2)[0]

    def _L0_xattn_ref(inputs, context, Wq, Wk, Wv, Wcq, Wck, Wcv, gamma, beta, W1, b1):
        import jax, jax.numpy as jnp
        import numpy as np
        B, S, E = (8, 256, 128)
        EPS = 0.001

        def _layer_norm(x, gamma, beta):
            mu = jnp.mean(x, axis=-1, keepdims=True)
            var = jnp.mean(jnp.square(x - mu), axis=-1, keepdims=True)
            return gamma * (x - mu) * jax.lax.rsqrt(var + EPS) + beta

        def _attention(q_in, k_in, v_in, WQ, WK, WV, causal):
            Q = jnp.einsum('bse,ed->bsd', q_in, WQ)
            K = jnp.einsum('bse,ed->bsd', k_in, WK)
            V = jnp.einsum('bse,ed->bsd', v_in, WV)
            d = K.shape[-1]
            scores = jnp.einsum('bqd,bkd->bqk', Q, K) / jnp.sqrt(jnp.float32(d))
            if causal:
                qlen, klen = (scores.shape[-2], scores.shape[-1])
                mask = jnp.triu(jnp.ones((qlen, klen), bool), k=1)
                scores = jnp.where(mask[None], -jnp.inf, scores)
            p = jax.nn.softmax(scores, axis=-1)
            return jnp.einsum('bqk,bkd->bqd', p, V)
        a = _attention(inputs, inputs, inputs, Wq, Wk, Wv, causal=True) + inputs
        h = _layer_norm(a, gamma, beta)
        c = _attention(h, context, context, Wcq, Wck, Wcv, causal=False) + h
        h = _layer_norm(c, gamma, beta)
        f = jax.nn.relu(jnp.einsum('bse,ed->bsd', h, W1) + b1)
        out = _layer_norm(f + h, gamma, beta)
        return jax.nn.relu(out)

    def _L0_ffn_ref(hidden_states, gate_w, dyn_gate_w, dyn_up_w, dyn_down_w, sh_gate_w, sh_up_w, sh_down_w):
        import jax, jax.numpy as jnp
        import numpy as np
        B, S, H = (2, 256, 128)
        E_DYN, E_FIX = (8, 1)
        I_DYN, I_FIX = (64, 256)
        TOP_K = 4
        TOP_P = 0.75
        JITTER_EPS = 0.1
        CAPACITY_FACTOR = 1.25
        MIN_CAPACITY = 4

        def _sparse_mixer(scores):
            T = scores.shape[0]
            rows = jnp.arange(T)
            masked_scores = scores
            mults, sels = ([], [])
            for _ in range(TOP_K):
                thr = jnp.max(masked_scores, axis=-1, keepdims=True)
                sel = jnp.argmax(masked_scores, axis=-1)
                factor = jnp.maximum(jnp.abs(scores), jnp.abs(thr))
                jmask = (thr - scores) / factor > 2.0 * JITTER_EPS
                gates = jax.nn.softmax(jnp.where(jmask, -jnp.inf, masked_scores), axis=-1)
                mult = jnp.take_along_axis(gates, sel[:, None], axis=-1)[:, 0]
                masked_scores = masked_scores.at[rows, sel].set(-jnp.inf)
                mults.append(mult)
                sels.append(sel)
            return (jnp.stack(mults, axis=-1), jnp.stack(sels, axis=-1))
        Bv, Sv, Hv = hidden_states.shape
        T = Bv * Sv
        x = hidden_states.reshape(T, Hv)
        full_logits = x @ gate_w.T
        dyn_logits = full_logits[:, :E_DYN]
        probs = jax.nn.softmax(dyn_logits, axis=-1)
        sorted_p = jnp.sort(probs, axis=-1)[:, ::-1]
        csum = jnp.cumsum(sorted_p, axis=-1)
        dyn_k = jnp.minimum(jnp.sum(csum < TOP_P, axis=-1) + 1, TOP_K)
        mult, sel = _sparse_mixer(dyn_logits)
        slot_valid = jnp.arange(TOP_K)[None, :] < dyn_k[:, None]
        mult = jnp.where(slot_valid, mult, 0.0)
        rows = jnp.arange(T)
        rw = jnp.zeros((T, E_DYN), x.dtype).at[rows[:, None], sel].add(mult)
        rw = rw / jnp.sum(rw, axis=-1, keepdims=True)
        mask_dyn = (rw > 0).astype(jnp.int32)
        cap = max(int(np.ceil(T / E_DYN * CAPACITY_FACTOR)), MIN_CAPACITY)
        mask_dyn = mask_dyn * (jnp.cumsum(mask_dyn, axis=0) <= cap)
        expert_mask = jnp.concatenate([mask_dyn, jnp.ones((T, E_FIX), jnp.int32)], axis=-1)
        maskf = expert_mask.astype(x.dtype)
        gw = jax.nn.softmax(jnp.where(expert_mask == 0, -jnp.inf, full_logits), axis=-1)
        gd = rw * jnp.sum(gw[:, :E_DYN], axis=-1, keepdims=True)
        global_w = jnp.concatenate([gd, gw[:, E_DYN:]], axis=-1) * maskf
        g = jnp.einsum('th,eih->tei', x, dyn_gate_w)
        u = jnp.einsum('th,eih->tei', x, dyn_up_w)
        y_dyn = jnp.einsum('tei,ehi->teh', jax.nn.silu(g) * u, dyn_down_w)
        out = jnp.einsum('te,teh->th', global_w[:, :E_DYN], y_dyn)
        gs = jnp.einsum('th,fih->tfi', x, sh_gate_w)
        us = jnp.einsum('th,fih->tfi', x, sh_up_w)
        y_sh = jnp.einsum('tfi,fhi->tfh', jax.nn.silu(gs) * us, sh_down_w)
        out = out + jnp.einsum('tf,tfh->th', global_w[:, E_DYN:], y_sh)
        return out.reshape(Bv, Sv, Hv)

    def _L1_attn_ref(hidden_states, Wq, Wk, Wv, q_conv_w, k_conv_w, v_conv_w, Wb, fir_w3, fir_w7, fir_w15, fir_w31, router_W1, router_b1, router_W2, router_b2, id_gate_W, id_gate_b, log_tau, o_norm_w, Wo):
        import jax, jax.numpy as jnp
        import numpy as np
        H, DK, DV, CHUNK = (4, 32, 32, 32)
        MIN_FLOOR, MAX_FLOOR, TEMP_MIN = (0.01, 0.1, 0.5)

        def _silu(x):
            return x * jax.nn.sigmoid(x)

        def _causal_dw_conv(x_bcl, w_ck):
            K = w_ck.shape[-1]
            return jax.lax.conv_general_dilated(x_bcl, w_ck[:, None, :], window_strides=(1,), padding=[(K - 1, 0)], feature_group_count=x_bcl.shape[1])

        def _l2norm(x):
            return x * jax.lax.rsqrt(jnp.sum(x * x, axis=-1, keepdims=True) + 1e-06)

        def _delta_rule_chunkwise(q, k, v, beta, chunk=CHUNK):
            b, h, L, dk = q.shape
            dv = v.shape[-1]
            n = L // chunk
            q = _l2norm(q)
            k = _l2norm(k)
            v = v * beta[..., None]
            kb = k * beta[..., None]
            qc, kc, vc, kbc = (t.reshape(b, h, n, chunk, -1) for t in (q, k, v, kb))
            A = jnp.einsum('bhncd,bhned->bhnce', kbc, kc)
            eye = jnp.eye(chunk, dtype=q.dtype)
            T = eye + jnp.tril(A, -1)
            inv = jax.scipy.linalg.solve_triangular(T, jnp.broadcast_to(eye, T.shape), lower=True, unit_diagonal=True)
            u = inv @ vc
            w = inv @ kbc
            strict = jnp.triu(jnp.ones((chunk, chunk), dtype=bool), 1)

            def step(S, xs):
                q_i, k_i, u_i, w_i = xs
                att = jnp.where(strict, 0.0, jnp.einsum('bhcd,bhed->bhce', q_i, k_i))
                u_adj = u_i - jnp.einsum('bhck,bhkd->bhcd', w_i, S)
                o = jnp.einsum('bhck,bhkd->bhcd', q_i, S) + att @ u_adj
                S = S + jnp.einsum('bhck,bhcd->bhkd', k_i, u_adj)
                return (S, o)
            mv = lambda t: jnp.moveaxis(t, 2, 0)
            S0 = jnp.zeros((b, h, dk, dv), dtype=q.dtype)
            S, outs = jax.lax.scan(step, S0, (mv(qc), mv(kc), mv(u), mv(w)))
            out = jnp.moveaxis(outs, 0, 2).reshape(b, h, L, dv)
            return (out, S)

        def _fir(x, filt):
            b, l, h, d = x.shape
            xc = x.transpose(0, 2, 3, 1).reshape(b, h * d, l)
            y = _causal_dw_conv(xc, filt.reshape(h * d, -1))
            return y.reshape(b, h, d, l).transpose(0, 3, 1, 2)
        B, L, D = hidden_states.shape
        conv = lambda x, w: _silu(_causal_dw_conv(x.transpose(0, 2, 1), w)).transpose(0, 2, 1)
        q = conv(hidden_states @ Wq, q_conv_w).reshape(B, L, H, DK)
        k = conv(hidden_states @ Wk, k_conv_w).reshape(B, L, H, DK)
        v_direct = conv(hidden_states @ Wv, v_conv_w).reshape(B, L, H, DV)
        beta = jax.nn.sigmoid(hidden_states @ Wb)
        delta_out, _ = _delta_rule_chunkwise(q.transpose(0, 2, 1, 3), k.transpose(0, 2, 1, 3), v_direct.transpose(0, 2, 1, 3), beta.transpose(0, 2, 1))
        delta_out = delta_out.transpose(0, 2, 1, 3)
        paths = [_fir(v_direct, f) for f in (fir_w3, fir_w7, fir_w15, fir_w31)] + [delta_out]
        p_value = jax.nn.sigmoid(hidden_states @ id_gate_W + id_gate_b)
        floor_tok = MIN_FLOOR + (MAX_FLOOR - MIN_FLOOR) * (1.0 - p_value)
        p_value_adj = (1.0 - floor_tok) * p_value
        context_mass = 1.0 - p_value_adj
        router_in = jnp.concatenate([hidden_states] + [p.reshape(B, L, H * DV) for p in paths], axis=-1)
        hmid = jax.nn.gelu(router_in @ router_W1 + router_b1, approximate=False)
        logits = (hmid @ router_W2 + router_b2).reshape(B, L, H, 5)
        tau = jnp.maximum(jnp.exp(log_tau), TEMP_MIN)
        probs = jax.nn.softmax(logits / tau[:, None], axis=-1)
        ctx = sum((probs[..., i:i + 1] * paths[i] for i in range(5)))
        o = context_mass[..., None] * ctx + p_value_adj[..., None] * v_direct
        o = o * jax.lax.rsqrt(jnp.mean(o * o, axis=-1, keepdims=True) + 1e-05) * o_norm_w
        return o.reshape(B, L, H * DV) @ Wo

    def _L1_xattn_ref(query, key, value, Wq, bq, Wk, bk, Wv, bv, Wo, bo):
        import jax, jax.numpy as jnp
        import numpy as np
        D_MODEL = 128
        d_model = query.shape[-1]
        q = jnp.einsum('bsd,ed->bse', query, Wq) + bq
        k = jnp.einsum('bsd,ed->bse', key, Wk) + bk
        v = jnp.einsum('bsd,ed->bse', value, Wv) + bv
        scores = jnp.einsum('bqe,bke->bqk', q, k) / jnp.sqrt(jnp.asarray(d_model, q.dtype))
        attn = jax.nn.softmax(scores, axis=-1)
        out = jnp.einsum('bqk,bke->bqe', attn, v)
        out = jnp.einsum('bqe,fe->bqf', out, Wo) + bo
        return out

    def _L1_ffn_ref(x, router_w, router_b, load_balancer, sw_w1, sw_w3, sw_w2, me_eq_w, me_eq_b, me_wv, me_bv, me_wo, me_bo, me_c1w, me_c1b, me_c2w, me_c2b, ce_syn_w, ce_syn_b, ce_wv, ce_bv, ce_wo, ce_bo, ce_n1g, ce_n1b, ce_f1w, ce_f1b, ce_f2w, ce_f2b, ce_n2g, ce_n2b, ce_gen_w, ce_gen_b, ml_w1, ml_b1, ml_w2, ml_b2):
        import jax, jax.numpy as jnp
        import numpy as np
        B, S, H, I, E, K = (4, 256, 128, 512, 4, 2)

        def _layer_norm(h, g, b, eps=1e-05):
            mu = h.mean(-1, keepdims=True)
            var = ((h - mu) ** 2).mean(-1, keepdims=True)
            return (h - mu) * jax.lax.rsqrt(var + eps) * g + b
        logits = jnp.einsum('bsh,he->bse', x, router_w) + router_b + load_balancer
        rw, sel = jax.lax.top_k(logits, K)
        rw = jax.nn.softmax(rw, axis=-1)
        e0 = jax.nn.silu(x @ sw_w1) * (x @ sw_w3) @ sw_w2
        eq = x @ me_eq_w + me_eq_b
        sym = (eq @ me_wv + me_bv) @ me_wo + me_bo
        e1 = jax.nn.gelu(sym @ me_c1w + me_c1b, approximate=False) @ me_c2w + me_c2b
        syn = x @ ce_syn_w + ce_syn_b
        attn = (syn @ ce_wv + ce_bv) @ ce_wo + ce_bo
        h2 = _layer_norm(syn + attn, ce_n1g, ce_n1b)
        ff = jax.nn.relu(h2 @ ce_f1w + ce_f1b) @ ce_f2w + ce_f2b
        h2 = _layer_norm(h2 + ff, ce_n2g, ce_n2b)
        e2 = h2 @ ce_gen_w + ce_gen_b
        e3 = jax.nn.gelu(x @ ml_w1 + ml_b1, approximate=False) @ ml_w2 + ml_b2
        stack = jnp.stack([e0, e1, e2, e3], axis=2)
        gathered = jnp.take_along_axis(stack, sel[..., None], axis=2)
        return (rw[..., None] * gathered).sum(axis=2)
    x = _layernorm(x + _L0_attn_ref(x, L0_attn_M_init, L0_attn_eta_w, L0_attn_eta_b, L0_attn_alpha_w, L0_attn_alpha_b, L0_attn_gate_w, L0_attn_gate_b, L0_attn_vg_w1, L0_attn_vg_w2), axis=-1)
    x = _layernorm(x + _L0_xattn_ref(x, ctx_1024, L0_xattn_Wq, L0_xattn_Wk, L0_xattn_Wv, L0_xattn_Wcq, L0_xattn_Wck, L0_xattn_Wcv, L0_xattn_gamma, L0_xattn_beta, L0_xattn_W1, L0_xattn_b1), axis=-1)
    x = _layernorm(x + _L0_ffn_ref(x, L0_ffn_gate_w, L0_ffn_dyn_gate_w, L0_ffn_dyn_up_w, L0_ffn_dyn_down_w, L0_ffn_sh_gate_w, L0_ffn_sh_up_w, L0_ffn_sh_down_w), axis=-1)
    x = _layernorm(x + _L1_attn_ref(x, L1_attn_Wq, L1_attn_Wk, L1_attn_Wv, L1_attn_q_conv_w, L1_attn_k_conv_w, L1_attn_v_conv_w, L1_attn_Wb, L1_attn_fir_w3, L1_attn_fir_w7, L1_attn_fir_w15, L1_attn_fir_w31, L1_attn_router_W1, L1_attn_router_b1, L1_attn_router_W2, L1_attn_router_b2, L1_attn_id_gate_W, L1_attn_id_gate_b, L1_attn_log_tau, L1_attn_o_norm_w, L1_attn_Wo), axis=-1)
    x = _layernorm(x + _L1_xattn_ref(x, ctx_1024, ctx_1024, L1_xattn_Wq, L1_xattn_bq, L1_xattn_Wk, L1_xattn_bk, L1_xattn_Wv, L1_xattn_bv, L1_xattn_Wo, L1_xattn_bo), axis=-1)
    x = _layernorm(x + _L1_ffn_ref(x, L1_ffn_router_w, L1_ffn_router_b, L1_ffn_load_balancer, L1_ffn_sw_w1, L1_ffn_sw_w3, L1_ffn_sw_w2, L1_ffn_me_eq_w, L1_ffn_me_eq_b, L1_ffn_me_wv, L1_ffn_me_bv, L1_ffn_me_wo, L1_ffn_me_bo, L1_ffn_me_c1w, L1_ffn_me_c1b, L1_ffn_me_c2w, L1_ffn_me_c2b, L1_ffn_ce_syn_w, L1_ffn_ce_syn_b, L1_ffn_ce_wv, L1_ffn_ce_bv, L1_ffn_ce_wo, L1_ffn_ce_bo, L1_ffn_ce_n1g, L1_ffn_ce_n1b, L1_ffn_ce_f1w, L1_ffn_ce_f1b, L1_ffn_ce_f2w, L1_ffn_ce_f2b, L1_ffn_ce_n2g, L1_ffn_ce_n2b, L1_ffn_ce_gen_w, L1_ffn_ce_gen_b, L1_ffn_ml_w1, L1_ffn_ml_b1, L1_ffn_ml_w2, L1_ffn_ml_b2), axis=-1)
    return x

_drawn_inputs = setup_inputs


def setup_inputs(seed=0):
    import zlib

    import numpy as np

    out = dict(_drawn_inputs(seed))
    spreads = {'L0_xattn_gamma': (1.0, 0.2),
     'L0_xattn_beta': (0.0, 0.1),
     'L0_xattn_b1': (0.0, 0.345),
     'L1_attn_router_b1': (0.0, 0.8),
     'L1_attn_router_b2': (0.0, 2.0),
     'L1_attn_id_gate_b': (2.0, 0.6),
     'L1_attn_log_tau': (0.0, 2.0),
     'L1_attn_o_norm_w': (1.0, 0.2),
     'L1_xattn_bq': (0.0, 0.376),
     'L1_xattn_bk': (0.0, 2.0),
     'L1_xattn_bv': (0.0, 0.1),
     'L1_xattn_bo': (0.0, 0.1),
     'L1_ffn_router_b': (0.0, 0.1),
     'L1_ffn_load_balancer': (1.0, 0.2),
     'L1_ffn_me_eq_b': (0.0, 0.8),
     'L1_ffn_me_bv': (0.0, 0.8),
     'L1_ffn_me_bo': (0.0, 0.8),
     'L1_ffn_me_c1b': (0.0, 2.0),
     'L1_ffn_me_c2b': (0.0, 2.0),
     'L1_ffn_ce_syn_b': (0.0, 0.445),
     'L1_ffn_ce_bv': (0.0, 0.779),
     'L1_ffn_ce_bo': (0.0, 0.668),
     'L1_ffn_ce_n1g': (1.0, 0.593),
     'L1_ffn_ce_n1b': (0.0, 0.592),
     'L1_ffn_ce_f1b': (0.0, 0.8),
     'L1_ffn_ce_f2b': (0.0, 2.0),
     'L1_ffn_ce_n2g': (1.0, 0.6),
     'L1_ffn_ce_n2b': (0.0, 0.572),
     'L1_ffn_ce_gen_b': (0.0, 0.1),
     'L1_ffn_ml_b1': (0.0, 0.768),
     'L1_ffn_ml_b2': (0.0, 0.1)}
    factors = {'L0_attn_eta_w': 200.0,
     'L0_attn_alpha_w': 8.0,
     'L0_attn_gate_w': 31.533,
     'L0_attn_vg_w1': 8.0,
     'L0_attn_vg_w2': 8.0,
     'L0_ffn_gate_w': 8.0,
     'L0_ffn_dyn_gate_w': 8.0,
     'L0_ffn_dyn_up_w': 8.0,
     'L0_ffn_dyn_down_w': 8.0,
     'L0_ffn_sh_gate_w': 8.0,
     'L0_ffn_sh_up_w': 8.0,
     'L0_ffn_sh_down_w': 8.0,
     'L1_attn_Wq': 8.0,
     'L1_attn_Wk': 8.0,
     'L1_attn_q_conv_w': 8.0,
     'L1_attn_k_conv_w': 8.0,
     'L1_attn_Wb': 32.142,
     'L1_attn_fir_w3': 34.976,
     'L1_attn_fir_w7': 8.0,
     'L1_attn_fir_w15': 8.0,
     'L1_attn_fir_w31': 8.0,
     'L1_attn_router_W1': 8.0,
     'L1_attn_router_W2': 8.0,
     'L1_attn_id_gate_W': 8.0,
     'L1_ffn_sw_w1': 8.0,
     'L1_ffn_sw_w3': 8.0,
     'L1_ffn_sw_w2': 8.0,
     'L1_ffn_me_eq_w': 8.0,
     'L1_ffn_me_wv': 8.0,
     'L1_ffn_me_wo': 8.0,
     'L1_ffn_me_c1w': 8.0,
     'L1_ffn_me_c2w': 8.0,
     'L1_ffn_ce_wv': 8.0,
     'L1_ffn_ce_wo': 4.43,
     'L1_ffn_ce_f1w': 8.0,
     'L1_ffn_ce_f2w': 7.324,
     'L1_ffn_ml_w1': 2.798}
    for name, (base, spread) in spreads.items():
        noise = np.random.default_rng([zlib.crc32(name.encode()), seed]).standard_normal(out[name].shape)
        drawn = base * np.exp(spread * noise) if base else spread * noise
        out[name] = jnp.asarray(drawn.astype(out[name].dtype))
    for name, factor in factors.items():
        out[name] = (out[name] * factor).astype(out[name].dtype)
    return out
```

```python
from contextlib import ExitStack

import numpy as np

import concourse.bass as bass
from concourse import mybir

F32 = mybir.dt.float32
U32 = mybir.dt.uint32
ALU = mybir.AluOpType
ACT = mybir.ActivationFunctionType
AX = mybir.AxisListType.X

P = 128
NB = 32
GB = 4
NG = NB // GB
GT = GB * P
NSTREAM = 2
HALF = 64
NE, TOPK = 8, 4
CAP = 640
NHT = 6
NH, DH = 4, 32
CH = 32
NP = NH * GB
FIRS = (3, 7, 15, 31)
FIR_GROUPS = [(f, kg) for f, k in enumerate(FIRS) for kg in range((k + 3) // 4)]
BIG = 1.0e30


class Mark:

    def __init__(self, lane, step):
        self.lane, self.step, self.used, self.value, self.finish = lane, step, False, None, None


def flat_marks(after):
    if isinstance(after, Mark):
        yield after
    elif after is not None:
        for a in after:
            yield from flat_marks(a)


class Lane:

    def __init__(self, sem, name):
        self.sem, self.name, self.count, self.free_at = sem, name, 0, 0.0


class Buf:

    def __init__(self, ap):
        self.ap, self.free = ap, []


class Stream:

    def __init__(self, prog, name, sbufs=(), banks=()):
        self.prog, self.name = prog, name
        self.sbufs, self.banks = [Buf(a) for a in sbufs], [Buf(a) for a in banks]
        self.queues = {e: [] for e in prog.engines}

    def put(self, engine, cost, fn, after=(), channel=None):
        marks = list(flat_marks(after))
        for m in marks:
            m.used = True
        mark = Mark(channel or self.prog.engines[engine], 16 if channel else 1)
        mark.used = bool(channel)
        self.queues[engine].append((cost, fn, marks, mark, engine))
        return mark

    def take(self):
        return self.sbufs.pop(0)

    def bank(self):
        return self.banks.pop(0)

    def give(self, buf, *readers):
        buf.free = list(readers)
        self.sbufs.append(buf)

    def give_bank(self, buf, *readers):
        buf.free = list(readers)
        self.banks.append(buf)

    def mm(self, out, lhsT, rhs, start=True, stop=True, after=()):
        n = 1
        for d in out.shape[1:]:
            n *= d
        m = out.shape[0]
        cost = max(n, 64) * 4 / 2.4 / (3.5 if m <= 32 else 1)
        return self.put("tensor", cost, lambda e: e.matmul(out, lhsT, rhs, start=start, stop=stop), after)

    def tr(self, out, in_, ident, after=()):
        return self.put("tensor", 60, lambda e: e.transpose(out, in_, ident), after)

    def act(self, out, in_, func, bias=None, scale=1.0, accum=None, after=()):
        n = 1
        for d in out.shape[1:]:
            n *= d
        kw = {}
        if bias is not None:
            kw["bias"] = bias
        if accum is not None:
            kw["accum_out"] = accum
        cost = 100 + n / 1.2 + (90 if bias is not None else 0) + (90 if accum is not None else 0)
        return self.put("scalar", cost, lambda e: e.activation(out, in_, func, scale=scale, **kw), after)

    def _vec(self, engine, out, fn, after, rate=1.0, fixed=60):
        n = 1
        for d in out.shape[1:]:
            n *= d
        cost = fixed + n / 0.96 / rate if engine == "vector" else 100 + 2.3 * n
        return self.put(engine, cost, fn, after)

    def tt(self, out, a, b, op, after=(), engine="vector"):
        return self._vec(engine, out, lambda e: e.tensor_tensor(out, a, b, op), after)

    def ts(self, out, a, s1, s2, op0, op1=None, after=(), engine="vector"):
        if op1 is None:
            return self._vec(engine, out, lambda e: e.tensor_scalar(out, a, s1, None, op0), after)
        return self._vec(engine, out, lambda e: e.tensor_scalar(out, a, s1, s2, op0, op1), after)

    def stt(self, out, a, s, b, op0, op1, after=()):
        return self._vec("vector", out, lambda e: e.scalar_tensor_tensor(
            out=out, in0=a, scalar=s, in1=b, op0=op0, op1=op1), after)

    def copy(self, out, in_, after=(), engine="vector"):
        if engine == "scalar":
            return self.act(out, in_, ACT.Copy, after=after)
        return self._vec(engine, out, lambda e: e.tensor_copy(out, in_), after)

    def red(self, out, in_, op, after=()):
        n = 1
        for d in in_.shape[1:]:
            n *= d
        return self.put("vector", 60 + n / 0.96, lambda e: e.tensor_reduce(out, in_, AX, op), after)

    def recip(self, out, in_, after=()):
        n = 1
        for d in out.shape[1:]:
            n *= d
        return self.put("vector", 60 + 6.4 * n, lambda e: e.reciprocal(out, in_), after)

    def power(self, out, in_, exponent, after=()):
        n = 1
        for d in out.shape[1:]:
            n *= d
        return self.put("gpsimd", 300 + 166 * n, lambda e: e.tensor_tensor(out, in_, exponent, ALU.pow), after)

    def dma(self, channel, out, in_, after=(), engine="sync"):
        return self.put(engine, 60, lambda e: e.dma_start(out, in_), after, channel=channel)


class Program:
    def __init__(self, nc, ctx):
        self.nc, self.ctx = nc, ctx
        self.engines = {e: Lane(ctx.enter_context(nc.semaphore("done_" + e)), e)
                        for e in ("tensor", "vector", "scalar", "gpsimd", "sync")}
        self.streams, self.order = [], {e: [] for e in self.engines}

    def stream(self, name, sbufs=(), banks=()):
        self.streams.append(Stream(self, name, sbufs, banks))
        return self.streams[-1]

    def channel(self, name):
        return Lane(self.ctx.enter_context(self.nc.semaphore(name)), name)

    def merge(self):
        heads = {(s, e): 0 for s in range(len(self.streams)) for e in self.engines}
        free_at = {e: 0.0 for e in self.engines}
        left = sum(len(q) for s in self.streams for q in s.queues.values())
        while left:
            best = None
            for (s, e), i in heads.items():
                q = self.streams[s].queues[e]
                if i >= len(q) or any(m.finish is None for m in q[i][2]):
                    continue
                ready = max([m.finish + 60 for m in q[i][2]], default=0.0)
                key = (max(ready, free_at[e]), ready, s)
                if best is None or key < best[0]:
                    best = (key, s, e)
            assert best, "the streams wait for each other"
            (start, _, _), s, e = best
            cost, fn, marks, mark, _ = self.streams[s].queues[e][heads[(s, e)]]
            heads[(s, e)] += 1
            free_at[e] = start + cost
            mark.finish = start + cost + (2000 if mark.step == 16 else 0)
            if e == "gpsimd":
                if self.order[e]:
                    marks = marks + [self.order[e][-1][2]]
                mark.used = True
            if mark.used:
                mark.lane.count += mark.step
                mark.value = mark.lane.count
            self.order[e].append((fn, marks, mark))
            left -= 1

    def emit(self):
        self.merge()
        with self.nc.Block() as block:
            enter = {"tensor": block.tensor, "vector": block.vector, "scalar": block.scalar,
                     "gpsimd": block.gpsimd, "sync": block.sync}
            for name, order in self.order.items():
                def body(e, order=order):
                    seen = {}
                    for fn, marks, mark in order:
                        need = {}
                        for m in marks:
                            need[m.lane] = max(need.get(m.lane, 0), m.value)
                        for lane, value in need.items():
                            if value > seen.get(lane, 0):
                                e.wait_ge(lane.sem, value)
                                seen[lane] = value
                        ins = fn(e)
                        if mark.used:
                            ins.then_inc(mark.lane.sem, mark.step)
                enter[name](body)


def build(nc, dram, cols, out, stop_after=99):
    ctx = ExitStack()
    with ctx:
        prog = Program(nc, ctx)

        def sb(name, shape, dt=F32):
            return ctx.enter_context(nc.sbuf_tensor(name, shape, dt))

        psum = ctx.enter_context(nc.psum_tensor("psum", [P, 8, GT], F32))

        setup = prog.stream("setup", banks=[psum[:, i, :] for i in range(8)])
        tiles, landed = {}, {}
        pairs = sb("pairs", [P, NSTREAM * 2, NP * P])
        once = pairs[:, :, :].rearrange("p a b -> p (a b)")
        once_at = 0
        for part in ("l0a", "const", "rows", "once_l0", "l0x", "l0f", "l1a", "once_rows", "once_l1", "l1x", "l1f"):
            n = sum(w for _, w in cols[part].values())
            if part.startswith("once"):
                tiles[part] = once[:, once_at:once_at + n]
                once_at += n
            else:
                tiles[part] = sb("sb_" + part, [P, n])[:, :]
            src = dram[part][0:1, :].to_broadcast([P, n]) if part.endswith("rows") else dram[part]
            landed[part] = setup.dma(prog.channel("ld_" + part), tiles[part], src)

        def w(part, piece, lo=0, n=None):
            first, width = cols[part][piece]
            n = width - lo if n is None else n
            return tiles[part][:, first + lo:first + lo + n]

        ident, ones = w("const", "ident"), w("const", "ones")
        up = w("const", "upto")
        cmask = w("const", "cmask")
        const, rows = landed["const"], landed["rows"]

        def temp(n):
            nonlocal once_at
            once_at += n
            assert once_at <= NSTREAM * 2 * NP * P
            return once[:, once_at - n:once_at]

        half, inv_half = sb("minus_half", [P, 32]), sb("plus_half", [P, 8])
        m_half = [setup.put("gpsimd", 100, lambda e: e.memset(half[:, :], -0.5)),
                  setup.put("gpsimd", 100, lambda e: e.memset(inv_half[:, :], 0.5))]

        def product(out_sb, n, terms, after, engine="vector"):
            bank = setup.bank()
            for i, (lhsT, rhs) in enumerate(terms):
                m = setup.mm(bank.ap[:, 0:n], lhsT, rhs, i == 0, i == len(terms) - 1,
                             after=[after, bank.free, const])
            c = setup.copy(out_sb, bank.ap[:, 0:n], after=[m], engine=engine)
            setup.give_bank(bank, c)
            return c

        la, ra = landed["l0a"], [landed["l0a"], rows, const]
        gates = sb("gates", [P, 3, P])
        for i, name in enumerate(("eta", "alpha", "gate")):
            m_gates = setup.ts(gates[:, i, :], ones, w("l0a", name), None, ALU.mult, after=ra)
        w1h = sb("w1h", [P, P])
        m_w1h = setup.ts(w1h[:, :], w("l0a", "w1T"), 0.5, None, ALU.mult, after=ra)
        hb = sb("half_gate_biases", [P, 3])
        m_hb = setup.ts(hb[:, :], w("rows", "gate_bias"), 0.5, None, ALU.mult, after=[rows])
        m0sq, m0col, m0all = temp(P), temp(1), sb("m0all", [P, 1])
        m = setup.tt(m0sq, w("l0a", "m0T"), w("l0a", "m0T"), ALU.mult, after=[la])
        m = setup.red(m0col, m0sq, ALU.add, after=[m])
        m_m0 = product(m0all[:, :], 1, [(ones, m0col)], [m])
        lx = landed["l0x"]
        a_self, a_cross = sb("a_self", [P, P]), sb("a_cross", [P, P])
        m_as = product(a_self[:, :], P, [(w("once_l0", "wqT"), w("once_l0", "wkT"))], landed["once_l0"])
        m_ac = product(a_cross[:, :], P, [(w("once_l0", "wcqT"), w("once_l0", "wckT"))], landed["once_l0"])
        lf = landed["l0f"]
        m_gt = setup.ts(w("l0f", "gate"), w("l0f", "gate"), 0.5, None, ALU.mult, after=[lf])
        l0f = [lf, m_gt]
        l1, o1 = landed["l1a"], [landed["once_l1"], landed["once_rows"]]
        wconv = sb("wconv", [P, 3, 4, P])
        for i, n in enumerate(("q", "k", "v")):
            taps = w("once_rows", n + "_conv").rearrange("p (s c) -> p s c", s=4)
            m_conv = setup.stt(wconv[:, i, :, :], taps, 0.5,
                               w("once_l1", "w" + n).unsqueeze(1).to_broadcast([P, 4, P]),
                               ALU.mult, ALU.mult, after=[o1])
        nfg = len(FIR_GROUPS)
        firw = sb("firw", [P, nfg * 4, CH])
        m_fir = setup.tt(firw[:, :, :], w("once_l1", "fir").unsqueeze(2).to_broadcast([P, nfg * 4, CH]),
                         w("once_l1", "eye32").unsqueeze(1).to_broadcast([P, nfg * 4, CH]), ALU.mult,
                         after=[o1])
        itau = sb("inverse_tau", [P, NH])
        m = setup.act(itau[:, :], w("rows", "log_tau"), ACT.Exp, after=[rows])
        m = setup.ts(itau[:, :], itau[:, :], 0.5, None, ALU.max, after=[m])
        m_tau = setup.recip(itau[:, :], itau[:, :], after=[m])
        l1a = [l1, m_conv, m_fir, m_tau]
        lc = landed["l1x"]
        wvo, bvb, bo_all = sb("wvo", [P, P]), temp(P), sb("bo_all", [P, P])
        m_wvo = product(wvo[:, :], P, [(w("once_l1", "x_wv"), w("once_l1", "x_woT"))], o1)
        m = setup.ts(bvb, ones, w("l1x", "bv"), None, ALU.mult, after=[lc, const])
        m = product(bo_all[:, :], P, [(bvb, w("once_l1", "x_woT"))], [m, o1])
        m_bo = setup.tt(bo_all[:, :], bo_all[:, :], w("rows", "bo"), ALU.add, after=[m, rows])
        l1x = [lc, m_wvo, m_bo]
        l2 = landed["l1f"]
        m_sw = setup.ts(w("l1f", "sw1"), w("l1f", "sw1"), 0.5, None, ALU.mult, after=[l2])
        r1, r2, wme = temp(256), temp(256), sb("wme", [P, 256])
        m1 = product(r1, 256, [(w("once_l1", "me_woT"), w("once_l1", "c1w"))], o1)
        m2 = product(r2, 256, [(w("once_l1", "me_wvT"), r1)], m1)
        m3 = product(wme[:, :], 256, [(w("once_l1", "me_eqT"), r2)], m2)
        bme = sb("bme", [P, 2])
        for k in range(2):
            m = product(bme[:, k:k + 1], 1, [(r2[:, k * P:k * P + P], w("l1f", "me_eq_b")),
                                             (r1[:, k * P:k * P + P], w("l1f", "me_bv")),
                                             (w("once_l1", "c1w", k * P, P), w("l1f", "me_bo"))], [m2, l2])
        m_bme = setup.tt(bme[:, :], bme[:, :], w("l1f", "c1b"), ALU.add, after=[m])
        rce, synb, bvc = (temp(P) for _ in range(3))
        wce, bce = sb("wce", [P, P]), sb("bce", [P, P])
        m = product(rce, P, [(w("once_l1", "ce_wvT"), w("once_l1", "ce_wo"))], o1)
        m = setup.tt(rce, rce, ident, ALU.add, after=[m, const])
        m_wce = product(wce[:, :], P, [(w("once_l1", "synT"), rce)], m)
        s1 = setup.ts(synb, ones, w("l1f", "ce_syn_b"), None, ALU.mult, after=[l2, const])
        s2 = setup.ts(bvc, ones, w("l1f", "ce_bv"), None, ALU.mult, after=[l2, const])
        m = product(bce[:, :], P, [(synb, rce), (bvc, w("once_l1", "ce_wo"))], [m, s1, s2])
        m_bce = setup.tt(bce[:, :], bce[:, :], w("rows", "ce_bo"), ALU.add, after=[m, rows])
        nfb = sb("n1b_plus_f2b", [P, 1])
        m_nfb = setup.tt(nfb[:, :], w("l1f", "n1b"), w("l1f", "f2b"), ALU.add, after=[l2])
        rbias = sb("router_bias", [P, 4])
        m_rb = setup.tt(rbias[:, :], w("rows", "router_b"), w("rows", "load_balancer"), ALU.add, after=[rows])
        l1f = [l2, m_sw, m3, m_bme, m_wce, m_bce, m_nfb, m_rb]
        setup_banks_free = [b.free for b in setup.banks]
        m_once = [m_m0, m_as, m_ac, m_conv, m_fir, m_wvo, m_bo, m3, m_bme, m_wce, m_bce]

        NBUF = 18
        pool = sb("pool", [P, NSTREAM, NBUF, GT])
        nbank = 8 // NSTREAM
        streams, own = [], []
        SM = 1400
        for s in range(NSTREAM):
            S = prog.stream(f"s{s}", [pool[:, s, i, :] for i in range(NBUF)],
                            [psum[:, s * nbank + i, :] for i in range(nbank)])
            for b in S.banks:
                b.free = [m for f in setup_banks_free for m in f]
            streams.append(S)
            o = {"small": sb(f"small{s}", [P, SM]),
                 "kk": pairs[:, 2 * s, :].rearrange("p (q t) -> p q t", q=NP),
                 "att": pairs[:, 2 * s + 1, :].rearrange("p (q t) -> p q t", q=NP),
                 "vs": sb(f"vshift{s}", [P, 4, GB, P]), "free": {"kk": m_once, "att": m_once}, "idx": sb(f"idx{s}", [P, GB, 8], U32),
                 "ch": {n: prog.channel(f"{n}{s}") for n in
                        ("xF", "xT", "cF", "ag", "xt", "out", "c2")},
                 "sh": [prog.channel(f"sh{s}_{i}") for i in range(4)]}
            o["m_vs"] = S.put("gpsimd", 2000, lambda e, o=o: e.memset(o["vs"][:, :, :, 0:3], 0.0))
            own.append(o)

        kk_dram, xt_dram = dram["kk"], dram["xt"]
        sol_a, sol_x, sol_t = sb("sol_a", [P, 32, 32]), sb("sol_x", [P, 32, 32]), sb("sol_t", [P, 256])
        solver = prog.stream("solver")
        sol_in, sol_out = prog.channel("sol_in"), prog.channel("sol_out")
        sol_state = {"read": [], "ready": {}, "fed": {}}
        carry = sb("taken_before", [P, NG * GB + 1, NE])
        m_carry = [setup.put("gpsimd", 100, lambda e: e.memset(carry[:, 0, :], 0.0))]

        def b4(ap):
            return ap.rearrange("p (b t) -> p b t", b=GB)

        def rep(ap, n):
            return ap.unsqueeze(2).to_broadcast([P, ap.shape[1], n])

        def rep_b(ap):
            return ap.unsqueeze(1).to_broadcast([P, GB, ap.shape[1]])

        class Small:

            def __init__(self, o, side, base, size):
                self.t, self.at, self.end, self.o, self.side = o["small"], base, base + size, o, side
                self.free = o["free"].get(side, [])

            def __call__(self, *shape):
                n = 1
                for d in shape:
                    n *= d
                ap = self.t[:, self.at:self.at + n]
                self.at += n
                assert self.at <= self.end
                if len(shape) == 2:
                    ap = ap.rearrange("p (a b) -> p a b", b=shape[1])
                if len(shape) == 3:
                    ap = ap.rearrange("p (a b c) -> p a b c", b=shape[1], c=shape[2])
                return ap

            def done(self, *marks):
                self.o["free"][self.side] = list(marks)

        def small(o, which):
            return Small(o, which, *{"ln": (0, 64), "st": (64, 1336)}[which])

        def norm(S, o, y, ready, eps, release=None):
            sm = small(o, "ln")
            st, mv, r = sm(GB, 6), sm(GB, 2), sm(GB)
            yb, out_b = b4(y), S.take()
            for b in range(GB):
                m = S.put("vector", 200, lambda e, b=b: e.bn_stats(st[:, b, :], yb[:, b, :]),
                          [ready, sm.free])
            for b in range(GB):
                m2_ = S.put("vector", 80, lambda e, b=b: e.bn_aggr(mv[:, b, :], st[:, b, :]), [m, sm.free])
            m = S.ts(r, mv[:, :, 1], eps, None, ALU.add, after=[m2_, sm.free])
            m = S.power(r, r, half[:, 0:GB], after=[m, m_half])
            for b in range(GB):
                m3_ = S.ts(b4(out_b.ap)[:, b, :], yb[:, b, :], mv[:, b, 0:1], r[:, b:b + 1], ALU.subtract,
                           ALU.mult, after=[m, out_b.free])
            sm.done(m3_)
            return out_b, m3_

        def to_feature(S, src, ready, engine="scalar", scale=None, bias=None, after=()):
            bank, out_b = S.bank(), S.take()
            for b in range(GB):
                m = S.tr(bank.ap[:, b * P:b * P + P], src[:, b * P:b * P + P], ident,
                         after=[ready, bank.free, const])
            if scale is None:
                m = S.copy(out_b.ap, bank.ap, after=[m, out_b.free], engine=engine)
            else:
                m = S.ts(out_b.ap, bank.ap, scale, bias, ALU.mult, ALU.add, after=[m, out_b.free, after])
            S.give_bank(bank, m)
            return out_b, m

        def proj(S, weight, src, ready, after, n=GT, engine="scalar", bias=None, func=None, scale=1.0):
            bank, out_b = S.bank(), S.take()
            m = S.mm(bank.ap[:, 0:n], weight, src, after=[ready, after, bank.free])
            if bias is None and func is None:
                m = S.copy(out_b.ap[:, 0:n], bank.ap[:, 0:n], after=[m, out_b.free], engine=engine)
            else:
                m = S.act(out_b.ap[:, 0:n], bank.ap[:, 0:n], func or ACT.Identity, bias=bias, scale=scale,
                          after=[m, out_b.free])
            S.give_bank(bank, m)
            return out_b, m

        def token_product(S, bank, terms, after):
            for b in range(GB):
                for i, (src, weight) in enumerate(terms):
                    m = S.mm(bank.ap[:, b * P:b * P + P], src[:, b * P:b * P + P], weight,
                             i == 0, i == len(terms) - 1, after=[after, bank.free])
            return m

        def attention(S, o, qF, kF, ready, causal):
            sm = small(o, "st")
            mx, sums = sm(GB), sm(GB)
            scale = float(P) ** -0.5
            bank = S.bank()
            for b in range(GB):
                m = S.mm(bank.ap[:, b * P:b * P + P], qF[:, b * P:b * P + P], kF[:, b * P:b * P + P],
                         after=[ready, bank.free])
            pr = S.take()
            src = bank.ap
            if causal:
                m = S.tt(b4(pr.ap), b4(bank.ap), rep_b(cmask), ALU.add, after=[m, pr.free, const])
                S.give_bank(bank, m)
                src = pr.ap
            m = S.red(mx, b4(src), ALU.max, after=[m, sm.free])
            m = S.ts(mx, mx, -scale, None, ALU.mult, after=[m])
            for b in range(GB):
                m2_ = S.act(pr.ap[:, b * P:b * P + P], src[:, b * P:b * P + P], ACT.Exp, bias=mx[:, b:b + 1],
                            scale=scale, accum=sums[:, b:b + 1], after=[m, pr.free, sm.free])
            if not causal:
                S.give_bank(bank, m2_)
            m = S.recip(sums, sums, after=[m2_])
            m = S.tt(b4(pr.ap), b4(pr.ap), rep(sums, P), ALU.mult, after=[m])
            sm.done(m)
            prT, m = to_feature(S, pr.ap, m)
            S.give(pr, m)
            return prT, m

        def l0_attention(S, o, g):
            sm = small(o, "st")
            fr = sm.free
            xF, xT = S.take(), S.take()
            m_xF = S.dma(o["ch"]["xF"], xF.ap, dram["xF"][:, g * GT:g * GT + GT], after=[xF.free])
            m_xT = S.dma(o["ch"]["xT"], b4(xT.ap), dram["x"][g * GB:g * GB + GB].rearrange("b t f -> t b f"),
                         after=[xT.free])
            xFb, xTb = b4(xF.ap), b4(xT.ap)
            yF, m_y = proj(S, w("l0a", "m0T"), xF.ap, m_xF, la)
            yFb = b4(yF.ap)
            sF, t = S.take(), S.take()
            sFb, tb = b4(sF.ap), b4(t.ap)

            def silu_half(c, ready):
                bank = S.bank()
                u = bank.ap[:, 0:GB * HALF].rearrange("p (b t) -> p b t", b=GB)
                m = S.mm(u, w1h[:, :], yFb[:, :, c * HALF:c * HALF + HALF], after=[ready, bank.free, m_w1h])
                m = S.act(tb[:, :, 0:HALF], u, ACT.Tanh, after=[m, t.free])
                m = S.stt(sFb[:, :, c * HALF:c * HALF + HALF], tb[:, :, 0:HALF], 1.0, u, ALU.add, ALU.mult,
                          after=[m, sF.free])
                S.give_bank(bank, m)
                return m

            m_s0 = silu_half(0, m_y)
            sbar, xbar, sq = sm(GB), sm(GB), sm(GB)
            m_sb = S.red(sbar, sFb[:, :, 0:HALF], ALU.add, after=[m_s0, fr])
            m_sb = S.ts(sbar, sbar, 1.0 / HALF, None, ALU.mult, after=[m_sb])
            m_xb = S.red(xbar, xFb[:, :, 0:HALF], ALU.add, after=[m_xF, fr])
            x2 = S.take()
            m = S.act(x2.ap[0:HALF, :], xT.ap[0:HALF, :], ACT.Square, after=[m_xT, x2.free])
            m = S.red(sq[0:HALF, :], b4(x2.ap)[0:HALF], ALU.add, after=[m, fr])
            S.give(x2, m)
            m = S.power(sq[0:HALF, :], sq[0:HALF, :], inv_half[0:HALF, 0:GB], after=[m, m_half])
            m = S.ts(sq[0:HALF, :], sq[0:HALF, :], 1e-5, float(HALF), ALU.max, ALU.mult, after=[m])
            m = S.recip(sq[0:HALF, :], sq[0:HALF, :], after=[m])
            bank = S.bank()
            for b in range(GB):
                mk = S.mm(bank.ap[:, b:b + 1], xTb[0:HALF, b, :], sq[0:HALF, b:b + 1], after=[m, bank.free])
            km, dk, vec = sm(GB), sm(GB), sm(3, GB)
            m_km = S.copy(km, bank.ap[:, 0:GB], after=[mk, fr])
            S.give_bank(bank, m_km)
            m_dk = S.stt(dk, xbar, 1.0 / HALF, km, ALU.mult, ALU.subtract, after=[m_km, m_xb, fr])
            bank = S.bank()
            S.mm(bank.ap[:, 0:GB], w("l0a", "w2T"), sbar, True, False, after=[m_sb, bank.free])
            S.mm(bank.ap[:, 0:GB], w("l0a", "m0T"), dk, False, True, after=[m_dk])
            S.mm(bank.ap[:, 8:8 + GB], w("l0a", "m0T"), km)
            m = S.mm(bank.ap[:, 16:16 + GB], gates[:, 2, :], km, after=[m_gates])
            err, mkv, gate = sm(GB), sm(GB), sm(GB)
            m_e = S.copy(err, bank.ap[:, 0:GB], after=[m, fr])
            m_mk = S.copy(mkv, bank.ap[:, 8:8 + GB], after=[m, fr])
            m_g = S.act(gate, bank.ap[:, 16:16 + GB], ACT.Tanh, scale=0.5, bias=hb[:, 2:3], after=[m_mk, fr, m_hb])
            S.give_bank(bank, m_mk, m_g)
            m_g = S.ts(gate, gate, 0.5, 0.5, ALU.mult, ALU.add, after=[m_g])
            bank = S.bank()
            n2 = GB * HALF
            for i in range(2):
                m = S.mm(bank.ap[:, i * n2:i * n2 + n2].rearrange("p (b t) -> p b t", b=GB),
                         gates[:, i, :], xFb[:, :, 0:HALF], after=[m_xF, m_gates, bank.free])
            for i in range(2):
                mt = S.act(t.ap[:, i * n2:i * n2 + n2], bank.ap[:, i * n2:i * n2 + n2], ACT.Tanh, scale=0.5,
                           bias=hb[:, i:i + 1], after=[m, m_s0, m_hb])
            S.give_bank(bank, mt)
            ea = sm(2 * GB)
            m = S.red(ea, t.ap.rearrange("p (k t) -> p k t", t=HALF), ALU.add, after=[mt, fr])
            m_eta = S.ts(ea[:, 0:GB], ea[:, 0:GB], 0.1 / HALF, 0.1, ALU.mult, ALU.add, after=[m])
            m_al = S.ts(ea[:, GB:], ea[:, GB:], 0.25 / HALF, -0.25, ALU.mult, ALU.add, after=[m])
            S.tt(vec[:, 0, :], err, mkv, ALU.mult, after=[m_e, m_mk, fr])
            S.tt(vec[:, 1, :], err, err, ALU.mult, after=[m_e, fr])
            m = S.tt(vec[:, 2, :], km, km, ALU.mult, after=[m_km, fr])
            bank = S.bank()
            md = S.mm(bank.ap[:, 0:3 * GB], ones, vec.rearrange("p a b -> p (a b)"), after=[m, bank.free, const])
            dots = sm(3, GB)
            m_d = S.copy(dots.rearrange("p a b -> p (a b)"), bank.ap[:, 0:3 * GB], after=[md, fr])
            S.give_bank(bank, m_d)
            c1, c2, n_, q_ = sm(GB), sm(GB), sm(GB), sm(GB)
            m = S.tt(c1, ea[:, GB:], gate, ALU.mult, after=[m_al, m_g, fr])
            m1_ = S.ts(c1, c1, 1.0, None, ALU.add, after=[m])
            m2_ = S.tt(c2, gate, ea[:, 0:GB], ALU.mult, after=[m_eta, m_g, fr])
            m = S.tt(n_, c1, c1, ALU.mult, after=[m1_, fr])
            m = S.ts(n_, n_, m0all[:, 0:1], None, ALU.mult, after=[m, m_m0])
            m3_ = S.tt(q_, c1, c2, ALU.mult, after=[m1_, m2_, fr])
            m3_ = S.stt(q_, q_, 2.0, dots[:, 0, :], ALU.mult, ALU.mult, after=[m3_, m_d])
            m = S.tt(n_, n_, q_, ALU.add, after=[m, m3_])
            m3_ = S.tt(q_, c2, c2, ALU.mult, after=[m])
            m3_ = S.tt(q_, q_, dots[:, 1, :], ALU.mult, after=[m3_])
            m3_ = S.tt(q_, q_, dots[:, 2, :], ALU.mult, after=[m3_])
            m = S.tt(n_, n_, q_, ALU.add, after=[m3_])
            m = S.ts(n_, n_, 0.0, None, ALU.max, after=[m])
            m = S.power(n_, n_, inv_half[:, 0:GB], after=[m, m_half])
            m = S.ts(n_, n_, 1e-6, None, ALU.add, after=[m])
            m = S.recip(n_, n_, after=[m])
            m = S.ts(n_, n_, 30.0, 1.0, ALU.mult, ALU.min, after=[m])
            m1_ = S.tt(c1, c1, n_, ALU.mult, after=[m])
            m2_ = S.tt(c2, c2, n_, ALU.mult, after=[m])
            m2_ = S.tt(c2, c2, err, ALU.mult, after=[m2_])
            kB = S.take()
            m = S.copy(b4(kB.ap), rep(km, P), after=[m_km, kB.free])
            bank = S.bank()
            u = bank.ap[:, 0:n2].rearrange("p (b t) -> p b t", b=GB)
            for b in range(GB):
                mk = S.mm(u[:, b, :], b4(kB.ap)[:, b, :], xFb[:, b, HALF:], after=[m, bank.free])
            S.give(kB, mk)
            m = S.tt(tb[:, :, 0:HALF], u, rep(c2, HALF), ALU.mult, after=[mk, m2_, ea and m_al])
            S.give_bank(bank, m)
            mm_ = S.tt(yFb[:, :, HALF:], yFb[:, :, HALF:], rep(c1, HALF), ALU.mult, after=[m1_, m_y])
            m_y2 = S.tt(yFb[:, :, HALF:], yFb[:, :, HALF:], tb[:, :, 0:HALF], ALU.add, after=[mm_, m])
            sm.done(m_y2, mk, m_e, m_mk)
            m_s1 = silu_half(1, [m_y2])
            S.give(xF, mk)
            bank = S.bank()
            m = token_product(S, bank, [(sF.ap, w("l0a", "w2T")), (yF.ap, ident)], [m_s1, m_y2, const])
            S.give(sF, m)
            S.give(yF, m)
            S.give(t, m_s1)
            m = S.tt(xT.ap, bank.ap, xT.ap, ALU.add, after=[m, m_xT])
            S.give_bank(bank, m)
            x1, m1_ = norm(S, o, xT.ap, m, 1e-5)
            S.give(xT, m1_)
            return x1, m1_

        def l0_cross(S, o, g, x1, ready):
            gam, bet = w("l0x", "gamma"), w("l0x", "beta")
            xF, m_x = to_feature(S, x1.ap, ready)
            cF = S.take()
            m_c = S.dma(o["ch"]["cF"], cF.ap, dram["cF"][:, g * GT:g * GT + GT], after=[cF.free])

            def block(src, m_src, keys, m_keys, a, m_a, wv, causal):
                q, m_q = proj(S, a, src, m_src, m_a)
                v = S.take()
                bank = S.bank()
                m = token_product(S, bank, [(keys, w("l0x", wv))], [m_keys, lx])
                m_v = S.copy(v.ap, bank.ap, after=[m, v.free], engine="scalar")
                S.give_bank(bank, m_v)
                pT, m_p = attention(S, o, q.ap, keys, [m_q, m_keys], causal)
                bank = S.bank()
                for b in range(GB):
                    c = slice(b * P, b * P + P)
                    S.mm(bank.ap[:, c], pT.ap[:, c], v.ap[:, c], True, False, after=[m_p, m_v, bank.free])
                    m = S.mm(bank.ap[:, c], src[:, c], ident, False, True, after=[m_src])
                S.give(q, m)
                S.give(v, m)
                S.give(pT, m)
                hx, m = norm(S, o, bank.ap, m, 1e-3)
                S.give_bank(bank, m)
                hF, m2_ = to_feature(S, hx.ap, m, scale=gam, bias=bet, after=[lx])
                S.give(hx, m2_)
                return hF, m2_

            hF, m_h = block(xF.ap, m_x, xF.ap, m_x, a_self[:, :], m_as, "wv", True)
            S.give(xF, m_h)
            h2F, m_h2 = block(hF.ap, m_h, cF.ap, m_c, a_cross[:, :], m_ac, "wcv", False)
            S.give(hF, m_h2)
            S.give(cF, m_h2)
            f, m = proj(S, w("l0x", "w1"), h2F.ap, m_h2, lx, bias=w("l0x", "b1"), func=ACT.Relu)
            m = S.tt(f.ap, f.ap, h2F.ap, ALU.add, after=[m])
            S.give(h2F, m)
            bank = S.bank()
            for b in range(GB):
                c = slice(b * P, b * P + P)
                m2_ = S.tr(bank.ap[:, c], f.ap[:, c], ident, after=[m, bank.free])
            S.give(f, m2_)
            y, m = norm(S, o, bank.ap, m2_, 1e-3)
            S.give_bank(bank, m)
            m = S.tt(b4(y.ap), b4(y.ap), rep_b(w("rows", "gamma")), ALU.mult, after=[m, rows])
            m = S.tt(b4(y.ap), b4(y.ap), rep_b(w("rows", "beta")), ALU.add, after=[m])
            m = S.stt(y.ap, y.ap, 0.0, x1.ap, ALU.max, ALU.add, after=[m, ready])
            S.give(x1, m)
            x2, m = norm(S, o, y.ap, m, 1e-5)
            S.give(y, m)
            return x2, m

        def l0_ffn(S, o, g, x2, ready):
            sm = small(o, "st")
            fr = sm.free
            xF, m_x = to_feature(S, x2.ap, ready)
            bank = S.bank()
            lgp = bank.ap[:, 0:GB * 9].rearrange("p (b e) -> p b e", b=GB)
            for b in range(GB):
                m = S.mm(lgp[:, b, :], xF.ap[:, b * P:b * P + P], w("l0f", "router"), after=[m_x, lf, bank.free])
            lg = sm(GB, 9)
            m_lg = S.copy(lg, lgp, after=[m, fr])
            S.give_bank(bank, m_lg)
            srt, ab, idf = sm(GB, 8), sm(GB, 8), sm(GB, 8)
            idx = o["idx"]
            for b in range(GB):
                m = S.put("vector", 70, lambda e, b=b: e.max(srt[:, b, :], lg[:, b, 0:8]), [m_lg, fr])
            m_srt = m
            for b in range(GB):
                m = S.put("vector", 140, lambda e, b=b: e.max_index(idx[:, b, :], srt[:, b, :], lg[:, b, 0:8]),
                          [m_srt, fr])
            m_idx = S.copy(idf, idx[:, :, :], after=[m, fr])
            m_ab = S.ts(ab, srt, -1.0, None, ALU.mult, after=[m_srt, fr])
            m_ab = S.tt(ab, ab, srt, ALU.max, after=[m_ab])
            shp = [P, GB, TOPK, 8]

            def over_i(a):
                return a[:, :, 0:TOPK].unsqueeze(3).to_broadcast(shp)

            def over_j(a):
                return a.unsqueeze(2).to_broadcast(shp)

            gap, lim = sm(GB, TOPK, 8), sm(GB, TOPK, 8)

            def flat(a):
                return a.rearrange("p a b c -> p (a b c)")

            m1_ = S.tt(gap, over_i(srt), over_j(srt), ALU.subtract, after=[m_srt, fr])
            m2_ = S.tt(lim, over_i(ab), over_j(ab), ALU.max, after=[m_ab, fr])
            m2_ = S.stt(flat(lim), flat(lim), 0.2, flat(gap), ALU.mult, ALU.is_ge, after=[m1_, m2_])
            m1_ = S.ts(flat(gap), flat(gap), 0.0, None, ALU.max, after=[m2_])
            m_e = S.act(flat(gap), flat(gap), ACT.Exp, scale=-1.0, after=[m1_])
            rank = w("const", "rank_ge").rearrange("p (j i) -> p j i", i=8).unsqueeze(1).to_broadcast(shp)
            m2_ = S.tt(lim, lim, rank, ALU.mult, after=[m2_, const])
            es, cs = sm(GB, 8), sm(GB, 8)
            m_es = S.copy(es, gap[:, :, 0, :], after=[m_e, fr])
            m = S.tt(flat(gap), flat(gap), flat(lim), ALU.mult, after=[m_es, m2_])
            mult = sm(GB, TOPK)
            m_mu = S.red(mult.rearrange("p a b -> p (a b)"), gap.rearrange("p a b c -> p (a b) c"), ALU.add,
                         after=[m, fr])
            m_mu = S.recip(mult, mult, after=[m_mu])
            tot, valid = sm(GB), sm(GB, TOPK)
            m_t = S.red(tot, es, ALU.add, after=[m_es, fr])
            m_t = S.ts(tot, tot, 0.75, None, ALU.mult, after=[m_t])
            m = S.copy(cs[:, :, 0:1], es[:, :, 0:1], after=[m_es, fr])
            for j in range(1, TOPK - 1):
                m = S.tt(cs[:, :, j:j + 1], cs[:, :, j - 1:j], es[:, :, j:j + 1], ALU.add, after=[m])
            m = S.tt(cs[:, :, 0:TOPK - 1], cs[:, :, 0:TOPK - 1], rep(tot, TOPK - 1), ALU.is_lt, after=[m, m_t])
            m = S.tt(mult[:, :, 1:], mult[:, :, 1:], cs[:, :, 0:TOPK - 1], ALU.mult, after=[m, m_mu])
            m_tm = S.red(tot, mult, ALU.add, after=[m])
            m_tm = S.recip(tot, tot, after=[m_tm])
            m1_ = S.tt(gap, idf[:, :, 0:TOPK].unsqueeze(3).to_broadcast(shp),
                       w("const", "iota").unsqueeze(1).unsqueeze(1).to_broadcast(shp), ALU.is_equal,
                       after=[m_idx, m_mu, const])
            m1_ = S.tt(gap, gap, mult.unsqueeze(3).to_broadcast(shp), ALU.mult, after=[m1_, m])
            rw, mask, keep = sm(GB, 8), sm(GB, 9), sm(GB, 8)
            m1_ = S.red(rw, gap.rearrange("p b j e -> p b e j"), ALU.add, after=[m1_, fr])
            m_k = S.ts(mask[:, :, 0:8], rw, 0.0, None, ALU.is_gt, after=[m1_, fr])
            m_rw = S.tt(rw, rw, rep(tot, 8), ALU.mult, after=[m_tm, m_k])
            m_cy = m_carry[0]
            for b in range(GB):
                i = g * GB + b
                m_cy = S.tt(carry[:, i + 1, :], carry[:, i, :], mask[:, b, 0:8], ALU.add, after=[m_k, m_cy])
            m_carry[0] = m_cy
            bank = S.bank()
            cnt = bank.ap[:, 0:GB * 8].rearrange("p (b e) -> p b e", b=GB)
            S.mm(cnt, up, mask[:, :, 0:8], True, False, after=[m_k, const, bank.free])
            m = S.mm(cnt, ones, carry[:, g * GB:g * GB + GB, :], False, True, after=[m_cy])
            m = S.ts(keep, cnt, float(CAP), None, ALU.is_le, after=[m, fr])
            S.give_bank(bank, m)
            m = S.tt(mask[:, :, 0:8], mask[:, :, 0:8], keep, ALU.mult, after=[m])
            m_m8 = S.put("vector", 60, lambda e: e.memset(mask[:, :, 8:9], 1.0), [fr])
            mxe = sm(GB)
            gl = sm(GB, 9)
            m2_ = S.ts(gl, mask, -1.0, BIG, ALU.add, ALU.mult, after=[m, m_m8, fr])
            m2_ = S.tt(lg, lg, mask, ALU.mult, after=[m2_, m_idx])
            m2_ = S.tt(gl, gl, lg, ALU.add, after=[m2_])
            m3_ = S.red(mxe, gl, ALU.max, after=[m2_, fr])
            m2_ = S.tt(gl, gl, rep(mxe, 9), ALU.subtract, after=[m3_])
            m2_ = S.act(gl, gl, ACT.Exp, after=[m2_])
            m3_ = S.red(mxe, gl, ALU.add, after=[m2_])
            m3_ = S.recip(mxe, mxe, after=[m3_])
            m2_ = S.tt(gl, gl, rep(mxe, 9), ALU.mult, after=[m3_])
            m3_ = S.red(mxe, gl[:, :, 0:8], ALU.add, after=[m2_])
            m3_ = S.tt(rw, rw, rep(mxe, 8), ALU.mult, after=[m3_, m_rw])
            m_w = S.tt(gl[:, :, 0:8], rw, mask[:, :, 0:8], ALU.mult, after=[m3_])
            bank, gw = S.bank(), S.take()
            for b in range(GB):
                m = S.tr(bank.ap[0:9, b * P:b * P + P], gl[:, b, :], ident, after=[m_w, bank.free, const])
            m_gw = S.copy(gw.ap[0:9, :], bank.ap[0:9, :], after=[m, gw.free], engine="scalar")
            S.give_bank(bank, m_gw)
            sm.done(m, m_gw, m_cy)
            acc = S.bank()
            t, h2 = S.take(), [S.take(), S.take()]
            m_use = [None, None]
            m_tu = None
            for k in range(NHT):
                h = h2[k % 2]
                bg, bu, bw = S.bank(), S.bank(), S.bank()
                m1_ = S.mm(bg.ap, w("l0f", "gate", k * P, P), xF.ap, after=[m_x, l0f, bg.free])
                m2_ = S.mm(bu.ap, w("l0f", "up", k * P, P), xF.ap, after=[bu.free])
                m3_ = S.mm(bw.ap, w("const", "expert", k * P, P)[0:9, :], gw.ap[0:9, :],
                           after=[m_gw, const, bw.free])
                m = S.act(t.ap, bg.ap, ACT.Tanh, after=[m1_, t.free, m_tu])
                m = S.stt(h.ap, t.ap, 1.0, bg.ap, ALU.add, ALU.mult, after=[m, h.free, m_use[k % 2]])
                m_tu = m
                S.give_bank(bg, m)
                m = S.tt(h.ap, h.ap, bu.ap, ALU.mult, after=[m, m2_])
                S.give_bank(bu, m)
                m = S.tt(h.ap, h.ap, bw.ap, ALU.mult, after=[m, m3_])
                S.give_bank(bw, m)
                for b in range(GB):
                    c = slice(b * P, b * P + P)
                    m_use[k % 2] = S.mm(acc.ap[:, c], h.ap[:, c], w("l0f", "down", k * P, P),
                                        k == 0 and b == 0, k == NHT - 1 and b == GB - 1,
                                        after=[m, acc.free])
            m = m_use[1]
            S.give(t, m)
            S.give(h2[0], m)
            S.give(h2[1], m)
            S.give(gw, m)
            S.give(xF, m)
            m = S.tt(x2.ap, acc.ap, x2.ap, ALU.add, after=[m, ready])
            S.give_bank(acc, m)
            x3, m2_ = norm(S, o, x2.ap, m, 1e-5)
            S.give(x2, m2_)
            return x3, m2_

        def solve(k):
            V = solver
            fed = sol_state["fed"][2 * k] + sol_state["fed"][2 * k + 1]
            m_in = V.dma(sol_in, sol_a[:, :, :].rearrange("p i j -> p (i j)"), kk_dram[k], after=[fed, sol_state["read"]])
            m = V.copy(sol_x[:, :, :].rearrange("p i j -> p (i j)"), w("const", "eye32flat"),
                       after=[const, sol_state["read"]])
            for j in range(CH - 1):
                nm, ni = j + 1, CH - 1 - j
                tmp = sol_t[:, 0:nm * ni].rearrange("p (m i) -> p m i", m=nm)
                m = V.tt(tmp, sol_x[:, 0:nm, j:j + 1].to_broadcast([P, nm, ni]),
                         sol_a[:, j + 1:, j].unsqueeze(1).to_broadcast([P, nm, ni]), ALU.mult,
                         after=[m, m_in])
                m = V.tt(sol_x[:, 0:nm, j + 1:], sol_x[:, 0:nm, j + 1:], tmp, ALU.subtract, after=[m])
            m_out = V.dma(sol_out, xt_dram[k], sol_x[:, :, :].rearrange("p i j -> p (i j)"), after=[m])
            sol_state["read"] = [m_out, m]
            sol_state["ready"][k] = m_out

        def l1_attention_front(S, o, g, x3, ready):
            sm = small(o, "st")
            fr = sm.free
            xF, m_x = to_feature(S, x3.ap, ready)
            xFb = b4(xF.ap)
            qkv, t = [], S.take()
            m_t = None
            for i in range(3):
                bank, q = S.bank(), S.take()
                for s in range(4):
                    m = S.mm(b4(bank.ap)[:, :, s:], wconv[:, i, s, :], xFb[:, :, 0:P - s], s == 0, s == 3,
                             after=[m_x, l1a, bank.free])
                m = S.act(t.ap, bank.ap, ACT.Tanh, after=[m, t.free, m_t])
                m_t = m = S.stt(q.ap, t.ap, 1.0, bank.ap, ALU.add, ALU.mult, after=[m, q.free])
                S.give_bank(bank, m)
                qkv.append((q, m))
            (q, m_q), (kk, m_k), (v, m_v) = qkv
            shifts = []
            for s in range(4):
                for c in range(4):
                    m = S.dma(o["sh"][s], o["vs"][32 * s:32 * s + 32, c, :, s:], b4(v.ap)[32 * c:32 * c + 32, :, 0:P - s],
                              after=[m_v, o["m_vs"], o["free"].get("vs")], engine="sync")
                shifts.append(m)
            x2a, x2b = S.take(), t
            m1_ = S.act(x2a.ap, q.ap, ACT.Square, after=[m_q, x2a.free])
            m2_ = S.act(x2b.ap, kk.ap, ACT.Square, after=[m_k, m_t])
            bank = S.bank()
            pn = bank.ap[:, 0:GB * 16].rearrange("p (b e) -> p b e", b=GB)
            hs = w("const", "heads")
            for b in range(GB):
                c = slice(b * P, b * P + P)
                S.mm(pn[:, b, 0:4], x2a.ap[:, c], hs, after=[m1_, bank.free, const])
                S.mm(pn[:, b, 4:8], x2b.ap[:, c], hs, after=[m2_])
                m = S.mm(pn[:, b, 8:16], xF.ap[:, c], w("l1a", "wb_id"), after=[l1])
            S.give(x2a, m)
            S.give(t, m)
            ss, r, z = sm(GB, 8), sm(GB, 8), sm(GB, 8)
            m1_ = S.ts(ss, pn[:, :, 0:8], 1e-6, None, ALU.add, after=[m, fr])
            m2_ = S.tt(z[:, :, 4:8], pn[:, :, 12:16], rep_b(w("rows", "id_b")), ALU.add, after=[m, fr, rows])
            m2_ = S.copy(z[:, :, 0:4], pn[:, :, 8:12], after=[m, fr])
            S.give_bank(bank, m2_)
            m_r = S.power(r, ss, half[:, 0:GB * 8].rearrange("p (b e) -> p b e", b=GB), after=[m1_, fr, m_half])
            m1_ = S.recip(ss, ss, after=[m_r])
            m2_ = S.act(z, z, ACT.Tanh, scale=0.5, after=[m2_])
            m2_ = S.ts(z, z, 0.5, 0.5, ALU.mult, ALU.add, after=[m2_])
            keep = {}
            gg, ng, rb, rq, padj, cm = (sm(NH, GB), sm(NH, GB), sm(GB, NH), sm(NH, GB), sm(GB, NH), sm(GB, NH))
            m_g = S.tt(gg.rearrange("p h b -> p b h"), z[:, :, 0:4], ss[:, :, 4:8], ALU.mult, after=[m1_, m2_, fr])
            m_ng = S.ts(ng, gg, -1.0, None, ALU.mult, after=[m_g, fr])
            m_rb = S.tt(rb, z[:, :, 0:4], r[:, :, 4:8], ALU.mult, after=[m_r, m2_, fr])
            m_rq = S.copy(rq.rearrange("p h b -> p b h"), r[:, :, 0:4], after=[m_r, fr])
            m = S.ts(padj, z[:, :, 4:8], 0.09, 0.9, ALU.mult, ALU.add, after=[m2_, fr])
            m = S.tt(padj, padj, z[:, :, 4:8], ALU.mult, after=[m])
            m_cm = S.ts(cm, padj, -1.0, 1.0, ALU.mult, ALU.add, after=[m, fr])
            bank, vT, rhs = S.bank(), S.take(), S.take()
            for b in range(GB):
                c = slice(b * P, b * P + P)
                m = S.tr(bank.ap[:, c], v.ap[:, c], ident, after=[m_v, bank.free, const])
            m_vT = S.copy(vT.ap, bank.ap, after=[m, vT.free])
            S.give_bank(bank, m_vT)
            S.give(v, m, *shifts)
            rhs_p = rhs.ap.rearrange("p (h b d) -> p b h d", h=NH, b=GB)
            m_rhs = S.tt(rhs_p, vT.ap.rearrange("p (b h d) -> p b h d", b=GB, h=NH),
                         rb.unsqueeze(3).to_broadcast([P, GB, NH, DH]), ALU.mult, after=[m_vT, m_rb, rhs.free])
            for dst, mov, m_mov, name in ((o["kk"], kk, m_k, "kk"), (o["att"], q, m_q, "att")):
                banks = [S.bank() for _ in range(NH)]
                for b in range(GB):
                    c = slice(b * P, b * P + P)
                    for h in range(NH):
                        d = slice(DH * h, DH * h + DH)
                        m = S.mm(banks[h].ap[:, c], kk.ap[d, c], mov.ap[d, c],
                                 after=[m_k, m_mov, [x for bb in banks for x in bb.free]])
                for h in range(NH):
                    dd = dst[:, h * GB:h * GB + GB, :]
                    if name == "kk":
                        m2_ = S.copy(dd, b4(banks[h].ap), after=[m, o["free"].get(name)],
                                     engine="scalar")
                    else:
                        m2_ = S.tt(dd, b4(banks[h].ap), rep_b(up), ALU.mult, after=[m, o["free"].get(name)])
                    S.give_bank(banks[h], m2_)
                if name == "kk":
                    m_kk = m2_
                else:
                    m_att = m2_
            S.give(q, m)
            S.give(kk, m)
            ag = S.take()
            agp = ag.ap.rearrange("p (q j) -> p q j", q=NP)
            fed = []
            for c in range(4):
                r_ = slice(CH * c, CH * c + CH)
                m = S.tt(agp[r_], o["kk"][r_, :, CH * c:CH * c + CH],
                         gg.rearrange("p h b -> p (h b)")[r_].unsqueeze(2).to_broadcast([CH, NP, CH]), ALU.mult,
                         after=[m_kk, m_g, ag.free], engine="gpsimd")
                dst = kk_dram[g // 2].rearrange("(s q c) (i j) -> s c i q j", s=2, c=4, j=CH)[g % 2, c]
                m = S.dma(o["ch"]["ag"], dst, agp[r_], after=[m])
                fed.append(m)
            sol_state["fed"][g] = [fed[-1]]
            S.give(ag, fed[-1])
            paths = []
            for f in range(4):
                bank, pf = S.bank(), S.take()
                kgs = [kg for ff, kg in FIR_GROUPS if ff == f]
                for n_, kg in enumerate(kgs):
                    for c in range(4):
                        col = FIR_GROUPS.index((f, kg)) * 4 + c
                        m = S.mm(b4(bank.ap)[32 * c:32 * c + 32, :, 4 * kg:], firw[:, col, :],
                                 o["vs"][:, c, :, 0:P - 4 * kg], n_ == 0, n_ == len(kgs) - 1,
                                 after=[shifts, bank.free, l1a])
                m2_ = S.copy(pf.ap, bank.ap, after=[m, pf.free], engine="scalar")
                S.give_bank(bank, m2_)
                paths.append((pf, m2_))
            o["free"]["vs"] = [m]
            return dict(sm=sm, xF=xF, m_x=m_x, vT=vT, m_vT=m_vT, rhs=rhs, m_rhs=m_rhs, ng=ng, m_ng=m_ng, rq=rq,
                        m_rq=m_rq, padj=padj, cm=cm, m_cm=m_cm, m_kk=m_kk, m_att=m_att, paths=paths)

        def l1_attention_back(S, o, g, x3, ready, s):
            sm, fr = s["sm"], s["sm"].free
            XT, YT = S.take(), S.take()
            xt, yt = (a.ap.rearrange("p (q i) -> p q i", q=NP) for a in (XT, YT))
            m_inv = sol_state["ready"][g // 2]
            for c in range(4):
                src = xt_dram[g // 2].rearrange("(s q c) (m i) -> s c m q i", s=2, c=4, i=CH)[g % 2, c]
                m_xt = S.dma(o["ch"]["xt"], xt[CH * c:CH * c + CH], src, after=[m_inv, XT.free])
            m_yt = S.tt(yt, xt, rep(s["ng"].rearrange("p h b -> p (h b)"), CH), ALU.mult,
                        after=[m_xt, s["m_ng"], YT.free])
            U, Pc = S.take(), S.take()
            u, pc, bp = (a.ap.rearrange("p (q d) -> p q d", q=NP) for a in (U, Pc, s["rhs"]))
            m_u = None
            bu = S.bank()
            ub = bu.ap.rearrange("p (q d) -> p q d", q=NP)
            bk = S.bank()
            pb = bk.ap.rearrange("p (q d) -> p q d", q=NP)
            for c in range(4):
                r_ = slice(CH * c, CH * c + CH)
                if c:
                    for q in range(NP):
                        m = S.mm(pb[r_, q, :], o["kk"][0:CH * c, q, r_], u[0:CH * c, q, :],
                                 after=[m_u, s["m_kk"], bk.free])
                    m_p = S.copy(pc[r_], pb[r_], after=[m, Pc.free])
                for q in range(NP):
                    m = S.mm(ub[r_, q, :], xt[r_, q, :], bp[r_, q, :], True, c == 0,
                             after=[m_xt, s["m_rhs"], bu.free])
                    if c:
                        m = S.mm(ub[r_, q, :], yt[r_, q, :], pc[r_, q, :], False, True, after=[m_p, m_yt])
                m_u = S.copy(u[r_], ub[r_], after=[m, U.free], engine="scalar")
            S.give_bank(bu, m_u)
            S.give_bank(bk, m_p)
            o["free"]["kk"] = [m]
            for x in (XT, YT, Pc, s["rhs"]):
                S.give(x, m)
            bank, oT = S.bank(), S.take()
            ob = bank.ap.rearrange("p (q d) -> p q d", q=NP)
            for q in range(NP):
                m = S.mm(ob[:, q, :], o["att"][:, q, :], u[:, q, :], after=[m_u, s["m_att"], bank.free])
            o["free"]["att"] = [m]
            S.give(U, m)
            m_o = S.tt(oT.ap.rearrange("p (b h d) -> p h b d", b=GB, h=NH),
                       bank.ap.rearrange("p (h b d) -> p h b d", h=NH, b=GB),
                       s["rq"].unsqueeze(3).to_broadcast([P, NH, GB, DH]), ALU.mult, after=[m, s["m_rq"], oT.free])
            S.give_bank(bank, m_o)
            oF, m_oF = to_feature(S, oT.ap, m_o)
            srcs = [(s["xF"], s["m_x"])] + s["paths"] + [(oF, m_oF)]
            hid = []
            for k in range(2):
                bank, hb_ = S.bank(), S.take()
                for i, (src, m_s) in enumerate(srcs):
                    m = S.mm(bank.ap, w("l1a", "rw1", i * 256 + k * P, P), src.ap, i == 0, i == len(srcs) - 1,
                             after=[m_s, bank.free, l1])
                m = S.act(hb_.ap, bank.ap, ACT.Gelu, bias=w("l1a", "rb1", k, 1), after=[m, hb_.free])
                S.give_bank(bank, m)
                hid.append((hb_, m))
            S.give(s["xF"], m)
            S.give(oF, m)
            bank = S.bank()
            lp = bank.ap[:, 0:GB * 20].rearrange("p (b e) -> p b e", b=GB)
            for b in range(GB):
                for k in range(2):
                    m = S.mm(lp[:, b, :], hid[k][0].ap[:, b * P:b * P + P], w("l1a", "rw2", k * 20, 20), k == 0,
                             k == 1, after=[hid[k][1], bank.free])
            for k in range(2):
                S.give(hid[k][0], m)
            wt, mx = sm(GB, 20), sm(NP)
            m = S.tt(wt, lp, rep_b(w("rows", "rb2")), ALU.add, after=[m, rows, fr])
            S.give_bank(bank, m)
            w4 = wt.rearrange("p b (h i) -> p b h i", i=5)
            w3 = wt.rearrange("p b (h i) -> p (b h) i", i=5)
            m = S.tt(w4, w4, itau[:, :].unsqueeze(1).unsqueeze(3).to_broadcast([P, GB, NH, 5]), ALU.mult,
                     after=[m, m_tau])
            m2_ = S.red(mx, w3, ALU.max, after=[m, fr])
            m = S.tt(w3, w3, rep(mx, 5), ALU.subtract, after=[m2_])
            m = S.act(wt, wt, ACT.Exp, after=[m])
            m2_ = S.red(mx, w3, ALU.add, after=[m])
            m2_ = S.recip(mx, mx, after=[m2_])
            m2_ = S.tt(mx, mx, s["cm"].rearrange("p b h -> p (b h)"), ALU.mult, after=[m2_, s["m_cm"]])
            m_w = S.tt(w3, w3, rep(mx, 5), ALU.mult, after=[m2_])
            acc, tmp = S.take(), [S.take(), S.take()]

            def hd(ap):
                return ap.rearrange("p (q d) -> p q d", d=DH)

            m_a = S.tt(hd(acc.ap), hd(oT.ap), rep(w3[:, :, 4], DH), ALU.mult, after=[m_w, m_o, acc.free])
            m_tp = [None, None]
            for i, (pf, m_pf) in enumerate(s["paths"]):
                bank = S.bank()
                for b in range(GB):
                    c = slice(b * P, b * P + P)
                    m = S.tr(bank.ap[:, c], pf.ap[:, c], ident, after=[m_pf, bank.free])
                S.give(pf, m)
                tt_ = tmp[i % 2]
                m = S.tt(hd(tt_.ap), hd(bank.ap), rep(w3[:, :, i], DH), ALU.mult,
                         after=[m, m_w, tt_.free, m_tp[i % 2]])
                S.give_bank(bank, m)
                m_tp[i % 2] = m_a = S.tt(acc.ap, acc.ap, tt_.ap, ALU.add, after=[m, m_a], engine="gpsimd")
            m = S.tt(hd(oT.ap), hd(s["vT"].ap), rep(s["padj"].rearrange("p b h -> p (b h)"), DH), ALU.mult,
                     after=[m_oF, m_a, s["m_vT"]])
            S.give(s["vT"], m)
            m_a = S.tt(acc.ap, acc.ap, oT.ap, ALU.add, after=[m, m_a])
            m = S.act(oT.ap, acc.ap, ACT.Square, after=[m_a])
            ms = sm(NP)
            m = S.red(ms, hd(oT.ap), ALU.add, after=[m, fr])
            m = S.ts(ms, ms, 1.0 / DH, 1e-5, ALU.mult, ALU.add, after=[m])
            m = S.power(ms, ms, half[:, 0:NP], after=[m, m_half])
            m = S.tt(hd(acc.ap), hd(acc.ap), rep(ms, DH), ALU.mult, after=[m])
            sm.done(m, s["m_g"] if "m_g" in s else m)
            S.give(oT, m)
            for x in tmp:
                S.give(x, m_a)
            nF, m2_ = to_feature(S, acc.ap, m, scale=w("l1a", "onw"), bias=0.0, after=[l1])
            S.give(acc, m2_)
            bank = S.bank()
            m = token_product(S, bank, [(nF.ap, w("l1a", "wo"))], [m2_])
            S.give(nF, m)
            m = S.tt(x3.ap, bank.ap, x3.ap, ALU.add, after=[m, ready])
            S.give_bank(bank, m)
            x4, m2_ = norm(S, o, x3.ap, m, 1e-5)
            S.give(x3, m2_)
            return x4, m2_

        def l1_cross(S, o, g, x4, ready):
            xF, m_x = to_feature(S, x4.ap, ready)
            cF = S.take()
            m_c = S.dma(o["ch"]["c2"], cF.ap, dram["cF"][:, g * GT:g * GT + GT], after=[cF.free])
            q, m_q = proj(S, w("l1x", "wqT"), xF.ap, m_x, l1x, bias=w("l1x", "bq"))
            S.give(xF, m_q)
            k, m_k = proj(S, w("l1x", "wkT"), cF.ap, m_c, l1x, bias=w("l1x", "bk"))
            bank, v = S.bank(), S.take()
            m = token_product(S, bank, [(cF.ap, wvo[:, :])], [m_c, l1x])
            S.give(cF, m)
            m_v = S.tt(b4(v.ap), b4(bank.ap), rep_b(bo_all[:, :]), ALU.add, after=[m, v.free, l1x])
            S.give_bank(bank, m_v)
            pT, m_p = attention(S, o, q.ap, k.ap, [m_q, m_k], False)
            S.give(q, m_p)
            S.give(k, m_p)
            bank = S.bank()
            for b in range(GB):
                c = slice(b * P, b * P + P)
                m = S.mm(bank.ap[:, c], pT.ap[:, c], v.ap[:, c], after=[m_p, m_v, bank.free])
            S.give(pT, m)
            S.give(v, m)
            m = S.tt(x4.ap, bank.ap, x4.ap, ALU.add, after=[m, ready])
            S.give_bank(bank, m)
            x5, m2_ = norm(S, o, x4.ap, m, 1e-5)
            S.give(x4, m2_)
            return x5, m2_

        def l1_ffn(S, o, g, x5, ready):
            sm = small(o, "st")
            fr = sm.free
            xF, m_x = to_feature(S, x5.ap, ready)
            bank = S.bank()
            lgp = bank.ap[:, 0:GB * 4].rearrange("p (b e) -> p b e", b=GB)
            for b in range(GB):
                m = S.mm(lgp[:, b, :], xF.ap[:, b * P:b * P + P], w("l1f", "router"), after=[m_x, l2, bank.free])
            lg, top, idf, wt, pr2 = sm(GB, 8), sm(GB, 8), sm(GB, 8), sm(GB, 2), sm(GB, 4)
            idx = o["idx"]
            m1_ = S.put("vector", 60, lambda e: e.memset(lg[:, :, 4:8], -BIG), [fr])
            m = S.tt(lg[:, :, 0:4], lgp, rep_b(rbias[:, :]), ALU.add, after=[m, fr, l1f])
            S.give_bank(bank, m)
            for b in range(GB):
                m2_ = S.put("vector", 70, lambda e, b=b: e.max(top[:, b, :], lg[:, b, :]), [m, m1_, fr])
            m_top = m2_
            for b in range(GB):
                m2_ = S.put("vector", 140, lambda e, b=b: e.max_index(idx[:, b, :], top[:, b, :], lg[:, b, :]),
                            [m_top, fr])
            m_idx = S.copy(idf, idx[:, :, :], after=[m2_, fr])
            m = S.tt(wt[:, :, 1:2], top[:, :, 1:2], top[:, :, 0:1], ALU.subtract, after=[m_top, fr])
            m = S.act(wt[:, :, 1:2], wt[:, :, 1:2], ACT.Exp, after=[m])
            m = S.ts(wt[:, :, 0:1], wt[:, :, 1:2], 1.0, None, ALU.add, after=[m])
            m = S.recip(wt[:, :, 0:1], wt[:, :, 0:1], after=[m])
            m = S.tt(wt[:, :, 1:2], wt[:, :, 1:2], wt[:, :, 0:1], ALU.mult, after=[m])
            we = sm(GB, 4)
            iota = rep_b(w("const", "iota", 0, 4))
            shp = [P, GB, 4]
            m1_ = S.tt(we, idf[:, :, 0:1].to_broadcast(shp), iota, ALU.is_equal, after=[m_idx, fr])
            m1_ = S.tt(we, we, wt[:, :, 0:1].to_broadcast(shp), ALU.mult, after=[m1_, m])
            m2_ = S.tt(pr2, idf[:, :, 1:2].to_broadcast(shp), iota, ALU.is_equal, after=[m_idx, fr])
            m2_ = S.tt(pr2, pr2, wt[:, :, 1:2].to_broadcast(shp), ALU.mult, after=[m2_, m])
            m_w = S.tt(we, we, pr2, ALU.add, after=[m1_, m2_])
            bank, wT = S.bank(), S.take()
            for b in range(GB):
                m = S.tr(bank.ap[0:4, b * P:b * P + P], we[:, b, :], ident, after=[m_w, bank.free, const])
            m = S.copy(wT.ap[0:4, :], bank.ap[0:4, :], after=[m, wT.free], engine="scalar")
            S.give_bank(bank, m)
            bank = S.bank()
            for b in range(GB):
                c = slice(b * P, b * P + P)
                m2_ = S.mm(bank.ap[:, c], wT.ap[0:4, c], w("l1f", "ebias")[0:4, :],
                           after=[m, bank.free])
            S.give(wT, m2_)
            m_y = S.tt(x5.ap, bank.ap, x5.ap, ALU.add, after=[m2_, ready])
            S.give_bank(bank, m_y)

            def add_expert(e, bank, m, m_y):
                for b in range(GB):
                    c = slice(b * P, b * P + P)
                    m2_ = S.stt(x5.ap[:, c], bank.ap[:, c], we[:, b, e:e + 1], x5.ap[:, c], ALU.mult, ALU.add,
                                after=[m, m_y, m_w])
                S.give_bank(bank, m2_)
                return m2_

            acc, t, hh = S.bank(), S.take(), [S.take(), S.take()]
            m_use, m_tu = [None, None], None
            for k in range(4):
                h = hh[k % 2]
                bg, bu = S.bank(), S.bank()
                m1_ = S.mm(bg.ap, w("l1f", "sw1", k * P, P), xF.ap, after=[m_x, l1f, bg.free])
                m2_ = S.mm(bu.ap, w("l1f", "sw3", k * P, P), xF.ap, after=[bu.free])
                m = S.act(t.ap, bg.ap, ACT.Tanh, after=[m1_, t.free, m_tu])
                m_tu = m = S.stt(h.ap, t.ap, 1.0, bg.ap, ALU.add, ALU.mult, after=[m, h.free, m_use[k % 2]])
                S.give_bank(bg, m)
                m = S.tt(h.ap, h.ap, bu.ap, ALU.mult, after=[m, m2_])
                S.give_bank(bu, m)
                for b in range(GB):
                    c = slice(b * P, b * P + P)
                    m_use[k % 2] = S.mm(acc.ap[:, c], h.ap[:, c], w("l1f", "sw2", k * P, P), k == 0 and b == 0,
                                        k == 3 and b == GB - 1, after=[m, acc.free])
            S.give(t, m_tu)
            m_y = add_expert(0, acc, m_use[1], m_y)

            def gelu_expert(e, nk, w1_, bias, w2_, m_y, m_use):
                acc = S.bank()
                for k in range(nk):
                    h = hh[k % 2]
                    bg = S.bank()
                    m = S.mm(bg.ap, w1_(k), xF.ap, after=[m_x, l1f, bg.free])
                    m = S.act(h.ap, bg.ap, ACT.Gelu, bias=bias(k), after=[m, h.free, m_use[k % 2]])
                    S.give_bank(bg, m)
                    for b in range(GB):
                        c = slice(b * P, b * P + P)
                        m_use[k % 2] = S.mm(acc.ap[:, c], h.ap[:, c], w2_(k), k == 0 and b == 0,
                                            k == nk - 1 and b == GB - 1, after=[m, acc.free])
                return add_expert(e, acc, m_use[1], m_y)

            m_y = gelu_expert(1, 2, lambda k: wme[:, k * P:k * P + P], lambda k: bme[:, k:k + 1],
                              lambda k: w("l1f", "c2w", k * P, P), m_y, m_use)
            m_y = gelu_expert(3, 4, lambda k: w("l1f", "ml1", k * P, P), lambda k: w("l1f", "mlb1", k, 1),
                              lambda k: w("l1f", "ml2", k * P, P), m_y, m_use)
            bank, y = S.bank(), S.take()
            m = token_product(S, bank, [(xF.ap, wce[:, :])], [m_x, l1f])
            S.give(xF, m)
            m = S.tt(b4(y.ap), b4(bank.ap), rep_b(bce[:, :]), ALU.add, after=[m, y.free, l1f])
            S.give_bank(bank, m)
            xh, m = norm(S, o, y.ap, m, 1e-5)
            S.give(y, m)
            bank, hF, rF = S.bank(), S.take(), S.take()
            for b in range(GB):
                c = slice(b * P, b * P + P)
                m2_ = S.tr(bank.ap[:, c], xh.ap[:, c], ident, after=[m, bank.free])
            S.give(xh, m2_)
            m_h = S.ts(hF.ap, bank.ap, w("l1f", "n1g"), w("l1f", "n1b"), ALU.mult, ALU.add, after=[m2_, hF.free, l1f])
            m_r = S.ts(rF.ap, bank.ap, w("l1f", "n1g"), nfb[:, 0:1], ALU.mult, ALU.add, after=[m2_, rF.free, l1f])
            S.give_bank(bank, m_r)
            acc = S.bank()
            for b in range(GB):
                c = slice(b * P, b * P + P)
                m = S.mm(acc.ap[:, c], rF.ap[:, c], ident, b == 0, False, after=[m_r, acc.free])
            S.give(rF, m)
            for k in range(2):
                h = hh[k % 2]
                bg = S.bank()
                m = S.mm(bg.ap, w("l1f", "f1w", k * P, P), hF.ap, after=[m_h, bg.free])
                m = S.act(h.ap, bg.ap, ACT.Relu, bias=w("l1f", "f1b", k, 1), after=[m, m_use[k % 2]])
                S.give_bank(bg, m)
                for b in range(GB):
                    c = slice(b * P, b * P + P)
                    m_use[k] = S.mm(acc.ap[:, c], h.ap[:, c], w("l1f", "f2w", k * P, P), False,
                                    k == 1 and b == GB - 1, after=[m])
            for x in (hF, hh[0], hh[1]):
                S.give(x, m_use[1])
            xh, m = norm(S, o, acc.ap, m_use[1], 1e-5)
            S.give_bank(acc, m)
            hF, m2_ = to_feature(S, xh.ap, m, scale=w("l1f", "n2g"), bias=w("l1f", "n2b"), after=[l1f])
            S.give(xh, m2_)
            bank = S.bank()
            m = token_product(S, bank, [(hF.ap, w("l1f", "gen"))], [m2_])
            S.give(hF, m)
            m_y = add_expert(2, bank, m, m_y)
            sm.done(m_y)
            x6, m = norm(S, o, x5.ap, m_y, 1e-5)
            S.give(x5, m)
            return x6, m

        last = []

        def finish(S, o, g, x, m):
            m2_ = S.dma(o["ch"]["out"], out[g * GB:g * GB + GB].rearrange("b t f -> t b f"), b4(x.ap), after=[m])
            S.give(x, m2_)
            last.append(m2_)

        for k in range(NG // NSTREAM):
            state = []
            for i in range(NSTREAM):
                S, o, g = streams[i], own[i], k * NSTREAM + i
                x, m = l0_attention(S, o, g)
                if stop_after >= 2:
                    x, m = l0_cross(S, o, g, x, m)
                if stop_after >= 3:
                    x, m = l0_ffn(S, o, g, x, m)
                st = l1_attention_front(S, o, g, x, m) if stop_after >= 4 else None
                state.append((x, m, st))
            if stop_after >= 4:
                solve(k)
            for i in range(NSTREAM):
                S, o, g = streams[i], own[i], k * NSTREAM + i
                x, m, st = state[i]
                if stop_after >= 4:
                    x, m = l1_attention_back(S, o, g, x, m, st)
                if stop_after >= 5:
                    x, m = l1_cross(S, o, g, x, m)
                if stop_after >= 6:
                    x, m = l1_ffn(S, o, g, x, m)
                finish(S, o, g, x, m)
        tail = prog.stream("tail")
        tail.put("sync", 50, lambda e: e.nop(), after=last)
        prog.emit()


def _pack(inp):
    a = {k: np.asarray(v) for k, v in inp.items()}
    f = np.float32

    def col(x, n=1):
        return x.reshape(n, P).T

    def tiles(x):
        return x.reshape(-1, P, x.shape[1]).transpose(1, 0, 2).reshape(P, -1)

    t, s = np.arange(P)[:, None], np.arange(P)[None, :]
    rank = (np.arange(8)[None, :] >= np.arange(TOPK)[:, None]).astype(f).reshape(1, -1)
    expert = np.zeros((P, NHT * P), f)
    for e in range(9):
        lo = 64 * e
        expert[e, lo:lo + (64 if e < 8 else 256)] = 1.0
    const = dict(ident=np.eye(P, dtype=f), ones=np.ones((P, P), f), upto=(t <= s).astype(f),
                 cmask=np.where(s > t, f(-BIG), f(0)), rank_ge=np.repeat(rank, P, 0),
                 iota=np.repeat(np.arange(8, dtype=f)[None], P, 0), expert=expert,
                 eye32flat=np.repeat(np.eye(32, dtype=f).reshape(1, -1), P, 0),
                 heads=np.repeat(np.eye(NH, dtype=f), DH, 0))
    rows = dict(gate_bias=np.concatenate([a["L0_attn_eta_b"], a["L0_attn_alpha_b"], a["L0_attn_gate_b"]]),
                gamma=a["L0_xattn_gamma"], beta=a["L0_xattn_beta"],
                log_tau=a["L1_attn_log_tau"], bo=a["L1_xattn_bo"],
                ce_bo=a["L1_ffn_ce_bo"], router_b=a["L1_ffn_router_b"], load_balancer=a["L1_ffn_load_balancer"],
                id_b=a["L1_attn_id_gate_b"], rb2=a["L1_attn_router_b2"])
    once_rows = dict(q_conv=a["L1_attn_q_conv_w"].T[::-1], k_conv=a["L1_attn_k_conv_w"].T[::-1],
                     v_conv=a["L1_attn_v_conv_w"].T[::-1])
    rows, once_rows = ({k: v.reshape(1, -1) for k, v in r.items()} for r in (rows, once_rows))
    l0a = dict(m0T=a["L0_attn_M_init"].T, w1T=a["L0_attn_vg_w1"].T, w2T=a["L0_attn_vg_w2"].T,
               eta=col(a["L0_attn_eta_w"]), alpha=col(a["L0_attn_alpha_w"]), gate=col(a["L0_attn_gate_w"]))
    x = "L0_xattn_"
    once_l0 = dict(wqT=a[x + "Wq"].T, wkT=a[x + "Wk"].T, wcqT=a[x + "Wcq"].T, wckT=a[x + "Wck"].T)
    l0x = dict(wv=a[x + "Wv"],
               wcv=a[x + "Wcv"], w1=a[x + "W1"], b1=col(a[x + "b1"]), gamma=col(a[x + "gamma"]),
               beta=col(a[x + "beta"]))
    x = "L0_ffn_"
    l0f = dict(router=a[x + "gate_w"].T,
               gate=np.concatenate([a[x + "dyn_gate_w"].reshape(512, P), a[x + "sh_gate_w"].reshape(256, P)]).T,
               up=np.concatenate([a[x + "dyn_up_w"].reshape(512, P), a[x + "sh_up_w"].reshape(256, P)]).T,
               down=tiles(np.concatenate([a[x + "dyn_down_w"].transpose(0, 2, 1).reshape(512, P),
                                          a[x + "sh_down_w"].transpose(0, 2, 1).reshape(256, P)])))
    x = "L1_attn_"
    fir = []
    for fi, kg in FIR_GROUPS:
        taps = a[x + f"fir_w{FIRS[fi]}"].reshape(P, FIRS[fi])[:, ::-1]
        taps = np.concatenate([taps, np.zeros((P, 4 * ((FIRS[fi] + 3) // 4) - FIRS[fi]), f)], 1)
        for c in range(4):
            fir.append(taps[32 * c:32 * c + 32, 4 * kg:4 * kg + 4].T.reshape(P, 1))
    once_l1 = dict(wq=a[x + "Wq"], wk=a[x + "Wk"], wv=a[x + "Wv"], fir=np.concatenate(fir, 1),
                   eye32=np.tile(np.eye(32, dtype=f), (4, 1)), x_wv=a["L1_xattn_Wv"], x_woT=a["L1_xattn_Wo"].T)
    l1a = dict(
               wb_id=np.concatenate([a[x + "Wb"], a[x + "id_gate_W"]], 1), rw1=tiles(a[x + "router_W1"]),
               rb1=col(a[x + "router_b1"], 2), rw2=tiles(a[x + "router_W2"]),
               onw=np.tile(a[x + "o_norm_w"], NH).reshape(P, 1), wo=a[x + "Wo"])
    x = "L1_xattn_"
    l1x = dict(wqT=a[x + "Wq"].T, wkT=a[x + "Wk"].T, bq=col(a[x + "bq"]),
               bk=col(a[x + "bk"]), bv=col(a[x + "bv"]))
    x = "L1_ffn_"
    once_l1.update(me_eqT=a[x + "me_eq_w"].T, me_wvT=a[x + "me_wv"].T, me_woT=a[x + "me_wo"].T,
                   c1w=a[x + "me_c1w"], synT=a[x + "ce_syn_w"].T, ce_wvT=a[x + "ce_wv"].T, ce_wo=a[x + "ce_wo"])
    eb = np.zeros((P, P), f)
    for e, n in ((1, "me_c2b"), (2, "ce_gen_b"), (3, "ml_b2")):
        eb[e] = a[x + n]
    l1f = dict(router=a[x + "router_w"], sw1=a[x + "sw_w1"], sw3=a[x + "sw_w3"], sw2=tiles(a[x + "sw_w2"]),
               c2w=tiles(a[x + "me_c2w"]), me_eq_b=col(a[x + "me_eq_b"]), me_bv=col(a[x + "me_bv"]),
               me_bo=col(a[x + "me_bo"]), c1b=col(a[x + "me_c1b"], 2), 
               ce_syn_b=col(a[x + "ce_syn_b"]),
               ce_bv=col(a[x + "ce_bv"]), n1g=col(a[x + "ce_n1g"]), n1b=col(a[x + "ce_n1b"]),
               f1w=a[x + "ce_f1w"], f1b=col(a[x + "ce_f1b"], 2), f2w=tiles(a[x + "ce_f2w"]),
               f2b=col(a[x + "ce_f2b"]), n2g=col(a[x + "ce_n2g"]), n2b=col(a[x + "ce_n2b"]),
               gen=a[x + "ce_gen_w"], ml1=a[x + "ml_w1"], mlb1=col(a[x + "ml_b1"], 4), ml2=tiles(a[x + "ml_w2"]),
               ebias=eb)
    arrays, cols = {}, {}
    for name, d in dict(const=const, rows=rows, l0a=l0a, l0x=l0x, l0f=l0f, l1a=l1a, l1x=l1x, l1f=l1f,
                       once_rows=once_rows, once_l0=once_l0, once_l1=once_l1).items():
        at, cols[name] = 0, {}
        for k, v in d.items():
            cols[name][k] = (at, v.shape[1])
            at += v.shape[1]
        arrays[name] = np.ascontiguousarray(np.concatenate(list(d.values()), 1))
    arrays["x"] = np.ascontiguousarray(a["x"])
    arrays["xF"] = np.ascontiguousarray(a["x"].transpose(2, 0, 1).reshape(P, NB * P))
    arrays["cF"] = np.ascontiguousarray(a["ctx_1024"].transpose(2, 0, 1).reshape(P, NB * P))
    return arrays, cols


def declare(nc, arrays, cols, stop_after=99):
    dram = {k: nc.dram_tensor("in_" + k, v.shape, F32, kind="ExternalInput").ap() for k, v in arrays.items()}
    for k in ("kk", "xt"):
        dram[k] = nc.dram_tensor("scratch_" + k, (NG // 2, P, CH * CH), F32, kind="Internal").ap()
    out = nc.dram_tensor("out_0", (NB, P, P), F32, kind="ExternalOutput").ap()
    build(nc, dram, cols, out, stop_after)


def kernel(**inputs):
    import concourse.bacc as _bacc
    from concourse.bass_utils import run_bass_kernel_spmd as _run

    nc = _bacc.Bacc("TRN2", target_bir_lowering=False, num_devices=1)
    arrays, cols = _pack(inputs)
    declare(nc, arrays, cols)
    r = _run(nc, [{"in_" + k: v for k, v in arrays.items()}], core_ids=[0])
    return r.results[0]["out_0"]
```

```python
from contextlib import ExitStack

import numpy as np

import concourse.bass as bass
from concourse import mybir

F32 = mybir.dt.float32
BF16 = mybir.dt.bfloat16
U32 = mybir.dt.uint32
ALU = mybir.AluOpType
ACT = mybir.ActivationFunctionType
AX = mybir.AxisListType.X

P = 128
NB = 32
GB = 4
NG = NB // GB
GT = GB * P
NSTREAM = 4
NSET = 2
NVS = 1
NBUF, RESERVE = 35, 8
NORM_ACT = 0
AHEAD = 1000
LN_COLS, ST_COLS = 44, 800
HALF = 64
NE, TOPK = 8, 4
CAP = 640
NHT = 6
NH, DH = 4, 32
CH = 32
NP = NH * GB
FIRS = (3, 7, 15, 31)
FIR_GROUPS = [(f, kg) for f, k in enumerate(FIRS) for kg in range((k + 3) // 4)]
BIG = 1.0e30


class Mark:

    def __init__(self, lane, step, start, end):
        self.lane, self.step, self.start, self.end, self.used, self.value = lane, step, start, end, False, None


class Place:

    def __init__(self, kind, ap, free=()):
        self.kind, self.ap, self.free = kind, ap, list(free)


def flat_marks(after):
    if isinstance(after, Mark):
        yield after
    elif after is not None:
        for a in after:
            yield from flat_marks(a)


class Lane:

    def __init__(self, sem, name):
        self.sem, self.name, self.count = sem, name, 0


class Strand:

    def __init__(self, queues, name, group=-1):
        self.queues, self.name, self.group, self.now, self.last = queues, name, group, 0.0, {}
        self.last_mark = {}

    def put(self, engine, cost, fn, after=(), channel=None):
        marks = list(flat_marks(after))
        for m in marks:
            m.used = True
        ready = max([m.end for m in marks] + [self.last.get(engine, 0.0)])
        start = self.queues.room(engine, ready, cost)
        before = self.last_mark.get(engine)
        self.last[engine] = start + 0.001
        end = start + cost + Queues.LATENCY[engine] + (2500 if channel else 0)
        mark = Mark(channel or self.queues.engines[engine], 16 if channel else 1, start, end)
        mark.used, mark.cost, mark.before = bool(channel), cost, before
        mark.serial = self.queues.serial = self.queues.serial + 1
        self.last_mark[engine] = mark
        self.queues.orders[engine].append((start, len(self.queues.orders[engine]), fn, marks, mark))
        self.now = max(self.now, start + cost)
        return mark

    def take(self, kind="buf"):
        yield
        pool, held = self.queues.pools[kind], self.queues.held
        while True:
            oldest = self.queues.oldest()
            spare = 0 if self.group == oldest else self.queues.reserve[kind] - held.get((oldest, kind), 0)
            if len(pool) > max(spare, 0) and (kind != "set" or self.group == self.queues.sets_out):
                break
            yield WAITS
        place = min(pool, key=lambda p: max([m.end for m in p.free] + [0.0]))
        pool.remove(place)
        held[(self.group, kind)] = held.get((self.group, kind), 0) + 1
        self.queues.sets_out += kind == "set"
        return place

    def bank(self):
        return self.take("bank")

    def give(self, place, *readers):
        place.free = list(flat_marks(readers))
        self.queues.pools[place.kind].append(place)
        self.queues.held[(self.group, place.kind)] -= 1

    give_bank = give

    def beside(self, name, body):
        strand = Strand(self.queues, name, self.group)
        strand.now = self.now
        self.queues.running.append((strand, body(strand)))

    def until(self, condition):
        while not condition():
            yield WAITS

    def mm(self, out, lhsT, rhs, start=True, stop=True, after=()):
        n = 1
        for d in out.shape[1:]:
            n *= d
        m = out.shape[0]
        cost = max(n, 128 if m > 32 else 64) * 4 / 2.15 / (4 if m <= 32 else 1)
        return self.put("tensor", cost, lambda e: e.matmul(out, lhsT, rhs, start=start, stop=stop), after)

    def tr(self, out, in_, ident, after=()):
        return self.put("tensor", 110, lambda e: e.transpose(out, in_, ident), after)

    def act(self, out, in_, func, bias=None, scale=1.0, accum=None, after=()):
        n = 1
        for d in out.shape[1:]:
            n *= d
        kw = {}
        if bias is not None:
            kw["bias"] = bias
        if accum is not None:
            kw["accum_out"] = accum
        cost = 75 + n / 1.28 + (0 if isinstance(scale, float) else 90) + (90 if bias is not None else 0) + (90 if accum is not None else 0)
        return self.put("scalar", cost, lambda e: e.activation(out, in_, func, scale=scale, **kw), after)

    def _vec(self, engine, out, fn, after, rate=1.0, fixed=60):
        n = 1
        for d in out.shape[1:]:
            n *= d
        cost = fixed + n / 0.96 / rate if engine == "vector" else 100 + 2.3 * n
        return self.put(engine, cost, fn, after)

    def tt(self, out, a, b, op, after=(), engine="vector"):
        return self._vec(engine, out, lambda e: e.tensor_tensor(out, a, b, op), after)

    def ts(self, out, a, s1, s2, op0, op1=None, after=(), engine="vector"):
        if op1 is None:
            return self._vec(engine, out, lambda e: e.tensor_scalar(out, a, s1, None, op0), after)
        fixed = 60 if isinstance(s1, float) else 125
        return self._vec(engine, out, lambda e: e.tensor_scalar(out, a, s1, s2, op0, op1), after, fixed=fixed)

    def stt(self, out, a, s, b, op0, op1, after=()):
        return self._vec("vector", out, lambda e: e.scalar_tensor_tensor(
            out=out, in0=a, scalar=s, in1=b, op0=op0, op1=op1), after)

    def copy(self, out, in_, after=(), engine="vector"):
        if engine == "scalar":
            return self.act(out, in_, ACT.Copy, after=after)
        return self._vec(engine, out, lambda e: e.tensor_copy(out, in_), after)

    def red(self, out, in_, op, after=()):
        n = 1
        for d in in_.shape[1:]:
            n *= d
        return self.put("vector", 60 + n / 0.96, lambda e: e.tensor_reduce(out, in_, AX, op), after)

    def recip(self, out, in_, after=()):
        n = 1
        for d in out.shape[1:]:
            n *= d
        return self.put("vector", 60 + 6.4 * n, lambda e: e.reciprocal(out, in_), after)

    def power(self, out, in_, exponent, after=()):
        n = 1
        for d in out.shape[1:]:
            n *= d
        return self.put("gpsimd", 300 + 166 * n, lambda e: e.tensor_tensor(out, in_, exponent, ALU.pow), after)

    def dma(self, channel, out, in_, after=(), engine="sync"):
        n = 4
        for d in out.shape:
            n *= d
        return self.put(engine, max(60, n / 190), lambda e: e.dma_start(out, in_), after, channel=channel)


WAITS, DONE = object(), object()


class Queues:

    LATENCY = {"tensor": 300, "vector": 130, "scalar": 145, "gpsimd": 380, "sync": 0}

    def __init__(self, engines, pools, reserve):
        self.engines, self.pools, self.reserve, self.held, self.sets_out = engines, pools, reserve, {}, 0
        self.orders = {e: [] for e in engines}
        self.busy = {e: [(-1.0, 0.0)] for e in engines}
        self.running, self.serial = [], 0

    def room(self, engine, ready, cost):
        busy = self.busy[engine]
        i = len(busy)
        while busy[i - 1][0] > ready:
            i -= 1
        start = max(ready, busy[i - 1][1])
        while i < len(busy) and busy[i][0] < start + cost:
            start = max(start, busy[i][1])
            i += 1
        if busy[i - 1][1] == start:
            busy[i - 1] = (busy[i - 1][0], start + cost)
        else:
            busy.insert(i, (start, start + cost))
        return start

    def oldest(self):
        return min(s.group for s, _ in self.running)

    def record(self):
        waiting = set()
        while self.running:
            ready = [p for p in self.running if p[0] not in waiting]
            assert ready, "the strands wait for each other"
            pair = min(ready, key=lambda p: (p[0].now + AHEAD * p[0].group, p[0].group))
            said = next(pair[1], DONE)
            if said is WAITS:
                waiting.add(pair[0])
                continue
            waiting.clear()
            if said is DONE:
                self.running.remove(pair)

    def settle(self):
        ops, at = [], {}
        for e, order in self.orders.items():
            for op in order:
                at[id(op[4])] = len(ops)
                ops.append((e, op))
        after, left, tail = [[] for _ in ops], [0] * len(ops), [0.0] * len(ops)
        for i, (e, op) in enumerate(ops):
            deps = {at[id(m)]: m.end - m.start for m in op[3]}
            if op[4].before is not None:
                deps.setdefault(at[id(op[4].before)], 0.0)
            left[i] = len(deps)
            for d, wait in deps.items():
                after[d].append((i, wait))
        for i in sorted(range(len(ops)), key=lambda i: -ops[i][1][4].serial):
            cost = ops[i][1][4].cost
            tail[i] = max([cost] + [tail[j] + max(wait, cost) for j, wait in after[i]])
        free, ready = {e: 0.0 for e in self.orders}, [0.0] * len(ops)
        waiting = {e: [i for i, (f, _) in enumerate(ops) if f == e and not left[i]] for e in self.orders}
        queues = {e: [] for e in self.orders}
        while any(waiting.values()):
            best = None
            for e, w in waiting.items():
                if w:
                    start = max(free[e], min(ready[i] for i in w))
                    if best is None or start < best[0]:
                        best = (start, e)
            start, e = best
            i = max((i for i in waiting[e] if ready[i] <= start), key=lambda i: tail[i])
            waiting[e].remove(i)
            mark = ops[i][1][4]
            length = mark.end - mark.start
            free[e] = start + mark.cost
            mark.start, mark.end = start, start + length
            queues[e].append((start, len(queues[e])) + ops[i][1][2:])
            for j, wait in after[i]:
                left[j] -= 1
                ready[j] = max(ready[j], start + wait)
                if not left[j]:
                    waiting[ops[j][0]].append(j)
        self.orders = queues

    def emit(self, nc):
        for name, order in self.orders.items():
            order.sort(key=lambda op: op[:2])
            last = None
            for i, (start, n, fn, marks, mark) in enumerate(order):
                if name == "gpsimd":
                    mark.used = True
                    if last:
                        order[i] = (start, n, fn, marks + [last], mark)
                    last = mark
                if mark.used:
                    mark.lane.count += mark.step
                    mark.value = mark.lane.count
        with nc.Block() as block:
            enter = {"tensor": block.tensor, "vector": block.vector, "scalar": block.scalar,
                     "gpsimd": block.gpsimd, "sync": block.sync}
            for name, order in self.orders.items():
                def body(e, order=order):
                    seen = {}
                    for _, _, fn, marks, mark in order:
                        need = {}
                        for m in marks:
                            need[m.lane] = max(need.get(m.lane, 0), m.value)
                        for lane, value in need.items():
                            if value > seen.get(lane, 0):
                                e.wait_ge(lane.sem, value)
                                seen[lane] = value
                        ins = fn(e)
                        if mark.used:
                            ins.then_inc(mark.lane.sem, mark.step)
                enter[name](body)


def build(nc, dram, cols, out, stop_after=99):
    with ExitStack() as ctx:
        tensors, channels = {}, {}

        def sb(name, shape, dt=F32):
            if name not in tensors:
                tensors[name] = ctx.enter_context(nc.sbuf_tensor(name, shape, dt))
            return tensors[name]

        def channel(name):
            if name not in channels:
                channels[name] = Lane(ctx.enter_context(nc.semaphore(name)), name)
            return channels[name]

        engines = {e: channel("done_" + e) for e in ("tensor", "vector", "scalar", "gpsimd", "sync")}
        psum = ctx.enter_context(nc.psum_tensor("psum", [P, 8, GT], F32))
        pool = sb("pool", [P, NBUF, GT])
        pairs = sb("pairs", [P, NSET * 2, NP * P])
        vs = sb("vshift", [P, NVS, 4, GB, P])
        memory = {"vshift": [vs[:, i, :, :, :] for i in range(NVS)], "bank": [psum[:, i, :] for i in range(8)], "buf": [pool[:, i, :] for i in range(NBUF)],
                  "set": [(pairs[:, 2 * i, :].rearrange("p (q t) -> p q t", q=NP),
                           pairs[:, 2 * i + 1, :].rearrange("p (q t) -> p q t", q=NP)) for i in range(NSET)]}
        queues = Queues(engines, {k: [Place(k, ap) for ap in v] for k, v in memory.items()},
                        {"bank": 4, "buf": RESERVE, "set": 0, "vshift": 0})
        record(nc, queues, sb, channel, pairs, vs, dram, cols, out, stop_after)
        queues.settle()
        queues.emit(nc)


def record(nc, queues, sb, channel, pairs, vs, dram, cols, out, stop_after):

        setup = Strand(queues, "setup")
        tiles, landed = {}, {}
        once = pairs[:, :, :].rearrange("p a b -> p (a b)")
        once_at = 0
        for part in ("l0a", "const", "rows", "once_l0", "l0x", "l0f", "l1a", "once_rows", "once_l1", "l1x", "l1f"):
            n = sum(w for _, w in cols[part].values())
            if part.startswith("once"):
                tiles[part] = once[:, once_at:once_at + n]
                once_at += n
            else:
                tiles[part] = sb("sb_" + part, [P, n])[:, :]
            src = dram[part][0:1, :].to_broadcast([P, n]) if part.endswith("rows") else dram[part]
            landed[part] = setup.dma(channel("ld_" + part), tiles[part], src)

        def w(part, piece, lo=0, n=None):
            first, width = cols[part][piece]
            n = width - lo if n is None else n
            return tiles[part][:, first + lo:first + lo + n]

        ident, ones = w("const", "ident"), w("const", "ones")
        up = w("const", "upto")
        cmask = w("const", "cmask")
        const, rows = landed["const"], landed["rows"]

        def temp(n):
            nonlocal once_at
            once_at += n
            assert once_at <= NSET * 2 * NP * P
            return once[:, once_at - n:once_at]

        half, inv_half = sb("minus_half", [P, 32]), sb("plus_half", [P, 8])
        m_half = [setup.put("gpsimd", 100, lambda e: e.memset(half[:, :], -0.5)),
                  setup.put("gpsimd", 100, lambda e: e.memset(inv_half[:, :], 0.5))]

        def product(out_sb, n, terms, after, engine="vector"):
            bank = queues.pools["bank"].pop(0)
            for i, (lhsT, rhs) in enumerate(terms):
                m = setup.mm(bank.ap[:, 0:n], lhsT, rhs, i == 0, i == len(terms) - 1,
                             after=[after, bank.free, const])
            c = setup.copy(out_sb, bank.ap[:, 0:n], after=[m], engine=engine)
            bank.free = [c]
            queues.pools["bank"].append(bank)
            return c

        la, ra = landed["l0a"], [landed["l0a"], rows, const]
        gates = sb("gates", [P, 3, P])
        for i, name in enumerate(("eta", "alpha", "gate")):
            m_gates = setup.ts(gates[:, i, :], ones, w("l0a", name), None, ALU.mult, after=ra)
        w1h = sb("w1h", [P, P])
        m_w1h = setup.ts(w1h[:, :], w("l0a", "w1T"), 0.5, None, ALU.mult, after=ra)
        hb = sb("half_gate_biases", [P, 3])
        m_hb = setup.ts(hb[:, :], w("rows", "gate_bias"), 0.5, None, ALU.mult, after=[rows])
        m0sq, m0col, m0all = temp(P), temp(1), sb("m0all", [P, 1])
        m = setup.tt(m0sq, w("l0a", "m0T"), w("l0a", "m0T"), ALU.mult, after=[la])
        m = setup.red(m0col, m0sq, ALU.add, after=[m])
        m_m0 = product(m0all[:, :], 1, [(ones, m0col)], [m])
        lx = landed["l0x"]
        a_self, a_cross = sb("a_self", [P, P]), sb("a_cross", [P, P])
        m_as = product(a_self[:, :], P, [(w("once_l0", "wqT"), w("once_l0", "wkT"))], landed["once_l0"])
        m_ac = product(a_cross[:, :], P, [(w("once_l0", "wcqT"), w("once_l0", "wckT"))], landed["once_l0"])
        lf = landed["l0f"]
        m_gt = setup.ts(w("l0f", "gate"), w("l0f", "gate"), 0.5, None, ALU.mult, after=[lf])
        l0f = [lf, m_gt]
        expert = sb("expert", [P, NHT * P], BF16)[0:27, :]
        m_ex = setup.copy(expert, w("const", "expert")[0:27, :], after=[const])
        l1, o1 = landed["l1a"], [landed["once_l1"], landed["once_rows"]]
        wconv = sb("wconv", [P, 3, 4, P])
        for i, n in enumerate(("q", "k", "v")):
            taps = w("once_rows", n + "_conv").rearrange("p (s c) -> p s c", s=4)
            m_conv = setup.stt(wconv[:, i, :, :], taps, 0.5,
                               w("once_l1", "w" + n).unsqueeze(1).to_broadcast([P, 4, P]),
                               ALU.mult, ALU.mult, after=[o1])
        nfg = len(FIR_GROUPS)
        firw = sb("firw", [P, nfg * 4, CH])
        m_fir = setup.tt(firw[:, :, :], w("once_l1", "fir").unsqueeze(2).to_broadcast([P, nfg * 4, CH]),
                         w("once_l1", "eye32").unsqueeze(1).to_broadcast([P, nfg * 4, CH]), ALU.mult,
                         after=[o1])
        itau = sb("inverse_tau", [P, NH])
        m = setup.act(itau[:, :], w("rows", "log_tau"), ACT.Exp, after=[rows])
        m = setup.ts(itau[:, :], itau[:, :], 0.5, None, ALU.max, after=[m])
        m_tau = setup.recip(itau[:, :], itau[:, :], after=[m])
        l1a = [l1, m_conv, m_fir, m_tau]
        lc = landed["l1x"]
        wvo, bvb, bo_all = sb("wvo", [P, P]), temp(P), sb("bo_all", [P, P])
        m_wvo = product(wvo[:, :], P, [(w("once_l1", "x_wv"), w("once_l1", "x_woT"))], o1)
        m = setup.ts(bvb, ones, w("l1x", "bv"), None, ALU.mult, after=[lc, const])
        m = product(bo_all[:, :], P, [(bvb, w("once_l1", "x_woT"))], [m, o1])
        m_bo = setup.tt(bo_all[:, :], bo_all[:, :], w("rows", "bo"), ALU.add, after=[m, rows])
        l1x = [lc, m_wvo, m_bo]
        l2 = landed["l1f"]
        m_sw = setup.ts(w("l1f", "sw1"), w("l1f", "sw1"), 0.5, None, ALU.mult, after=[l2])
        r1, r2, wme = temp(256), temp(256), sb("wme", [P, 256])
        m1 = product(r1, 256, [(w("once_l1", "me_woT"), w("once_l1", "c1w"))], o1)
        m2 = product(r2, 256, [(w("once_l1", "me_wvT"), r1)], m1)
        m3 = product(wme[:, :], 256, [(w("once_l1", "me_eqT"), r2)], m2)
        bme = sb("bme", [P, 2])
        for k in range(2):
            m = product(bme[:, k:k + 1], 1, [(r2[:, k * P:k * P + P], w("l1f", "me_eq_b")),
                                             (r1[:, k * P:k * P + P], w("l1f", "me_bv")),
                                             (w("once_l1", "c1w", k * P, P), w("l1f", "me_bo"))], [m2, l2])
        m_bme = setup.tt(bme[:, :], bme[:, :], w("l1f", "c1b"), ALU.add, after=[m])
        rce, synb, bvc = (temp(P) for _ in range(3))
        wce, bce = sb("wce", [P, P]), sb("bce", [P, P])
        m = product(rce, P, [(w("once_l1", "ce_wvT"), w("once_l1", "ce_wo"))], o1)
        m = setup.tt(rce, rce, ident, ALU.add, after=[m, const])
        m_wce = product(wce[:, :], P, [(w("once_l1", "synT"), rce)], m)
        s1 = setup.ts(synb, ones, w("l1f", "ce_syn_b"), None, ALU.mult, after=[l2, const])
        s2 = setup.ts(bvc, ones, w("l1f", "ce_bv"), None, ALU.mult, after=[l2, const])
        m = product(bce[:, :], P, [(synb, rce), (bvc, w("once_l1", "ce_wo"))], [m, s1, s2])
        m_bce = setup.tt(bce[:, :], bce[:, :], w("rows", "ce_bo"), ALU.add, after=[m, rows])
        nfb = sb("n1b_plus_f2b", [P, 1])
        m_nfb = setup.tt(nfb[:, :], w("l1f", "n1b"), w("l1f", "f2b"), ALU.add, after=[l2])
        rbias = sb("router_bias", [P, 4])
        m_rb = setup.tt(rbias[:, :], w("rows", "router_b"), w("rows", "load_balancer"), ALU.add, after=[rows])
        l1f = [l2, m_sw, m3, m_bme, m_wce, m_bce, m_nfb, m_rb]
        m_once = [m_m0, m_as, m_ac, m_conv, m_fir, m_wvo, m_bo, m3, m_bme, m_wce, m_bce]

        m_vs = [setup.put("gpsimd", 500, lambda e, i=i: e.memset(vs[:, i, :, :, 0:3], 0.0))
                for i in range(NVS)]
        for place in queues.pools["set"]:
            place.free = m_once
        for place in queues.pools["vshift"]:
            place.free = m_vs
        own = [{"small": sb(f"small{s}", [P, 2 * LN_COLS + ST_COLS]), "free": {},
                "idx": sb(f"idx{s}", [P, GB, 8], U32), "top": sb(f"top{s}", [P, GB, 9], BF16)[:, :, :],
                "ch": {n: channel(f"{n}{s}") for n in
                       ("xF", "xT", "cF", "ag", "a_in", "x_out", "xt", "out", "c2", "shift")}}
               for s in range(NSTREAM)]

        kk_dram, xt_dram = dram["kk"], dram["xt"]
        sol_a = [sb(f"sol_a{i}", [P, CH, CH]) for i in range(2)]
        sol_x = [sb(f"sol_x{i}", [P, CH // 2, CH]) for i in range(2)]
        sol_t = [sb(f"sol_t{i}", [P, 160]) for i in range(2)]
        sol_read = [[], []]
        carry = sb("taken_before", [P, NG * GB + 1, NE])
        m_carry = [setup.put("gpsimd", 100, lambda e: e.memset(carry[:, 0, :], 0.0))]

        def b4(ap):
            return ap.rearrange("p (b t) -> p b t", b=GB)

        def rep(ap, n):
            return ap.unsqueeze(2).to_broadcast([P, ap.shape[1], n])

        def rep_b(ap):
            return ap.unsqueeze(1).to_broadcast([P, GB, ap.shape[1]])

        class Small:

            def __init__(self, o, side, base, size):
                self.t, self.at, self.end, self.o, self.side = o["small"], base, base + size, o, side
                self.free = o["free"].get(side, [])

            def __call__(self, *shape):
                n = 1
                for d in shape:
                    n *= d
                ap = self.t[:, self.at:self.at + n]
                self.at += n
                assert self.at <= self.end
                if len(shape) == 2:
                    ap = ap.rearrange("p (a b) -> p a b", b=shape[1])
                if len(shape) == 3:
                    ap = ap.rearrange("p (a b c) -> p a b c", b=shape[1], c=shape[2])
                return ap

            def done(self, *marks):
                self.o["free"][self.side] = list(marks)

        def small(o, which):
            return Small(o, which, *{"ln": (0, LN_COLS), "ln2": (LN_COLS, LN_COLS), "st": (2 * LN_COLS, ST_COLS)}[which])

        def norm(S, o, y, ready, eps, bank=False):
            sm = small(o, "ln2" if S.name == "block" else "ln")
            st, mv, r = sm(GB, 6), sm(GB, 2), sm(GB)
            yb, out_b = b4(y), (yield from S.take())
            for b in range(GB):
                m = S.put("vector", 200, lambda e, b=b: e.bn_stats(st[:, b, :], yb[:, b, :]),
                          [ready, sm.free])
            for b in range(GB):
                m2_ = S.put("vector", 80, lambda e, b=b: e.bn_aggr(mv[:, b, :], st[:, b, :]), [m, sm.free])
            m = S.ts(r, mv[:, :, 1], eps, None, ALU.add, after=[m2_, sm.free])
            m = S.power(r, r, half[:, 0:GB], after=[m, m_half])
            shift, nv = sm(GB), GB if bank else GB - NORM_ACT
            if nv < GB:
                m4_ = S.stt(shift[:, nv:], mv[:, nv:, 0], -1.0, r[:, nv:], ALU.mult, ALU.mult, after=[m, sm.free])
            for b in range(nv):
                m3_ = S.ts(b4(out_b.ap)[:, b, :], yb[:, b, :], mv[:, b, 0:1], r[:, b:b + 1], ALU.subtract,
                           ALU.mult, after=[m, out_b.free])
            for b in range(nv, GB):
                m4_ = S.act(b4(out_b.ap)[:, b, :], yb[:, b, :], ACT.Identity, bias=shift[:, b:b + 1],
                            scale=r[:, b:b + 1], after=[m, m4_, out_b.free])
            done = [m3_, m4_] if nv < GB else [m3_]
            sm.done(done)
            return out_b, done

        def to_feature(S, src, ready, engine="scalar", scale=None, bias=None, after=()):
            bank, out_b = (yield from S.bank()), (yield from S.take())
            for b in range(GB):
                m = S.tr(bank.ap[:, b * P:b * P + P], src[:, b * P:b * P + P], ident,
                         after=[ready, bank.free, const])
            if scale is None:
                m = S.copy(out_b.ap, bank.ap, after=[m, out_b.free], engine=engine)
            else:
                m = S.act(out_b.ap, bank.ap, ACT.Identity, bias=bias, scale=scale, after=[m, out_b.free, after])
            S.give_bank(bank, m)
            return out_b, m

        def proj(S, weight, src, ready, after, n=GT, engine="scalar", bias=None, func=None, scale=1.0):
            bank, out_b = (yield from S.bank()), (yield from S.take())
            m = S.mm(bank.ap[:, 0:n], weight, src, after=[ready, after, bank.free])
            if bias is None and func is None:
                m = S.copy(out_b.ap[:, 0:n], bank.ap[:, 0:n], after=[m, out_b.free], engine=engine)
            else:
                m = S.act(out_b.ap[:, 0:n], bank.ap[:, 0:n], func or ACT.Identity, bias=bias, scale=scale,
                          after=[m, out_b.free])
            S.give_bank(bank, m)
            return out_b, m

        def token_product(S, bank, terms, after):
            for b in range(GB):
                for i, (src, weight) in enumerate(terms):
                    m = S.mm(bank.ap[:, b * P:b * P + P], src[:, b * P:b * P + P], weight,
                             i == 0, i == len(terms) - 1, after=[after, bank.free])
            return m

        def attention(S, o, qF, kF, ready, causal):
            sm = small(o, "st")
            mx, sums = sm(GB), sm(GB)
            scale = float(P) ** -0.5
            bank = yield from S.bank()
            for b in range(GB):
                m = S.mm(bank.ap[:, b * P:b * P + P], qF[:, b * P:b * P + P], kF[:, b * P:b * P + P],
                         after=[ready, bank.free])
            pr = yield from S.take()
            src = bank.ap
            if causal:
                m = S.tt(b4(pr.ap), b4(bank.ap), rep_b(cmask), ALU.add, after=[m, pr.free, const])
                S.give_bank(bank, m)
                src = pr.ap
            m = S.red(mx, b4(src), ALU.max, after=[m, sm.free])
            m = S.ts(mx, mx, -scale, None, ALU.mult, after=[m])
            for b in range(GB):
                m2_ = S.act(pr.ap[:, b * P:b * P + P], src[:, b * P:b * P + P], ACT.Exp, bias=mx[:, b:b + 1],
                            scale=scale, accum=sums[:, b:b + 1], after=[m, pr.free, sm.free])
            if not causal:
                S.give_bank(bank, m2_)
            m = S.recip(sums, sums, after=[m2_])
            m = S.tt(b4(pr.ap), b4(pr.ap), rep(sums, P), ALU.mult, after=[m])
            sm.done(m)
            prT, m = yield from to_feature(S, pr.ap, m)
            S.give(pr, m)
            return prT, m

        def l0_attention(S, o, g):
            sm = small(o, "st")
            fr = sm.free
            xF, xT = (yield from S.take()), (yield from S.take())
            m_xF = S.dma(o["ch"]["xF"], xF.ap, dram["xF"][:, g * GT:g * GT + GT], after=[xF.free])
            m_xT = S.dma(o["ch"]["xT"], b4(xT.ap), dram["x"][g * GB:g * GB + GB].rearrange("b t f -> t b f"),
                         after=[xT.free])
            xFb, xTb = b4(xF.ap), b4(xT.ap)
            yF, m_y = yield from proj(S, w("l0a", "m0T"), xF.ap, m_xF, la)
            yFb = b4(yF.ap)
            sF, t = (yield from S.take()), (yield from S.take())
            sFb, tb = b4(sF.ap), b4(t.ap)

            def silu_half(c, ready):
                bank = yield from S.bank()
                u = bank.ap[:, 0:GB * HALF].rearrange("p (b t) -> p b t", b=GB)
                m = S.mm(u, w1h[:, :], yFb[:, :, c * HALF:c * HALF + HALF], after=[ready, bank.free, m_w1h])
                m = S.act(tb[:, :, 0:HALF], u, ACT.Tanh, after=[m, t.free])
                m = S.stt(sFb[:, :, c * HALF:c * HALF + HALF], tb[:, :, 0:HALF], 1.0, u, ALU.add, ALU.mult,
                          after=[m, sF.free])
                S.give_bank(bank, m)
                return m

            m_s0 = yield from silu_half(0, m_y)
            sbar, xbar, sq = sm(GB), sm(GB), sm(GB)
            m_sb = S.red(sbar, sFb[:, :, 0:HALF], ALU.add, after=[m_s0, fr])
            m_sb = S.ts(sbar, sbar, 1.0 / HALF, None, ALU.mult, after=[m_sb])
            m_xb = S.red(xbar, xFb[:, :, 0:HALF], ALU.add, after=[m_xF, fr])
            x2 = yield from S.take()
            m = S.act(x2.ap[0:HALF, :], xT.ap[0:HALF, :], ACT.Square, after=[m_xT, x2.free])
            m = S.red(sq[0:HALF, :], b4(x2.ap)[0:HALF], ALU.add, after=[m, fr])
            S.give(x2, m)
            m = S.power(sq[0:HALF, :], sq[0:HALF, :], inv_half[0:HALF, 0:GB], after=[m, m_half])
            m = S.ts(sq[0:HALF, :], sq[0:HALF, :], 1e-5, float(HALF), ALU.max, ALU.mult, after=[m])
            m = S.recip(sq[0:HALF, :], sq[0:HALF, :], after=[m])
            bank = yield from S.bank()
            for b in range(GB):
                mk = S.mm(bank.ap[:, b:b + 1], xTb[0:HALF, b, :], sq[0:HALF, b:b + 1], after=[m, bank.free])
            km, dk, vec = sm(GB), sm(GB), sm(3, GB)
            m_km = S.copy(km, bank.ap[:, 0:GB], after=[mk, fr])
            S.give_bank(bank, m_km)
            m_dk = S.stt(dk, xbar, 1.0 / HALF, km, ALU.mult, ALU.subtract, after=[m_km, m_xb, fr])
            bank = yield from S.bank()
            S.mm(bank.ap[:, 0:GB], w("l0a", "w2T"), sbar, True, False, after=[m_sb, bank.free])
            S.mm(bank.ap[:, 0:GB], w("l0a", "m0T"), dk, False, True, after=[m_dk])
            S.mm(bank.ap[:, 8:8 + GB], w("l0a", "m0T"), km)
            m = S.mm(bank.ap[:, 16:16 + GB], gates[:, 2, :], km, after=[m_gates])
            err, mkv, gate = sm(GB), sm(GB), sm(GB)
            m_e = S.copy(err, bank.ap[:, 0:GB], after=[m, fr])
            m_mk = S.copy(mkv, bank.ap[:, 8:8 + GB], after=[m, fr])
            m_g = S.act(gate, bank.ap[:, 16:16 + GB], ACT.Tanh, scale=0.5, bias=hb[:, 2:3], after=[m_mk, fr, m_hb])
            S.give_bank(bank, m_mk, m_g)
            m_g = S.ts(gate, gate, 0.5, 0.5, ALU.mult, ALU.add, after=[m_g])
            bank = yield from S.bank()
            n2 = GB * HALF
            for i in range(2):
                m = S.mm(bank.ap[:, i * n2:i * n2 + n2].rearrange("p (b t) -> p b t", b=GB),
                         gates[:, i, :], xFb[:, :, 0:HALF], after=[m_xF, m_gates, bank.free])
            for i in range(2):
                mt = S.act(t.ap[:, i * n2:i * n2 + n2], bank.ap[:, i * n2:i * n2 + n2], ACT.Tanh, scale=0.5,
                           bias=hb[:, i:i + 1], after=[m, m_s0, m_hb])
            S.give_bank(bank, mt)
            ea = sm(2 * GB)
            m = S.red(ea, t.ap.rearrange("p (k t) -> p k t", t=HALF), ALU.add, after=[mt, fr])
            m_eta = S.ts(ea[:, 0:GB], ea[:, 0:GB], 0.1 / HALF, 0.1, ALU.mult, ALU.add, after=[m])
            m_al = S.ts(ea[:, GB:], ea[:, GB:], 0.25 / HALF, -0.25, ALU.mult, ALU.add, after=[m])
            S.tt(vec[:, 0, :], err, mkv, ALU.mult, after=[m_e, m_mk, fr])
            S.tt(vec[:, 1, :], err, err, ALU.mult, after=[m_e, fr])
            m = S.tt(vec[:, 2, :], km, km, ALU.mult, after=[m_km, fr])
            bank = yield from S.bank()
            md = S.mm(bank.ap[:, 0:3 * GB], ones, vec.rearrange("p a b -> p (a b)"), after=[m, bank.free, const])
            dots = sm(3, GB)
            m_d = S.copy(dots.rearrange("p a b -> p (a b)"), bank.ap[:, 0:3 * GB], after=[md, fr])
            S.give_bank(bank, m_d)
            c1, c2, n_, q_ = sm(GB), sm(GB), sm(GB), sm(GB)
            m = S.tt(c1, ea[:, GB:], gate, ALU.mult, after=[m_al, m_g, fr])
            m1_ = S.ts(c1, c1, 1.0, None, ALU.add, after=[m])
            m2_ = S.tt(c2, gate, ea[:, 0:GB], ALU.mult, after=[m_eta, m_g, fr])
            m = S.tt(n_, c1, c1, ALU.mult, after=[m1_, fr])
            m = S.ts(n_, n_, m0all[:, 0:1], None, ALU.mult, after=[m, m_m0])
            m3_ = S.tt(q_, c1, c2, ALU.mult, after=[m1_, m2_, fr])
            m3_ = S.stt(q_, q_, 2.0, dots[:, 0, :], ALU.mult, ALU.mult, after=[m3_, m_d])
            m = S.tt(n_, n_, q_, ALU.add, after=[m, m3_])
            m3_ = S.tt(q_, c2, c2, ALU.mult, after=[m])
            m3_ = S.tt(q_, q_, dots[:, 1, :], ALU.mult, after=[m3_])
            m3_ = S.tt(q_, q_, dots[:, 2, :], ALU.mult, after=[m3_])
            m = S.tt(n_, n_, q_, ALU.add, after=[m3_])
            m = S.ts(n_, n_, 0.0, None, ALU.max, after=[m])
            m = S.power(n_, n_, inv_half[:, 0:GB], after=[m, m_half])
            m = S.ts(n_, n_, 1e-6, None, ALU.add, after=[m])
            m = S.recip(n_, n_, after=[m])
            m = S.ts(n_, n_, 30.0, 1.0, ALU.mult, ALU.min, after=[m])
            m1_ = S.tt(c1, c1, n_, ALU.mult, after=[m])
            m2_ = S.tt(c2, c2, n_, ALU.mult, after=[m])
            m2_ = S.tt(c2, c2, err, ALU.mult, after=[m2_])
            kB = yield from S.take()
            m = S.copy(b4(kB.ap), rep(km, P), after=[m_km, kB.free])
            bank = yield from S.bank()
            u = bank.ap[:, 0:n2].rearrange("p (b t) -> p b t", b=GB)
            for b in range(GB):
                mk = S.mm(u[:, b, :], b4(kB.ap)[:, b, :], xFb[:, b, HALF:], after=[m, bank.free])
            S.give(kB, mk)
            m = S.tt(tb[:, :, 0:HALF], u, rep(c2, HALF), ALU.mult, after=[mk, m2_, ea and m_al])
            S.give_bank(bank, m)
            mm_ = S.tt(yFb[:, :, HALF:], yFb[:, :, HALF:], rep(c1, HALF), ALU.mult, after=[m1_, m_y])
            m_y2 = S.tt(yFb[:, :, HALF:], yFb[:, :, HALF:], tb[:, :, 0:HALF], ALU.add, after=[mm_, m])
            sm.done(m_y2, mk, m_e, m_mk)
            m_s1 = yield from silu_half(1, [m_y2])
            S.give(xF, mk)
            bank = yield from S.bank()
            m = token_product(S, bank, [(sF.ap, w("l0a", "w2T")), (yF.ap, ident)], [m_s1, m_y2, const])
            S.give(sF, m)
            S.give(yF, m)
            S.give(t, m_s1)
            m = S.tt(xT.ap, bank.ap, xT.ap, ALU.add, after=[m, m_xT])
            S.give_bank(bank, m)
            x1, m1_ = yield from norm(S, o, xT.ap, m, 1e-5)
            S.give(xT, m1_)
            return x1, m1_

        def l0_cross(S, o, g, x1, ready):
            gam, bet = w("l0x", "gamma"), w("l0x", "beta")
            xF, m_x = yield from to_feature(S, x1.ap, ready)
            cF = yield from S.take()
            m_c = S.dma(o["ch"]["cF"], cF.ap, dram["cF"][:, g * GT:g * GT + GT], after=[cF.free])

            def block(src, m_src, keys, m_keys, a, m_a, wv, causal):
                q, m_q = yield from proj(S, a, src, m_src, m_a)
                v = yield from S.take()
                bank = yield from S.bank()
                m = token_product(S, bank, [(keys, w("l0x", wv))], [m_keys, lx])
                m_v = S.copy(v.ap, bank.ap, after=[m, v.free], engine="scalar")
                S.give_bank(bank, m_v)
                pT, m_p = yield from attention(S, o, q.ap, keys, [m_q, m_keys], causal)
                bank = yield from S.bank()
                for b in range(GB):
                    c = slice(b * P, b * P + P)
                    S.mm(bank.ap[:, c], pT.ap[:, c], v.ap[:, c], True, False, after=[m_p, m_v, bank.free])
                    m = S.mm(bank.ap[:, c], src[:, c], ident, False, True, after=[m_src])
                S.give(q, m)
                S.give(v, m)
                S.give(pT, m)
                hx, m = yield from norm(S, o, bank.ap, m, 1e-3, bank=True)
                S.give_bank(bank, m)
                hF, m2_ = yield from to_feature(S, hx.ap, m, scale=gam, bias=bet, after=[lx])
                S.give(hx, m2_)
                return hF, m2_

            hF, m_h = yield from block(xF.ap, m_x, xF.ap, m_x, a_self[:, :], m_as, "wv", True)
            S.give(xF, m_h)
            h2F, m_h2 = yield from block(hF.ap, m_h, cF.ap, m_c, a_cross[:, :], m_ac, "wcv", False)
            S.give(hF, m_h2)
            S.give(cF, m_h2)
            f, m = yield from proj(S, w("l0x", "w1"), h2F.ap, m_h2, lx, bias=w("l0x", "b1"), func=ACT.Relu)
            m = S.tt(f.ap, f.ap, h2F.ap, ALU.add, after=[m])
            S.give(h2F, m)
            bank = yield from S.bank()
            for b in range(GB):
                c = slice(b * P, b * P + P)
                m2_ = S.tr(bank.ap[:, c], f.ap[:, c], ident, after=[m, bank.free])
            S.give(f, m2_)
            y, m = yield from norm(S, o, bank.ap, m2_, 1e-3, bank=True)
            S.give_bank(bank, m)
            m = S.tt(b4(y.ap), b4(y.ap), rep_b(w("rows", "gamma")), ALU.mult, after=[m, rows])
            m = S.tt(b4(y.ap), b4(y.ap), rep_b(w("rows", "beta")), ALU.add, after=[m])
            m = S.stt(y.ap, y.ap, 0.0, x1.ap, ALU.max, ALU.add, after=[m, ready])
            S.give(x1, m)
            x2, m = yield from norm(S, o, y.ap, m, 1e-5)
            S.give(y, m)
            return x2, m

        def l0_ffn(S, o, g, x2, ready):
            sm = small(o, "st")
            fr = sm.free
            xF, m_x = yield from to_feature(S, x2.ap, ready)
            hidden = []

            def hidden_units(F):
                for k in range(NHT):
                    h, t, bg, bu = (yield from F.take()), (yield from F.take()), (yield from F.bank()), (yield from F.bank())
                    m1_ = F.mm(bg.ap, w("l0f", "gate", k * P, P), xF.ap, after=[m_x, l0f, bg.free])
                    m2_ = F.mm(bu.ap, w("l0f", "up", k * P, P), xF.ap, after=[m_x, bu.free])
                    m = F.act(t.ap, bg.ap, ACT.Tanh, after=[m1_, t.free])
                    m = F.stt(h.ap, t.ap, 1.0, bg.ap, ALU.add, ALU.mult, after=[m, h.free])
                    F.give(t, m)
                    F.give_bank(bg, m)
                    m = F.tt(h.ap, h.ap, bu.ap, ALU.mult, after=[m, m2_])
                    F.give_bank(bu, m)
                    hidden.append((h, m, m2_))

            S.beside("hidden", hidden_units)
            bank = yield from S.bank()
            lgp = bank.ap[:, 0:GB * 9].rearrange("p (b e) -> p b e", b=GB)
            for b in range(GB):
                m = S.mm(lgp[:, b, :], xF.ap[:, b * P:b * P + P], w("l0f", "router"), after=[m_x, lf, bank.free])
            m_lgp = m
            lg = sm(GB, 9)
            m_lg = S.copy(lg, lgp, after=[m, fr])
            S.give_bank(bank, m_lg)
            srt, ab, idf = sm(GB, 8), sm(GB, 8), sm(GB, 8)
            idx = o["idx"]
            for b in range(GB):
                m = S.put("vector", 70, lambda e, b=b: e.max(srt[:, b, :], lg[:, b, 0:8]), [m_lg, fr])
            m_srt = m
            for b in range(GB):
                m = S.put("vector", 77, lambda e, b=b: e.max_index(idx[:, b, :], srt[:, b, :], lg[:, b, 0:8]),
                          [m_srt, fr])
            m_idx = S.copy(idf, idx[:, :, :], after=[m, fr])
            m_ab = S.ts(ab, srt, -1.0, None, ALU.mult, after=[m_srt, fr])
            m_ab = S.tt(ab, ab, srt, ALU.max, after=[m_ab])
            shp = [P, GB, TOPK, 8]

            def over_i(a):
                return a[:, :, 0:TOPK].unsqueeze(3).to_broadcast(shp)

            def over_j(a):
                return a.unsqueeze(2).to_broadcast(shp)

            gap, lim = sm(GB, TOPK, 8), sm(GB, TOPK, 8)

            def flat(a):
                return a.rearrange("p a b c -> p (a b c)")

            m1_ = S.tt(gap, over_i(srt), over_j(srt), ALU.subtract, after=[m_srt, fr])
            m2_ = S.tt(lim, over_i(ab), over_j(ab), ALU.max, after=[m_ab, fr])
            m2_ = S.stt(flat(lim), flat(lim), 0.2, flat(gap), ALU.mult, ALU.is_ge, after=[m1_, m2_])
            m1_ = S.ts(flat(gap), flat(gap), 0.0, None, ALU.max, after=[m2_])
            m_e = S.act(flat(gap), flat(gap), ACT.Exp, scale=-1.0, after=[m1_])
            rank = w("const", "rank_ge").rearrange("p (j i) -> p j i", i=8).unsqueeze(1).to_broadcast(shp)
            m2_ = S.tt(lim, lim, rank, ALU.mult, after=[m2_, const])
            es, cs = sm(GB, 8), sm(GB, 8)
            m_es = S.copy(es, gap[:, :, 0, :], after=[m_e, fr])
            m = S.tt(flat(gap), flat(gap), flat(lim), ALU.mult, after=[m_es, m2_])
            mult = sm(GB, TOPK)
            m_mu = S.red(mult.rearrange("p a b -> p (a b)"), gap.rearrange("p a b c -> p (a b) c"), ALU.add,
                         after=[m, fr])
            m_mu = S.recip(mult, mult, after=[m_mu])
            tot, valid = sm(GB), sm(GB, TOPK)
            m_t = S.red(tot, es, ALU.add, after=[m_es, fr])
            m_t = S.ts(tot, tot, 0.75, None, ALU.mult, after=[m_t])
            m = S.copy(cs[:, :, 0:1], es[:, :, 0:1], after=[m_es, fr])
            for j in range(1, TOPK - 1):
                m = S.tt(cs[:, :, j:j + 1], cs[:, :, j - 1:j], es[:, :, j:j + 1], ALU.add, after=[m])
            m = S.tt(cs[:, :, 0:TOPK - 1], cs[:, :, 0:TOPK - 1], rep(tot, TOPK - 1), ALU.is_lt, after=[m, m_t])
            m = S.tt(mult[:, :, 1:], mult[:, :, 1:], cs[:, :, 0:TOPK - 1], ALU.mult, after=[m, m_mu])
            m_tm = S.red(tot, mult, ALU.add, after=[m])
            m_tm = S.recip(tot, tot, after=[m_tm])
            m1_ = S.tt(gap, idf[:, :, 0:TOPK].unsqueeze(3).to_broadcast(shp),
                       w("const", "iota").unsqueeze(1).unsqueeze(1).to_broadcast(shp), ALU.is_equal,
                       after=[m_idx, m_mu, const])
            m1_ = S.tt(gap, gap, mult.unsqueeze(3).to_broadcast(shp), ALU.mult, after=[m1_, m])
            rw, mask, keep = sm(GB, 8), sm(GB, 9), sm(GB, 8)
            m1_ = S.red(rw, gap.rearrange("p b j e -> p b e j"), ALU.add, after=[m1_, fr])
            m_k = S.ts(mask[:, :, 0:8], rw, 0.0, None, ALU.is_gt, after=[m1_, fr])
            m_rw = S.tt(rw, rw, rep(tot, 8), ALU.mult, after=[m_tm, m_k])
            yield from S.until(lambda: len(m_carry) > g)
            m_cy = m_carry[g]
            for b in range(GB):
                i = g * GB + b
                m_cy = S.tt(carry[:, i + 1, :], carry[:, i, :], mask[:, b, 0:8], ALU.add, after=[m_k, m_cy])
            m_carry.append(m_cy)
            bank = yield from S.bank()
            cnt = bank.ap[:, 0:GB * 8].rearrange("p (b e) -> p b e", b=GB)
            S.mm(cnt, up, mask[:, :, 0:8], True, False, after=[m_k, const, bank.free])
            m = S.mm(cnt, ones, carry[:, g * GB:g * GB + GB, :], False, True, after=[m_cy])
            m = S.ts(keep, cnt, float(CAP), None, ALU.is_le, after=[m, fr])
            S.give_bank(bank, m)
            m = S.tt(mask[:, :, 0:8], mask[:, :, 0:8], keep, ALU.mult, after=[m])
            m_m8 = S.put("vector", 60, lambda e: e.memset(mask[:, :, 8:9], 1.0), [fr])
            mxe = sm(GB)
            gl = sm(GB, 9)
            m2_ = S.ts(gl, mask, -1.0, BIG, ALU.add, ALU.mult, after=[m, m_m8, fr])
            m2_ = S.tt(lg, lg, mask, ALU.mult, after=[m2_, m_idx])
            m2_ = S.tt(gl, gl, lg, ALU.add, after=[m2_])
            m3_ = S.red(mxe, gl, ALU.max, after=[m2_, fr])
            m2_ = S.tt(gl, gl, rep(mxe, 9), ALU.subtract, after=[m3_])
            m2_ = S.act(gl, gl, ACT.Exp, after=[m2_])
            m3_ = S.red(mxe, gl, ALU.add, after=[m2_])
            m3_ = S.recip(mxe, mxe, after=[m3_])
            m2_ = S.tt(gl, gl, rep(mxe, 9), ALU.mult, after=[m3_])
            m3_ = S.red(mxe, gl[:, :, 0:8], ALU.add, after=[m2_])
            m3_ = S.tt(rw, rw, rep(mxe, 8), ALU.mult, after=[m3_, m_rw])
            m_w = S.tt(gl[:, :, 0:8], rw, mask[:, :, 0:8], ALU.mult, after=[m3_])
            thirds, top = sm(GB, 3, 9), o["top"]
            for i in range(3):
                m = S.copy(top, gl, after=[m_w, o["free"].get("top")])
                m = S.copy(thirds[:, :, i, :], top, after=[m, fr])
                if i < 2:
                    m_w = S.tt(gl, gl, thirds[:, :, i, :], ALU.subtract, after=[m, m_w])
                o["free"]["top"] = m
            bank, gw = (yield from S.bank()), (yield from S.take())
            gw16 = gw.ap.bitcast(BF16)
            for b in range(GB):
                m2_ = S.tr(bank.ap[0:27, b * P:b * P + P], thirds[:, b, :, :].rearrange("p i e -> p (i e)"), ident,
                           after=[m, bank.free, const])
            m = m2_
            m_gw = S.copy(gw16[0:27, 0:GT], bank.ap[0:27, :], after=[m, gw.free], engine="scalar")
            gw16 = gw16[:, 0:GT]
            S.give_bank(bank, m_gw)
            sm.done(m, m_gw, m_cy)
            acc = yield from S.bank()
            for k in range(NHT):
                yield from S.until(lambda: len(hidden) > k)
                h, m_h, m_xF_read = hidden[k]
                bw = yield from S.bank()
                m = S.mm(bw.ap, expert[:, k * P:k * P + P], gw16[0:27, :], after=[m_gw, m_ex, bw.free])
                m = S.tt(h.ap, h.ap, bw.ap, ALU.mult, after=[m, m_h])
                S.give_bank(bw, m)
                for b in range(GB):
                    c = slice(b * P, b * P + P)
                    m2_ = S.mm(acc.ap[:, c], h.ap[:, c], w("l0f", "down", k * P, P),
                               k == 0 and b == 0, k == NHT - 1 and b == GB - 1, after=[m, acc.free])
                S.give(h, m2_)
            m = m2_
            S.give(gw, m)
            S.give(xF, m, m_xF_read, m_lgp)
            m = S.tt(x2.ap, acc.ap, x2.ap, ALU.add, after=[m, ready])
            S.give_bank(acc, m)
            x3, m2_ = yield from norm(S, o, x2.ap, m, 1e-5)
            S.give(x2, m2_)
            return x3, m2_

        def solve(S, o, g, fed, XT):
            a, x, t = sol_a[g % 2], sol_x[g % 2], sol_t[g % 2]
            for h in range(2):
                m_in = S.dma(o["ch"]["a_in"], a[64 * h:64 * h + 64].rearrange("p i j -> p (i j)"), kk_dram[g],
                             after=[fed, sol_read[g % 2]])
            m = S.copy(x[:, :, :].rearrange("p m i -> p (m i)"), w("const", "unit_rows"),
                       after=[const, sol_read[g % 2]])
            for j in range(CH - 1):
                nm, ni = j // 2 + 1, CH - 1 - j
                tmp = t[:, 0:nm * ni].rearrange("p (m i) -> p m i", m=nm)
                m = S.tt(tmp, x[:, 0:nm, j:j + 1].to_broadcast([P, nm, ni]),
                         a[:, j + 1:, j].unsqueeze(1).to_broadcast([P, nm, ni]), ALU.mult, after=[m, m_in])
                m = S.tt(x[:, 0:nm, j + 1:], x[:, 0:nm, j + 1:], tmp, ALU.subtract, after=[m])
            for h in range(2):
                dst = xt_dram[g].rearrange("q (m h i) -> h q m i", h=2, i=CH)[h]
                m_out = S.dma(o["ch"]["x_out"], dst, x[64 * h:64 * h + 64], after=[m])
            sol_read[g % 2] = [m_out, m]
            for c in range(4):
                src = xt_dram[g].rearrange("(q c) (m i) -> c m q i", c=4, i=CH)[c]
                dst = XT.ap[CH * c:CH * c + CH].rearrange("m (q i) -> m q i", q=NP)
                m_xt = S.dma(o["ch"]["xt"], dst, src, after=[m_out, XT.free])
            return m_xt

        def l1_attention_front(S, o, g, x3, ready):
            sm = small(o, "st")
            fr = sm.free
            xF, m_x = yield from to_feature(S, x3.ap, ready)
            xFb = b4(xF.ap)

            def project(T, i):
                bank, t, y = (yield from T.bank()), (yield from T.take()), (yield from T.take())
                for s in range(4):
                    m_in = T.mm(b4(bank.ap)[:, :, s:], wconv[:, i, s, :], xFb[:, :, 0:P - s], s == 0, s == 3,
                                after=[m_x, l1a, bank.free])
                m = T.act(t.ap, bank.ap, ACT.Tanh, after=[m_in, t.free])
                m = T.stt(y.ap, t.ap, 1.0, bank.ap, ALU.add, ALU.mult, after=[m, y.free])
                T.give_bank(bank, m)
                T.give(t, m)
                return y, m, m_in

            heads = w("const", "heads")

            def masked(T, src, m_src, h):
                y = yield from T.take()
                return y, T.act(y.ap, src.ap, ACT.Copy, scale=heads[:, h:h + 1], after=[m_src, y.free, const])

            def square_sums(T, src, m_src, more=None):
                x2, bank = (yield from T.take()), (yield from T.bank())
                m2_ = T.act(x2.ap, src.ap, ACT.Square, after=[m_src, x2.free])
                pn = bank.ap[:, 0:GB * 12].rearrange("p (b e) -> p b e", b=GB)
                for b in range(GB):
                    c = slice(b * P, b * P + P)
                    if more is not None:
                        T.mm(pn[:, b, 4:12], xF.ap[:, c], more, after=[m_x, l1, bank.free])
                    m = T.mm(pn[:, b, 0:4], x2.ap[:, c], heads, after=[m2_, bank.free, const])
                T.give(x2, m)
                return bank, pn, m

            val, key = {}, {}

            def values(F):
                v, m_v, m_xF_read = yield from project(F, 2)
                shifted = yield from F.take("vshift")
                vsh = shifted.ap
                for s in range(4):
                    for c in range(4):
                        shifts = F.dma(o["ch"]["shift"], vsh[32 * s:32 * s + 32, c, :, s:],
                                       b4(v.ap)[32 * c:32 * c + 32, :, 0:P - s], after=[m_v, shifted.free])
                bank, vT = (yield from F.bank()), (yield from F.take())
                for b in range(GB):
                    c = slice(b * P, b * P + P)
                    m = F.tr(bank.ap[:, c], v.ap[:, c], ident, after=[m_v, bank.free, const])
                m_vT = F.copy(vT.ap, bank.ap, after=[m, vT.free], engine="scalar")
                F.give_bank(bank, m_vT)
                F.give(v, m, shifts)
                paths = []
                for f in range(4):
                    bank, pf = (yield from F.bank()), (yield from F.take())
                    kgs = [kg for ff, kg in FIR_GROUPS if ff == f]
                    for n_, kg in enumerate(kgs):
                        for c in range(4):
                            col = FIR_GROUPS.index((f, kg)) * 4 + c
                            m_vs = F.mm(b4(bank.ap)[32 * c:32 * c + 32, :, 4 * kg:], firw[:, col, :],
                                        vsh[:, c, :, 0:P - 4 * kg], n_ == 0, n_ == len(kgs) - 1,
                                        after=[shifts, bank.free, l1a])
                    m = F.copy(pf.ap, bank.ap, after=[m_vs, pf.free], engine="scalar")
                    F.give_bank(bank, m)
                    paths.append((pf, m))
                F.give(shifted, m_vs)
                yield from F.until(lambda: "rb" in key)
                rhs = yield from F.take()
                rhs_p = rhs.ap.rearrange("p (h b d) -> p b h d", h=NH, b=GB)
                m_rhs = F.tt(rhs_p, vT.ap.rearrange("p (b h d) -> p b h d", b=GB, h=NH),
                             key["rb"].unsqueeze(3).to_broadcast([P, GB, NH, DH]), ALU.mult,
                             after=[m_vT, key["m_rb"], rhs.free])
                val.update(m_xF_read=m_xF_read, vT=vT, m_vT=m_vT, paths=paths, rhs=rhs, m_rhs=m_rhs)

            def queries(F):
                q, m_q, m_xF_q = yield from project(F, 0)
                bank, pn, m = yield from square_sums(F, q, m_q)
                rq = sm(GB, NH)
                m = F.ts(rq, pn[:, :, 0:4], 1e-6, None, ALU.add, after=[m, fr])
                F.give_bank(bank, m)
                m_rq = F.power(rq, rq, half[:, 0:NP].rearrange("p (b e) -> p b e", b=GB), after=[m, m_half])
                yield from F.until(lambda: "set" in key)
                att = key["set"].ap[1]
                kk, m_k = key["k"]
                for h in range(NH):
                    qx, m_qx = yield from masked(F, q, m_q, h)
                    bank = yield from F.bank()
                    for b in range(GB):
                        c = slice(b * P, b * P + P)
                        m = F.mm(bank.ap[:, c], kk.ap[:, c], qx.ap[:, c], after=[m_qx, m_k, bank.free])
                    F.give(qx, m)
                    m_att = F.tt(att[:, h * GB:h * GB + GB, :], b4(bank.ap), rep_b(up), ALU.mult,
                                 after=[m, key["set"].free])
                    F.give_bank(bank, m_att)
                F.give(q, m_qx)
                key["k_read"] = m
                F.give(kk, m, key["m_kx"])
                val.update(rq=rq, m_rq=m_rq, m_att=m_att, m_xF_q=m_xF_q)

            kk, m_k, _ = yield from project(S, 1)
            key["k"] = kk, m_k
            S.beside("queries", queries)
            S.beside("values", values)
            bank, pn, m = yield from square_sums(S, kk, m_k, w("l1a", "wb_id"))
            ss, r, z = sm(GB, NH), sm(GB, NH), sm(GB, 8)
            m1_ = S.ts(ss, pn[:, :, 0:4], 1e-6, None, ALU.add, after=[m, fr])
            m2_ = S.tt(z[:, :, 4:8], pn[:, :, 8:12], rep_b(w("rows", "id_b")), ALU.add, after=[m, fr, rows])
            m2_ = S.copy(z[:, :, 0:4], pn[:, :, 4:8], after=[m, fr])
            S.give_bank(bank, m2_)
            m_r = S.power(r, ss, half[:, 0:NP].rearrange("p (b e) -> p b e", b=GB), after=[m1_, fr, m_half])
            m1_ = S.recip(ss, ss, after=[m_r])
            m2_ = S.act(z, z, ACT.Tanh, scale=0.5, after=[m2_])
            m2_ = S.ts(z, z, 0.5, 0.5, ALU.mult, ALU.add, after=[m2_])
            gg, ng, rb, padj, cm = (sm(NH, GB), sm(NH, GB), sm(GB, NH), sm(GB, NH), sm(GB, NH))
            m_g = S.tt(gg.rearrange("p h b -> p b h"), z[:, :, 0:4], ss, ALU.mult, after=[m1_, m2_, fr])
            big = yield from S.take("set")
            kkt = big.ap[0]
            key["m_kx"] = None
            for h in range(NH):
                kx, m_kx = yield from masked(S, kk, m_k, h)
                bank = yield from S.bank()
                for b in range(GB):
                    c = slice(b * P, b * P + P)
                    m = S.mm(bank.ap[:, c], kx.ap[:, c], kk.ap[:, c], after=[m_kx, m_k, bank.free])
                S.give(kx, m)
                m_kk = S.copy(kkt[:, h * GB:h * GB + GB, :], b4(bank.ap), after=[m, big.free], engine="scalar")
                S.give_bank(bank, m_kk)
            key.update(set=big, m_kx=m)
            ag = yield from S.take()
            agp = ag.ap.rearrange("p (q j) -> p q j", q=NP)
            for c in range(4):
                r_ = slice(CH * c, CH * c + CH)
                m = S.tt(agp[r_], kkt[r_, :, CH * c:CH * c + CH],
                         gg.rearrange("p h b -> p (h b)")[r_].unsqueeze(2).to_broadcast([CH, NP, CH]), ALU.mult,
                         after=[m_kk, m_g, ag.free], engine="gpsimd" if c % 2 else "vector")
                dst = kk_dram[g].rearrange("(q c) (i j) -> c i q j", c=4, j=CH)[c]
                fed = S.dma(o["ch"]["ag"], dst, agp[r_], after=[m])
            S.give(ag, fed)
            m_ng = S.ts(ng, gg, -1.0, None, ALU.mult, after=[m_g, fr])
            m_rb = S.tt(rb, z[:, :, 0:4], r, ALU.mult, after=[m_r, m2_, fr])
            m = S.ts(padj, z[:, :, 4:8], 0.09, 0.9, ALU.mult, ALU.add, after=[m2_, fr])
            m = S.tt(padj, padj, z[:, :, 4:8], ALU.mult, after=[m])
            m_cm = S.ts(cm, padj, -1.0, 1.0, ALU.mult, ALU.add, after=[m, fr])
            key.update(rb=rb, m_rb=m_rb)
            XT = yield from S.take()
            m_xt = solve(S, o, g, fed, XT)
            return dict(sm=sm, big=big, XT=XT, m_xt=m_xt, xF=xF, m_x=m_x, val=val, ng=ng, m_ng=m_ng,
                        padj=padj, cm=cm, m_cm=m_cm, m_kk=m_kk)

        def l1_attention_back(S, o, g, x3, ready, s):
            sm, fr = s["sm"], s["sm"].free
            yield from S.until(lambda: "rhs" in s["val"] and "m_att" in s["val"])
            s.update(s["val"])
            XT, m_xt = s["XT"], s["m_xt"]
            xt = XT.ap.rearrange("p (q i) -> p q i", q=NP)
            kkt, att = s["big"].ap
            first = []

            def router(F):
                for k in range(2):
                    bank = yield from F.bank()
                    for i, (src, m_s) in enumerate([(s["xF"], s["m_x"])] + s["paths"]):
                        m = F.mm(bank.ap, w("l1a", "rw1", i * 256 + k * P, P), src.ap, i == 0, False,
                                 after=[m_s, bank.free, l1])
                    first.append((bank, m))

            S.beside("router", router)
            U, Pc = (yield from S.take()), (yield from S.take())
            u, pc, bp = (a.ap.rearrange("p (q d) -> p q d", q=NP) for a in (U, Pc, s["rhs"]))
            m_u = None
            bu = yield from S.bank()
            ub = bu.ap.rearrange("p (q d) -> p q d", q=NP)
            bk = yield from S.bank()
            pb = bk.ap.rearrange("p (q d) -> p q d", q=NP)
            for c in range(4):
                r_ = slice(CH * c, CH * c + CH)
                if c:
                    for q in range(NP):
                        m = S.mm(pb[r_, q, :], kkt[0:CH * c, q, r_], u[0:CH * c, q, :],
                                 after=[m_u, s["m_kk"], bk.free])
                    m_p = S.tt(pc[r_], pb[r_],
                               s["ng"].rearrange("p h b -> p (h b)")[r_].unsqueeze(2).to_broadcast([CH, NP, DH]),
                               ALU.mult, after=[m, Pc.free, s["m_ng"]])
                for q in range(NP):
                    m = S.mm(ub[r_, q, :], xt[r_, q, :], bp[r_, q, :], True, c == 0,
                             after=[m_xt, s["m_rhs"], bu.free])
                    if c:
                        m = S.mm(ub[r_, q, :], xt[r_, q, :], pc[r_, q, :], False, True, after=[m_p])
                m_u = S.copy(u[r_], ub[r_], after=[m, U.free], engine="scalar")
            S.give_bank(bu, m_u)
            S.give_bank(bk, m_p)
            m_kk_read = m
            for x in (XT, Pc, s["rhs"]):
                S.give(x, m)
            bank, oT = (yield from S.bank()), (yield from S.take())
            ob = bank.ap.rearrange("p (q d) -> p q d", q=NP)
            for q in range(NP):
                m = S.mm(ob[:, q, :], att[:, q, :], u[:, q, :], after=[m_u, s["m_att"], bank.free])
            S.give(s["big"], m, m_kk_read)
            S.give(U, m)
            m_o = S.tt(oT.ap.rearrange("p (b h d) -> p b h d", b=GB, h=NH),
                       bank.ap.rearrange("p (h b d) -> p b h d", h=NH, b=GB),
                       s["rq"].unsqueeze(3).to_broadcast([P, GB, NH, DH]), ALU.mult, after=[m, s["m_rq"], oT.free])
            S.give_bank(bank, m_o)
            oF, m_oF = yield from to_feature(S, oT.ap, m_o)
            yield from S.until(lambda: len(first) == 2)
            hid = []
            for k in range(2):
                bank, m_first = first[k]
                hb_ = yield from S.take()
                m = S.mm(bank.ap, w("l1a", "rw1", 5 * 256 + k * P, P), oF.ap, False, True,
                         after=[m_oF, m_first, l1])
                m2_ = S.act(hb_.ap, bank.ap, ACT.Gelu, bias=w("l1a", "rb1", k, 1), after=[m, hb_.free])
                S.give_bank(bank, m2_)
                hid.append((hb_, m2_))
            S.give(s["xF"], m, s["m_xF_read"], s["m_xF_q"])
            S.give(oF, m)
            bank = yield from S.bank()
            lp = bank.ap[:, 0:GB * 20].rearrange("p (b e) -> p b e", b=GB)
            for b in range(GB):
                for k in range(2):
                    m = S.mm(lp[:, b, :], hid[k][0].ap[:, b * P:b * P + P], w("l1a", "rw2", k * 20, 20), k == 0,
                             k == 1, after=[hid[k][1], bank.free])
            for k in range(2):
                S.give(hid[k][0], m)
            wt, mx = sm(GB, 20), sm(NP)
            m = S.tt(wt, lp, rep_b(w("rows", "rb2")), ALU.add, after=[m, rows, fr])
            S.give_bank(bank, m)
            w4 = wt.rearrange("p b (h i) -> p b h i", i=5)
            w3 = wt.rearrange("p b (h i) -> p (b h) i", i=5)
            m = S.tt(w4, w4, itau[:, :].unsqueeze(1).unsqueeze(3).to_broadcast([P, GB, NH, 5]), ALU.mult,
                     after=[m, m_tau])
            m2_ = S.red(mx, w3, ALU.max, after=[m, fr])
            m = S.tt(w3, w3, rep(mx, 5), ALU.subtract, after=[m2_])
            m = S.act(wt, wt, ACT.Exp, after=[m])
            m2_ = S.red(mx, w3, ALU.add, after=[m])
            m2_ = S.recip(mx, mx, after=[m2_])
            m2_ = S.tt(mx, mx, s["cm"].rearrange("p b h -> p (b h)"), ALU.mult, after=[m2_, s["m_cm"]])
            m_w = S.tt(w3, w3, rep(mx, 5), ALU.mult, after=[m2_])
            acc, tmp = (yield from S.take()), []

            def hd(ap):
                return ap.rearrange("p (q d) -> p q d", d=DH)

            m_a = S.tt(hd(acc.ap), hd(oT.ap), rep(w3[:, :, 4], DH), ALU.mult, after=[m_w, m_o, acc.free])
            for i, (pf, m_pf) in enumerate(s["paths"]):
                bank = yield from S.bank()
                tmp.append((yield from S.take()))
                for b in range(GB):
                    c = slice(b * P, b * P + P)
                    m = S.tr(bank.ap[:, c], pf.ap[:, c], ident, after=[m_pf, bank.free])
                S.give(pf, m)
                tt_ = tmp[i]
                m = S.tt(hd(tt_.ap), hd(bank.ap), rep(w3[:, :, i], DH), ALU.mult,
                         after=[m, m_w, tt_.free])
                S.give_bank(bank, m)
                if i == 0:
                    m_t0 = m
                elif i == 1:
                    m_01 = S.tt(tmp[0].ap, tmp[0].ap, tmp[1].ap, ALU.add, after=[m, m_t0], engine="gpsimd")
                else:
                    m_a = S.tt(acc.ap, acc.ap, tt_.ap, ALU.add, after=[m, m_a])
            m = S.tt(hd(oT.ap), hd(s["vT"].ap), rep(s["padj"].rearrange("p b h -> p (b h)"), DH), ALU.mult,
                     after=[m_oF, m_a, s["m_vT"]])
            S.give(s["vT"], m)
            m_a = S.tt(acc.ap, acc.ap, oT.ap, ALU.add, after=[m, m_a])
            m_a = S.tt(acc.ap, acc.ap, tmp[0].ap, ALU.add, after=[m_01, m_a])
            m = S.act(oT.ap, acc.ap, ACT.Square, after=[m_a])
            ms = sm(NP)
            m = S.red(ms, hd(oT.ap), ALU.add, after=[m, fr])
            m = S.ts(ms, ms, 1.0 / DH, 1e-5, ALU.mult, ALU.add, after=[m])
            m = S.power(ms, ms, half[:, 0:NP], after=[m, m_half])
            m = S.tt(hd(acc.ap), hd(acc.ap), rep(ms, DH), ALU.mult, after=[m])
            sm.done(m)
            S.give(oT, m)
            for x in tmp:
                S.give(x, m_a)
            nF, m2_ = yield from to_feature(S, acc.ap, m, scale=w("l1a", "onw"), after=[l1])
            S.give(acc, m2_)
            bank = yield from S.bank()
            m = token_product(S, bank, [(nF.ap, w("l1a", "wo"))], [m2_])
            S.give(nF, m)
            m = S.tt(x3.ap, bank.ap, x3.ap, ALU.add, after=[m, ready])
            S.give_bank(bank, m)
            x4, m2_ = yield from norm(S, o, x3.ap, m, 1e-5)
            S.give(x3, m2_)
            return x4, m2_

        def l1_cross(S, o, g, x4, ready):
            xF, m_x = yield from to_feature(S, x4.ap, ready)
            cF = yield from S.take()
            m_c = S.dma(o["ch"]["c2"], cF.ap, dram["cF"][:, g * GT:g * GT + GT], after=[cF.free])
            q, m_q = yield from proj(S, w("l1x", "wqT"), xF.ap, m_x, l1x, bias=w("l1x", "bq"))
            S.give(xF, m_q)
            k, m_k = yield from proj(S, w("l1x", "wkT"), cF.ap, m_c, l1x, bias=w("l1x", "bk"))
            bank, v = (yield from S.bank()), (yield from S.take())
            m = token_product(S, bank, [(cF.ap, wvo[:, :])], [m_c, l1x])
            S.give(cF, m)
            m_v = S.tt(b4(v.ap), b4(bank.ap), rep_b(bo_all[:, :]), ALU.add, after=[m, v.free, l1x])
            S.give_bank(bank, m_v)
            pT, m_p = yield from attention(S, o, q.ap, k.ap, [m_q, m_k], False)
            S.give(q, m_p)
            S.give(k, m_p)
            bank = yield from S.bank()
            for b in range(GB):
                c = slice(b * P, b * P + P)
                m = S.mm(bank.ap[:, c], pT.ap[:, c], v.ap[:, c], after=[m_p, m_v, bank.free])
            S.give(pT, m)
            S.give(v, m)
            m = S.tt(x4.ap, bank.ap, x4.ap, ALU.add, after=[m, ready])
            S.give_bank(bank, m)
            x5, m2_ = yield from norm(S, o, x4.ap, m, 1e-5)
            S.give(x4, m2_)
            return x5, m2_

        def l1_ffn(S, o, g, x5, ready):
            sm = small(o, "st")
            fr = sm.free
            xF, m_x = yield from to_feature(S, x5.ap, ready)
            products = []

            def hidden_units(F):
                def silu_tile(k):
                    bg, bu, t, h = (yield from F.bank()), (yield from F.bank()), (yield from F.take()), (yield from F.take())
                    m1_ = F.mm(bg.ap, w("l1f", "sw1", k * P, P), xF.ap, after=[m_x, l1f, bg.free])
                    m2_ = F.mm(bu.ap, w("l1f", "sw3", k * P, P), xF.ap, after=[m_x, bu.free])
                    m = F.act(t.ap, bg.ap, ACT.Tanh, after=[m1_, t.free])
                    m = F.stt(h.ap, t.ap, 1.0, bg.ap, ALU.add, ALU.mult, after=[m, h.free])
                    F.give(t, m)
                    F.give_bank(bg, m)
                    m = F.tt(h.ap, h.ap, bu.ap, ALU.mult, after=[m, m2_])
                    F.give_bank(bu, m)
                    return h, m, m2_

                def gelu_tile(weight, bias):
                    bg, h = (yield from F.bank()), (yield from F.take())
                    m_in = F.mm(bg.ap, weight, xF.ap, after=[m_x, l1f, bg.free])
                    m = F.act(h.ap, bg.ap, ACT.Gelu, bias=bias, after=[m_in, h.free])
                    F.give_bank(bg, m)
                    return h, m, m_in

                jobs = [(0, lambda k=k: silu_tile(k), w("l1f", "sw2", k * P, P), k == 0, k == 3) for k in range(4)]
                jobs += [(1, lambda k=k: gelu_tile(wme[:, k * P:k * P + P], bme[:, k:k + 1]),
                          w("l1f", "c2w", k * P, P), k == 0, k == 1) for k in range(2)]
                jobs += [(3, lambda k=k: gelu_tile(w("l1f", "ml1", k * P, P), w("l1f", "mlb1", k, 1)),
                          w("l1f", "ml2", k * P, P), k == 0, k == 3) for k in range(4)]
                made = yield from jobs[0][1]()
                for i, (e, _, weight, first, final) in enumerate(jobs):
                    h, m_h, m_in = made
                    if i + 1 < len(jobs):
                        made = yield from jobs[i + 1][1]()
                    if first:
                        acc = yield from F.bank()
                    for b in range(GB):
                        c = slice(b * P, b * P + P)
                        m = F.mm(acc.ap[:, c], h.ap[:, c], weight, first and b == 0, final and b == GB - 1,
                                 after=[m_h, acc.free])
                    F.give(h, m)
                    if final:
                        products.append((e, acc, m, m_in))

            S.beside("hidden", hidden_units)

            def block(F):
                bank, y = (yield from F.bank()), (yield from F.take())
                m = m_block = token_product(F, bank, [(xF.ap, wce[:, :])], [m_x, l1f])
                m = F.tt(b4(y.ap), b4(bank.ap), rep_b(bce[:, :]), ALU.add, after=[m, y.free, l1f])
                F.give_bank(bank, m)
                xh, m = yield from norm(F, o, y.ap, m, 1e-5)
                F.give(y, m)
                bank, hF, rF = (yield from F.bank()), (yield from F.take()), (yield from F.take())
                for b in range(GB):
                    c = slice(b * P, b * P + P)
                    m2_ = F.tr(bank.ap[:, c], xh.ap[:, c], ident, after=[m, bank.free])
                F.give(xh, m2_)
                m_h = F.ts(hF.ap, bank.ap, w("l1f", "n1g"), w("l1f", "n1b"), ALU.mult, ALU.add, after=[m2_, hF.free, l1f])
                m_r = F.ts(rF.ap, bank.ap, w("l1f", "n1g"), nfb[:, 0:1], ALU.mult, ALU.add, after=[m2_, rF.free, l1f])
                F.give_bank(bank, m_r)
                halves = []
                for k in range(2):
                    h, bg = (yield from F.take()), (yield from F.bank())
                    m = F.mm(bg.ap, w("l1f", "f1w", k * P, P), hF.ap, after=[m_h, bg.free])
                    m2_ = F.act(h.ap, bg.ap, ACT.Relu, bias=w("l1f", "f1b", k, 1), after=[m, h.free])
                    F.give_bank(bg, m2_)
                    halves.append((h, m2_))
                F.give(hF, m)
                acc = yield from F.bank()
                for b in range(GB):
                    c = slice(b * P, b * P + P)
                    m = F.mm(acc.ap[:, c], rF.ap[:, c], ident, b == 0, False, after=[m_r, acc.free])
                F.give(rF, m)
                for k, (h, m_h) in enumerate(halves):
                    for b in range(GB):
                        c = slice(b * P, b * P + P)
                        m = F.mm(acc.ap[:, c], h.ap[:, c], w("l1f", "f2w", k * P, P), False,
                                 k == 1 and b == GB - 1, after=[m_h])
                    F.give(h, m)
                xh, m = yield from norm(F, o, acc.ap, m, 1e-5, bank=True)
                F.give_bank(acc, m)
                hF, m2_ = yield from to_feature(F, xh.ap, m, scale=w("l1f", "n2g"), bias=w("l1f", "n2b"), after=[l1f])
                F.give(xh, m2_)
                bank = yield from F.bank()
                m = token_product(F, bank, [(hF.ap, w("l1f", "gen"))], [m2_])
                F.give(hF, m)
                products.append((2, bank, m, m_block))


            S.beside("block", block)
            bank = yield from S.bank()
            lgp = bank.ap[:, 0:GB * 4].rearrange("p (b e) -> p b e", b=GB)
            for b in range(GB):
                m = S.mm(lgp[:, b, :], xF.ap[:, b * P:b * P + P], w("l1f", "router"), after=[m_x, l2, bank.free])
            m_lgp = m
            lg, top, idf, wt, pr2 = sm(GB, 8), sm(GB, 8), sm(GB, 8), sm(GB, 2), sm(GB, 4)
            idx = o["idx"]
            m1_ = S.put("vector", 60, lambda e: e.memset(lg[:, :, 4:8], -BIG), [fr])
            m = S.tt(lg[:, :, 0:4], lgp, rep_b(rbias[:, :]), ALU.add, after=[m, fr, l1f])
            S.give_bank(bank, m)
            for b in range(GB):
                m2_ = S.put("vector", 70, lambda e, b=b: e.max(top[:, b, :], lg[:, b, :]), [m, m1_, fr])
            m_top = m2_
            for b in range(GB):
                m2_ = S.put("vector", 77, lambda e, b=b: e.max_index(idx[:, b, :], top[:, b, :], lg[:, b, :]),
                            [m_top, fr])
            m_idx = S.copy(idf, idx[:, :, :], after=[m2_, fr])
            m = S.tt(wt[:, :, 1:2], top[:, :, 1:2], top[:, :, 0:1], ALU.subtract, after=[m_top, fr])
            m = S.act(wt[:, :, 1:2], wt[:, :, 1:2], ACT.Exp, after=[m])
            m = S.ts(wt[:, :, 0:1], wt[:, :, 1:2], 1.0, None, ALU.add, after=[m])
            m = S.recip(wt[:, :, 0:1], wt[:, :, 0:1], after=[m])
            m = S.tt(wt[:, :, 1:2], wt[:, :, 1:2], wt[:, :, 0:1], ALU.mult, after=[m])
            we = sm(GB, 4)
            iota = rep_b(w("const", "iota", 0, 4))
            shp = [P, GB, 4]
            m1_ = S.tt(we, idf[:, :, 0:1].to_broadcast(shp), iota, ALU.is_equal, after=[m_idx, fr])
            m1_ = S.tt(we, we, wt[:, :, 0:1].to_broadcast(shp), ALU.mult, after=[m1_, m])
            m2_ = S.tt(pr2, idf[:, :, 1:2].to_broadcast(shp), iota, ALU.is_equal, after=[m_idx, fr])
            m2_ = S.tt(pr2, pr2, wt[:, :, 1:2].to_broadcast(shp), ALU.mult, after=[m2_, m])
            m_w = S.tt(we, we, pr2, ALU.add, after=[m1_, m2_])
            bank, wT = (yield from S.bank()), (yield from S.take())
            for b in range(GB):
                m = S.tr(bank.ap[0:4, b * P:b * P + P], we[:, b, :], ident, after=[m_w, bank.free, const])
            m = S.copy(wT.ap[0:4, :], bank.ap[0:4, :], after=[m, wT.free], engine="scalar")
            S.give_bank(bank, m)
            bank = yield from S.bank()
            for b in range(GB):
                c = slice(b * P, b * P + P)
                m2_ = S.mm(bank.ap[:, c], wT.ap[0:4, c], w("l1f", "ebias")[0:4, :],
                           after=[m, bank.free])
            S.give(wT, m2_)
            m_y = S.tt(x5.ap, bank.ap, x5.ap, ALU.add, after=[m2_, ready])
            S.give_bank(bank, m_y)

            def add_expert(e, bank, m, m_y):
                for b in range(GB):
                    c = slice(b * P, b * P + P)
                    m2_ = S.stt(x5.ap[:, c], bank.ap[:, c], we[:, b, e:e + 1], x5.ap[:, c], ALU.mult, ALU.add,
                                after=[m, m_y, m_w])
                S.give_bank(bank, m2_)
                return m2_

            xF_read = [m_lgp]
            for i in range(4):
                yield from S.until(lambda: len(products) > i)
                e, acc, m, m_in = products[i]
                m_y = add_expert(e, acc, m, m_y)
                xF_read.append(m_in)
            S.give(xF, *xF_read)
            sm.done(m_y)
            x6, m = yield from norm(S, o, x5.ap, m_y, 1e-5)
            S.give(x5, m)
            return x6, m

        last = []

        def finish(S, o, g, x, m):
            m2_ = S.dma(o["ch"]["out"], out[g * GB:g * GB + GB].rearrange("b t f -> t b f"), b4(x.ap), after=[m])
            S.give(x, m2_)
            last.append(m2_)

        def groups(S, slot):
            for g in range(slot, NG, NSTREAM):
                S.group, o = g, own[slot]
                x, m = yield from l0_attention(S, o, g)
                if stop_after >= 2:
                    x, m = yield from l0_cross(S, o, g, x, m)
                if stop_after >= 3:
                    x, m = yield from l0_ffn(S, o, g, x, m)
                if stop_after >= 4:
                    st = yield from l1_attention_front(S, o, g, x, m)
                    x, m = yield from l1_attention_back(S, o, g, x, m, st)
                if stop_after >= 5:
                    x, m = yield from l1_cross(S, o, g, x, m)
                if stop_after >= 6:
                    x, m = yield from l1_ffn(S, o, g, x, m)
                finish(S, o, g, x, m)

        for slot in range(NSTREAM):
            S = Strand(queues, f"s{slot}", slot)
            queues.running.append((S, groups(S, slot)))
        queues.record()
        tail = Strand(queues, "tail", NG)
        tail.put("sync", 50, lambda e: e.nop(), after=last)


def _pack(inp):
    a = {k: np.asarray(v) for k, v in inp.items()}
    f = np.float32

    def col(x, n=1):
        return x.reshape(n, P).T

    def tiles(x):
        return x.reshape(-1, P, x.shape[1]).transpose(1, 0, 2).reshape(P, -1)

    t, s = np.arange(P)[:, None], np.arange(P)[None, :]
    rank = (np.arange(8)[None, :] >= np.arange(TOPK)[:, None]).astype(f).reshape(1, -1)
    expert = np.zeros((P, NHT * P), f)
    for r in range(27):
        e = r % 9
        lo = 64 * e
        expert[r, lo:lo + (64 if e < 8 else 256)] = 1.0
    const = dict(ident=np.eye(P, dtype=f), ones=np.ones((P, P), f), upto=(t <= s).astype(f),
                 cmask=np.where(s > t, f(-BIG), f(0)), rank_ge=np.repeat(rank, P, 0),
                 iota=np.repeat(np.arange(8, dtype=f)[None], P, 0), expert=expert,
                 unit_rows=np.repeat(np.stack([np.eye(32, dtype=f)[h::2].reshape(-1) for h in (0, 1)]), 64, 0),
                 heads=np.repeat(np.eye(NH, dtype=f), DH, 0))
    rows = dict(gate_bias=np.concatenate([a["L0_attn_eta_b"], a["L0_attn_alpha_b"], a["L0_attn_gate_b"]]),
                gamma=a["L0_xattn_gamma"], beta=a["L0_xattn_beta"],
                log_tau=a["L1_attn_log_tau"], bo=a["L1_xattn_bo"],
                ce_bo=a["L1_ffn_ce_bo"], router_b=a["L1_ffn_router_b"], load_balancer=a["L1_ffn_load_balancer"],
                id_b=a["L1_attn_id_gate_b"], rb2=a["L1_attn_router_b2"])
    once_rows = dict(q_conv=a["L1_attn_q_conv_w"].T[::-1], k_conv=a["L1_attn_k_conv_w"].T[::-1],
                     v_conv=a["L1_attn_v_conv_w"].T[::-1])
    rows, once_rows = ({k: v.reshape(1, -1) for k, v in r.items()} for r in (rows, once_rows))
    l0a = dict(m0T=a["L0_attn_M_init"].T, w1T=a["L0_attn_vg_w1"].T, w2T=a["L0_attn_vg_w2"].T,
               eta=col(a["L0_attn_eta_w"]), alpha=col(a["L0_attn_alpha_w"]), gate=col(a["L0_attn_gate_w"]))
    x = "L0_xattn_"
    once_l0 = dict(wqT=a[x + "Wq"].T, wkT=a[x + "Wk"].T, wcqT=a[x + "Wcq"].T, wckT=a[x + "Wck"].T)
    l0x = dict(wv=a[x + "Wv"],
               wcv=a[x + "Wcv"], w1=a[x + "W1"], b1=col(a[x + "b1"]), gamma=col(a[x + "gamma"]),
               beta=col(a[x + "beta"]))
    x = "L0_ffn_"
    l0f = dict(router=a[x + "gate_w"].T,
               gate=np.concatenate([a[x + "dyn_gate_w"].reshape(512, P), a[x + "sh_gate_w"].reshape(256, P)]).T,
               up=np.concatenate([a[x + "dyn_up_w"].reshape(512, P), a[x + "sh_up_w"].reshape(256, P)]).T,
               down=tiles(np.concatenate([a[x + "dyn_down_w"].transpose(0, 2, 1).reshape(512, P),
                                          a[x + "sh_down_w"].transpose(0, 2, 1).reshape(256, P)])))
    x = "L1_attn_"
    fir = []
    for fi, kg in FIR_GROUPS:
        taps = a[x + f"fir_w{FIRS[fi]}"].reshape(P, FIRS[fi])[:, ::-1]
        taps = np.concatenate([taps, np.zeros((P, 4 * ((FIRS[fi] + 3) // 4) - FIRS[fi]), f)], 1)
        for c in range(4):
            fir.append(taps[32 * c:32 * c + 32, 4 * kg:4 * kg + 4].T.reshape(P, 1))
    once_l1 = dict(wq=a[x + "Wq"], wk=a[x + "Wk"], wv=a[x + "Wv"], fir=np.concatenate(fir, 1),
                   eye32=np.tile(np.eye(32, dtype=f), (4, 1)), x_wv=a["L1_xattn_Wv"], x_woT=a["L1_xattn_Wo"].T)
    l1a = dict(
               wb_id=np.concatenate([a[x + "Wb"], a[x + "id_gate_W"]], 1), rw1=tiles(a[x + "router_W1"]),
               rb1=col(a[x + "router_b1"], 2), rw2=tiles(a[x + "router_W2"]),
               onw=np.tile(a[x + "o_norm_w"], NH).reshape(P, 1), wo=a[x + "Wo"])
    x = "L1_xattn_"
    l1x = dict(wqT=a[x + "Wq"].T, wkT=a[x + "Wk"].T, bq=col(a[x + "bq"]),
               bk=col(a[x + "bk"]), bv=col(a[x + "bv"]))
    x = "L1_ffn_"
    once_l1.update(me_eqT=a[x + "me_eq_w"].T, me_wvT=a[x + "me_wv"].T, me_woT=a[x + "me_wo"].T,
                   c1w=a[x + "me_c1w"], synT=a[x + "ce_syn_w"].T, ce_wvT=a[x + "ce_wv"].T, ce_wo=a[x + "ce_wo"])
    eb = np.zeros((P, P), f)
    for e, n in ((1, "me_c2b"), (2, "ce_gen_b"), (3, "ml_b2")):
        eb[e] = a[x + n]
    l1f = dict(router=a[x + "router_w"], sw1=a[x + "sw_w1"], sw3=a[x + "sw_w3"], sw2=tiles(a[x + "sw_w2"]),
               c2w=tiles(a[x + "me_c2w"]), me_eq_b=col(a[x + "me_eq_b"]), me_bv=col(a[x + "me_bv"]),
               me_bo=col(a[x + "me_bo"]), c1b=col(a[x + "me_c1b"], 2), 
               ce_syn_b=col(a[x + "ce_syn_b"]),
               ce_bv=col(a[x + "ce_bv"]), n1g=col(a[x + "ce_n1g"]), n1b=col(a[x + "ce_n1b"]),
               f1w=a[x + "ce_f1w"], f1b=col(a[x + "ce_f1b"], 2), f2w=tiles(a[x + "ce_f2w"]),
               f2b=col(a[x + "ce_f2b"]), n2g=col(a[x + "ce_n2g"]), n2b=col(a[x + "ce_n2b"]),
               gen=a[x + "ce_gen_w"], ml1=a[x + "ml_w1"], mlb1=col(a[x + "ml_b1"], 4), ml2=tiles(a[x + "ml_w2"]),
               ebias=eb)
    arrays, cols = {}, {}
    for name, d in dict(const=const, rows=rows, l0a=l0a, l0x=l0x, l0f=l0f, l1a=l1a, l1x=l1x, l1f=l1f,
                       once_rows=once_rows, once_l0=once_l0, once_l1=once_l1).items():
        at, cols[name] = 0, {}
        for k, v in d.items():
            cols[name][k] = (at, v.shape[1])
            at += v.shape[1]
        arrays[name] = np.ascontiguousarray(np.concatenate(list(d.values()), 1))
    arrays["x"] = np.ascontiguousarray(a["x"])
    arrays["xF"] = np.ascontiguousarray(a["x"].transpose(2, 0, 1).reshape(P, NB * P))
    arrays["cF"] = np.ascontiguousarray(a["ctx_1024"].transpose(2, 0, 1).reshape(P, NB * P))
    return arrays, cols


def declare(nc, arrays, cols, stop_after=99):
    dram = {k: nc.dram_tensor("in_" + k, v.shape, F32, kind="ExternalInput").ap() for k, v in arrays.items()}
    for k in ("kk", "xt"):
        dram[k] = nc.dram_tensor("scratch_" + k, (NG, 4 * NP, CH * CH), F32, kind="Internal").ap()
    out = nc.dram_tensor("out_0", (NB, P, P), F32, kind="ExternalOutput").ap()
    build(nc, dram, cols, out, stop_after)


def kernel(**inputs):
    import concourse.bacc as _bacc
    from concourse.bass_utils import run_bass_kernel_spmd as _run

    nc = _bacc.Bacc("TRN2", target_bir_lowering=False, num_devices=1)
    arrays, cols = _pack(inputs)
    declare(nc, arrays, cols)
    r = _run(nc, [{"in_" + k: v for k, v in arrays.items()}], core_ids=[0])
    return r.results[0]["out_0"]
```
